# Optimizing a Trainium2 kernel written in Bass

```python
import numpy as np
import jax
import jax.numpy as jnp

def _softmax(x, axis=-1):
    return jax.nn.softmax(x, axis=axis)

def _gelu(x):
    return jax.nn.gelu(x, approximate=True)

def _silu(x):
    return jax.nn.silu(x)

def _sigmoid(x):
    return jax.nn.sigmoid(x)

def _layernorm(x, axis=-1, eps=1e-05):
    m = jnp.mean(x, axis=axis, keepdims=True)
    v = jnp.var(x, axis=axis, keepdims=True)
    return (x - m) / jnp.sqrt(v + eps)

def _scatter_add(tgt, idx, src, axis=0):
    return tgt.at[idx].add(src)

def _segment_sum(src, seg, n):
    return jax.ops.segment_sum(src, seg, n)
kernel_name = 'mk_lm_tower_d2_tok_ids256_r4_a35104'

def setup_inputs(seed: int=0):
    np.random.seed(seed)
    _w = jnp.asarray

    def _rec_inputs():
        import jax
        import jax.numpy as jnp
        _rk = jax.random.key(seed)
        x = jax.random.randint(jax.random.fold_in(_rk, 1), (16, 512), 0, 64, jnp.int32)
        itok_BS_0_255 = jax.random.randint(jax.random.fold_in(_rk, 21), (16, 512), 0, 64, jnp.int32)
        itok_BS_0_511 = jax.random.randint(jax.random.fold_in(_rk, 22), (16, 512), 0, 128, jnp.int32)
        itok_BS_0_127 = jax.random.randint(jax.random.fold_in(_rk, 23), (16, 512), 0, 128, jnp.int32)
        itok_BS_0_63 = jax.random.randint(jax.random.fold_in(_rk, 24), (16, 512), 0, 64, jnp.int32)
        itok_BS_0_3 = jax.random.randint(jax.random.fold_in(_rk, 25), (16, 512), 0, 4, jnp.int32)
        return (x, itok_BS_0_255, itok_BS_0_511, itok_BS_0_127, itok_BS_0_63, itok_BS_0_3)
    x, itok_BS_0_255, itok_BS_0_511, itok_BS_0_127, itok_BS_0_63, itok_BS_0_3 = _rec_inputs()

    def _L0_tok_setup():
        import jax, jax.numpy as jnp
        import numpy as np
        B, S = (128, 512)
        D_OUT = 64
        EMB = 16
        EPS_W = 1e-08
        EPS_LN = 1e-05

        def ternary_linear(x, W, b):
            scale = jnp.mean(jnp.abs(W))
            w_q = jnp.clip(jnp.round(W / (scale + EPS_W)), -1.0, 1.0) * scale
            w_eff = W + jax.lax.stop_gradient(w_q - W)
            return jnp.einsum('bsk,ok->bso', x, w_eff) + b

        def layer_norm(x, gamma, beta):
            mu = jnp.mean(x, axis=-1, keepdims=True)
            var = jnp.mean(jnp.square(x - mu), axis=-1, keepdims=True)
            return (x - mu) * jax.lax.rsqrt(var + EPS_LN) * gamma + beta
        key = jax.random.key(seed)
        ks = jax.random.split(key, 16)
        vocabs = {'event_type': 64, 'fault_class': 64, 'syscall_class': 128, 'opcode_family': 128, 'transition_type': 64, 'result_class': 4}
        inp = {}
        for i, (name, v) in enumerate(vocabs.items()):
            inp[name] = jax.random.randint(ks[i], (B, S), 0, v, dtype=jnp.int64)
        inp['E_et'] = jax.random.normal(ks[6], (64, EMB), dtype=jnp.float32)
        inp['E_fc'] = jax.random.normal(ks[7], (64, EMB), dtype=jnp.float32)
        inp['E_sc'] = jax.random.normal(ks[8], (128, EMB), dtype=jnp.float32)
        inp['E_of'] = jax.random.normal(ks[9], (128, EMB), dtype=jnp.float32)
        inp['E_tt'] = jax.random.normal(ks[10], (64, EMB), dtype=jnp.float32)
        inp['E_rc'] = jax.random.normal(ks[11], (4, EMB), dtype=jnp.float32)
        inp['W'] = jax.random.normal(ks[12], (D_OUT, 96), dtype=jnp.float32) * 0.1
        inp['b'] = jnp.zeros((D_OUT,), dtype=jnp.float32)
        inp['gamma'] = jnp.ones((D_OUT,), dtype=jnp.float32)
        inp['beta'] = jnp.zeros((D_OUT,), dtype=jnp.float32)
        return inp
    _L0_tok_all = _L0_tok_setup()
    _L0_tok_in = {k: v for k, v in _L0_tok_all.items() if k in ('E_et', 'E_fc', 'E_sc', 'E_of', 'E_tt', 'E_rc', 'W', 'b', 'gamma', 'beta')}
    del _L0_tok_all

    def _L0_attn_setup():
        import jax, jax.numpy as jnp
        import numpy as np
        B, L, H, P = (4, 2048, 64, 64)

        def discretize(log_real, imag, log_Delta, B_real, B_imag):
            Lr = -jnp.exp(log_real)
            Li = imag
            Delta = jnp.exp(log_Delta)
            ad = Lr * Delta
            bd = Li * Delta
            exp_ad = jnp.exp(ad)
            Lbar_r = exp_ad * jnp.cos(bd)
            Lbar_i = exp_ad * jnp.sin(bd)
            denom = jnp.maximum(Lr * Lr + Li * Li, 1e-12)
            inv_Lr = Lr / denom
            inv_Li = -Li / denom
            diff_r = Lbar_r - 1.0
            diff_i = Lbar_i
            coeff_r = inv_Lr * diff_r - inv_Li * diff_i
            coeff_i = inv_Lr * diff_i + inv_Li * diff_r
            B_bar_r = coeff_r[:, None] * B_real - coeff_i[:, None] * B_imag
            B_bar_i = coeff_r[:, None] * B_imag + coeff_i[:, None] * B_real
            return (Lbar_r, Lbar_i, B_bar_r, B_bar_i)

        def binop(ei, ej):
            Ar_i, Ai_i, xr_i, xi_i = ei
            Ar_j, Ai_j, xr_j, xi_j = ej
            return (Ar_j * Ar_i - Ai_j * Ai_i, Ar_j * Ai_i + Ai_j * Ar_i, Ar_j * xr_i - Ai_j * xi_i + xr_j, Ar_j * xi_i + Ai_j * xr_i + xi_j)

        def apply_ssm(Lbar_r, Lbar_i, B_bar_r, B_bar_i, C_real, C_imag, D, x):
            Bu_r = jnp.einsum('blh,ph->blp', x, B_bar_r)
            Bu_i = jnp.einsum('blh,ph->blp', x, B_bar_i)
            A_r = jnp.broadcast_to(Lbar_r, Bu_r.shape)
            A_i = jnp.broadcast_to(Lbar_i, Bu_i.shape)
            _, _, xs_r, xs_i = jax.lax.associative_scan(binop, (A_r, A_i, Bu_r, Bu_i), axis=1)
            ys = jnp.einsum('blp,hp->blh', xs_r, C_real) - jnp.einsum('blp,hp->blh', xs_i, C_imag)
            return ys + D * x

        def s5(log_real, imag, log_Delta, B_real, B_imag, C_real, C_imag, D, x):
            Lbar_r, Lbar_i, B_bar_r, B_bar_i = discretize(log_real, imag, log_Delta, B_real, B_imag)
            y = apply_ssm(Lbar_r, Lbar_i, B_bar_r, B_bar_i, C_real, C_imag, D, x)
            return jax.nn.gelu(y, approximate=False)
        key = jax.random.key(seed)
        ks = jax.random.split(key, 17)
        std_b = 1.0 / H ** 0.5
        std_c = 1.0 / P ** 0.5

        def params(ki):
            k = jax.random.split(ks[ki], 8)
            return dict(log_real=jax.random.normal(k[0], (P,), jnp.float32) * 0.5, imag=jax.random.normal(k[1], (P,), jnp.float32), log_Delta=jnp.zeros((P,), jnp.float32), B_real=jax.random.normal(k[2], (P, H), jnp.float32) * std_b, B_imag=jax.random.normal(k[3], (P, H), jnp.float32) * std_b, C_real=jax.random.normal(k[4], (H, P), jnp.float32) * std_c, C_imag=jax.random.normal(k[5], (H, P), jnp.float32) * std_c, D=jnp.ones((H,), jnp.float32))
        f = params(1)
        b = params(2)
        inp = {'x': jax.random.normal(ks[0], (B, L, H), jnp.float32)}
        for name, v in f.items():
            inp['fwd_' + name] = v
        for name, v in b.items():
            inp['bwd_' + name] = v
        return inp
    _L0_attn_all = _L0_attn_setup()
    _L0_attn_in = {k: v for k, v in _L0_attn_all.items() if k in ('fwd_log_real', 'fwd_imag', 'fwd_log_Delta', 'fwd_B_real', 'fwd_B_imag', 'fwd_C_real', 'fwd_C_imag', 'fwd_D', 'bwd_log_real', 'bwd_imag', 'bwd_log_Delta', 'bwd_B_real', 'bwd_B_imag', 'bwd_C_real', 'bwd_C_imag', 'bwd_D')}
    del _L0_attn_all

    def _L0_ffn_setup():
        import jax, jax.numpy as jnp
        import numpy as np
        DIM = 64
        HEADS = 8
        NUM_KEYS = 64
        NUM_KV = NUM_KEYS ** 2
        PK_TOPK = 16
        FINAL_TOPK = 16
        DIM_KEY = DIM // 2
        P = 2

        def _pk(x, Wq_pk, pk_keys):
            b, n, _ = x.shape
            q = (x @ Wq_pk).reshape(b, n, P, HEADS, DIM_KEY).transpose(2, 0, 1, 3, 4)
            sim = jnp.einsum('pbnhd,pkhd->pbnhk', q, pk_keys)
            scores, idx = jax.lax.top_k(sim, PK_TOPK)
            idx0 = idx[0]
            idx1 = idx[1] * NUM_KEYS
            index = (idx0[..., :, None] + idx1[..., None, :]).reshape(b, n, HEADS, PK_TOPK * PK_TOPK)
            score = (scores[0][..., :, None] + scores[1][..., None, :]).reshape(b, n, HEADS, PK_TOPK * PK_TOPK)
            final_scores, pk_idx = jax.lax.top_k(score, FINAL_TOPK)
            final_indices = jnp.take_along_axis(index, pk_idx, axis=-1)
            final_scores = jax.nn.softmax(final_scores, axis=-1)
            return (final_scores, final_indices)
        key = jax.random.key(seed)
        ks = jax.random.split(key, 7)
        b, n = (2, 256)
        std = 0.02
        x = jax.random.normal(ks[0], (b, n, DIM), dtype=jnp.float32)
        Wq_pk = jax.random.normal(ks[1], (DIM, P * HEADS * DIM_KEY), dtype=jnp.float32) * std
        pk_keys = jax.random.normal(ks[2], (P, NUM_KEYS, HEADS, DIM_KEY), dtype=jnp.float32) * std
        Wq = jax.random.normal(ks[3], (DIM, HEADS * DIM), dtype=jnp.float32) * std
        keys_table = jax.random.normal(ks[4], (NUM_KV * HEADS, DIM), dtype=jnp.float32) * std
        values_table = jax.random.normal(ks[5], (NUM_KV * HEADS, DIM), dtype=jnp.float32) * std
        Wo = jax.random.normal(ks[6], (DIM * HEADS, DIM), dtype=jnp.float32) * std
        return {'x': x, 'Wq_pk': Wq_pk, 'pk_keys': pk_keys, 'Wq': Wq, 'keys_table': keys_table, 'values_table': values_table, 'Wo': Wo}
    _L0_ffn_all = _L0_ffn_setup()
    _L0_ffn_in = {k: v for k, v in _L0_ffn_all.items() if k in ('Wq_pk', 'pk_keys', 'Wq', 'keys_table', 'values_table', 'Wo')}
    del _L0_ffn_all

    def _L1_attn_setup():
        import jax, jax.numpy as jnp
        import numpy as np
        B, N, C = (2, 12500, 64)
        H, W = (8, 64)
        HD = C // H
        key = jax.random.key(seed)
        k1, k2, k3, k4, k5 = jax.random.split(key, 5)
        s = 1.0 / np.sqrt(C)
        return {'x': jax.random.normal(k1, (B, N, C), dtype=jnp.float32), 'qkv_w': jax.random.uniform(k2, (C, 3 * C), jnp.float32, -s, s), 'qkv_b': jax.random.uniform(k3, (3 * C,), jnp.float32, -s, s), 'proj_w': jax.random.uniform(k4, (C, C), jnp.float32, -s, s), 'proj_b': jax.random.uniform(k5, (C,), jnp.float32, -s, s)}
    _L1_attn_all = _L1_attn_setup()
    _L1_attn_in = {k: v for k, v in _L1_attn_all.items() if k in ('qkv_w', 'qkv_b', 'proj_w', 'proj_b')}
    del _L1_attn_all

    def _L1_ffn_setup():
        import jax, jax.numpy as jnp
        import numpy as np
        NUM_EXPERTS = 8
        TOP_K = 2
        B, S, D = (8, 2048, 64)

        def _moe(tokens, router_w, w1, b1, w2, b2):
            N = tokens.shape[0]
            E = router_w.shape[0]
            logits = tokens.astype(jnp.float32) @ router_w.astype(jnp.float32).T
            probs = jax.nn.softmax(logits, axis=-1)
            rw, re = jax.lax.top_k(probs, TOP_K)
            if TOP_K > 1:
                rw = rw / jnp.maximum(rw.sum(-1, keepdims=True), 1e-12)
            rw = rw.astype(tokens.dtype)
            combine = jnp.zeros((N, E), tokens.dtype).at[jnp.arange(N)[:, None], re].set(rw)
            out = tokens
            for e in range(E):
                h = jax.nn.gelu(tokens @ w1[e] + b1[e], approximate=False)
                y = h @ w2[e] + b2[e]
                out = out + combine[:, e:e + 1] * y
            return out
        key = jax.random.key(seed)
        ks = jax.random.split(key, 4)
        scale = 1.0 / np.sqrt(D).astype(np.float32)
        return {'input_embeddings': jax.random.normal(ks[0], (B, S, D), jnp.float32), 'router_w': jax.random.normal(ks[1], (NUM_EXPERTS, D), jnp.float32) * scale, 'w1': jax.random.normal(ks[2], (NUM_EXPERTS, D, D), jnp.float32) * scale, 'b1': jnp.zeros((NUM_EXPERTS, D), jnp.float32), 'w2': jax.random.normal(ks[3], (NUM_EXPERTS, D, D), jnp.float32) * scale, 'b2': jnp.zeros((NUM_EXPERTS, D), jnp.float32)}
    _L1_ffn_all = _L1_ffn_setup()
    _L1_ffn_in = {k: v for k, v in _L1_ffn_all.items() if k in ('router_w', 'w1', 'b1', 'w2', 'b2')}
    del _L1_ffn_all
    return {'x': x, 'itok_BS_0_255': itok_BS_0_255, 'itok_BS_0_511': itok_BS_0_511, 'itok_BS_0_127': itok_BS_0_127, 'itok_BS_0_63': itok_BS_0_63, 'itok_BS_0_3': itok_BS_0_3, 'L0_tok_E_et': _L0_tok_in['E_et'], 'L0_tok_E_fc': _L0_tok_in['E_fc'], 'L0_tok_E_sc': _L0_tok_in['E_sc'], 'L0_tok_E_of': _L0_tok_in['E_of'], 'L0_tok_E_tt': _L0_tok_in['E_tt'], 'L0_tok_E_rc': _L0_tok_in['E_rc'], 'L0_tok_W': _L0_tok_in['W'], 'L0_tok_b': _L0_tok_in['b'], 'L0_tok_gamma': _L0_tok_in['gamma'], 'L0_tok_beta': _L0_tok_in['beta'], 'L0_attn_fwd_log_real': _L0_attn_in['fwd_log_real'], 'L0_attn_fwd_imag': _L0_attn_in['fwd_imag'], 'L0_attn_fwd_log_Delta': _L0_attn_in['fwd_log_Delta'], 'L0_attn_fwd_B_real': _L0_attn_in['fwd_B_real'], 'L0_attn_fwd_B_imag': _L0_attn_in['fwd_B_imag'], 'L0_attn_fwd_C_real': _L0_attn_in['fwd_C_real'], 'L0_attn_fwd_C_imag': _L0_attn_in['fwd_C_imag'], 'L0_attn_fwd_D': _L0_attn_in['fwd_D'], 'L0_attn_bwd_log_real': _L0_attn_in['bwd_log_real'], 'L0_attn_bwd_imag': _L0_attn_in['bwd_imag'], 'L0_attn_bwd_log_Delta': _L0_attn_in['bwd_log_Delta'], 'L0_attn_bwd_B_real': _L0_attn_in['bwd_B_real'], 'L0_attn_bwd_B_imag': _L0_attn_in['bwd_B_imag'], 'L0_attn_bwd_C_real': _L0_attn_in['bwd_C_real'], 'L0_attn_bwd_C_imag': _L0_attn_in['bwd_C_imag'], 'L0_attn_bwd_D': _L0_attn_in['bwd_D'], 'L0_ffn_Wq_pk': _L0_ffn_in['Wq_pk'], 'L0_ffn_pk_keys': _L0_ffn_in['pk_keys'], 'L0_ffn_Wq': _L0_ffn_in['Wq'], 'L0_ffn_keys_table': _L0_ffn_in['keys_table'], 'L0_ffn_values_table': _L0_ffn_in['values_table'], 'L0_ffn_Wo': _L0_ffn_in['Wo'], 'L1_attn_qkv_w': _L1_attn_in['qkv_w'], 'L1_attn_qkv_b': _L1_attn_in['qkv_b'], 'L1_attn_proj_w': _L1_attn_in['proj_w'], 'L1_attn_proj_b': _L1_attn_in['proj_b'], 'L1_ffn_router_w': _L1_ffn_in['router_w'], 'L1_ffn_w1': _L1_ffn_in['w1'], 'L1_ffn_b1': _L1_ffn_in['b1'], 'L1_ffn_w2': _L1_ffn_in['w2'], 'L1_ffn_b2': _L1_ffn_in['b2']}

def reference(x, itok_BS_0_255, itok_BS_0_511, itok_BS_0_127, itok_BS_0_63, itok_BS_0_3, L0_tok_E_et, L0_tok_E_fc, L0_tok_E_sc, L0_tok_E_of, L0_tok_E_tt, L0_tok_E_rc, L0_tok_W, L0_tok_b, L0_tok_gamma, L0_tok_beta, L0_attn_fwd_log_real, L0_attn_fwd_imag, L0_attn_fwd_log_Delta, L0_attn_fwd_B_real, L0_attn_fwd_B_imag, L0_attn_fwd_C_real, L0_attn_fwd_C_imag, L0_attn_fwd_D, L0_attn_bwd_log_real, L0_attn_bwd_imag, L0_attn_bwd_log_Delta, L0_attn_bwd_B_real, L0_attn_bwd_B_imag, L0_attn_bwd_C_real, L0_attn_bwd_C_imag, L0_attn_bwd_D, L0_ffn_Wq_pk, L0_ffn_pk_keys, L0_ffn_Wq, L0_ffn_keys_table, L0_ffn_values_table, L0_ffn_Wo, L1_attn_qkv_w, L1_attn_qkv_b, L1_attn_proj_w, L1_attn_proj_b, L1_ffn_router_w, L1_ffn_w1, L1_ffn_b1, L1_ffn_w2, L1_ffn_b2):
    import jax
    import jax.numpy as jnp

    def _L0_tok_ref(event_type, fault_class, syscall_class, opcode_family, transition_type, result_class, E_et, E_fc, E_sc, E_of, E_tt, E_rc, W, b, gamma, beta):
        import jax, jax.numpy as jnp
        import numpy as np
        B, S = (128, 512)
        D_OUT = 64
        EMB = 16
        EPS_W = 1e-08
        EPS_LN = 1e-05

        def ternary_linear(x, W, b):
            scale = jnp.mean(jnp.abs(W))
            w_q = jnp.clip(jnp.round(W / (scale + EPS_W)), -1.0, 1.0) * scale
            w_eff = W + jax.lax.stop_gradient(w_q - W)
            return jnp.einsum('bsk,ok->bso', x, w_eff) + b

        def layer_norm(x, gamma, beta):
            mu = jnp.mean(x, axis=-1, keepdims=True)
            var = jnp.mean(jnp.square(x - mu), axis=-1, keepdims=True)
            return (x - mu) * jax.lax.rsqrt(var + EPS_LN) * gamma + beta
        combined = jnp.concatenate([E_et[event_type], E_fc[fault_class], E_sc[syscall_class], E_of[opcode_family], E_tt[transition_type], E_rc[result_class]], axis=-1)
        z = ternary_linear(combined, W, b)
        return layer_norm(z, gamma, beta)

    def _L0_attn_ref(x, fwd_log_real, fwd_imag, fwd_log_Delta, fwd_B_real, fwd_B_imag, fwd_C_real, fwd_C_imag, fwd_D, bwd_log_real, bwd_imag, bwd_log_Delta, bwd_B_real, bwd_B_imag, bwd_C_real, bwd_C_imag, bwd_D):
        import jax, jax.numpy as jnp
        import numpy as np
        B, L, H, P = (4, 2048, 64, 64)

        def discretize(log_real, imag, log_Delta, B_real, B_imag):
            Lr = -jnp.exp(log_real)
            Li = imag
            Delta = jnp.exp(log_Delta)
            ad = Lr * Delta
            bd = Li * Delta
            exp_ad = jnp.exp(ad)
            Lbar_r = exp_ad * jnp.cos(bd)
            Lbar_i = exp_ad * jnp.sin(bd)
            denom = jnp.maximum(Lr * Lr + Li * Li, 1e-12)
            inv_Lr = Lr / denom
            inv_Li = -Li / denom
            diff_r = Lbar_r - 1.0
            diff_i = Lbar_i
            coeff_r = inv_Lr * diff_r - inv_Li * diff_i
            coeff_i = inv_Lr * diff_i + inv_Li * diff_r
            B_bar_r = coeff_r[:, None] * B_real - coeff_i[:, None] * B_imag
            B_bar_i = coeff_r[:, None] * B_imag + coeff_i[:, None] * B_real
            return (Lbar_r, Lbar_i, B_bar_r, B_bar_i)

        def binop(ei, ej):
            Ar_i, Ai_i, xr_i, xi_i = ei
            Ar_j, Ai_j, xr_j, xi_j = ej
            return (Ar_j * Ar_i - Ai_j * Ai_i, Ar_j * Ai_i + Ai_j * Ar_i, Ar_j * xr_i - Ai_j * xi_i + xr_j, Ar_j * xi_i + Ai_j * xr_i + xi_j)

        def apply_ssm(Lbar_r, Lbar_i, B_bar_r, B_bar_i, C_real, C_imag, D, x):
            Bu_r = jnp.einsum('blh,ph->blp', x, B_bar_r)
            Bu_i = jnp.einsum('blh,ph->blp', x, B_bar_i)
            A_r = jnp.broadcast_to(Lbar_r, Bu_r.shape)
            A_i = jnp.broadcast_to(Lbar_i, Bu_i.shape)
            _, _, xs_r, xs_i = jax.lax.associative_scan(binop, (A_r, A_i, Bu_r, Bu_i), axis=1)
            ys = jnp.einsum('blp,hp->blh', xs_r, C_real) - jnp.einsum('blp,hp->blh', xs_i, C_imag)
            return ys + D * x

        def s5(log_real, imag, log_Delta, B_real, B_imag, C_real, C_imag, D, x):
            Lbar_r, Lbar_i, B_bar_r, B_bar_i = discretize(log_real, imag, log_Delta, B_real, B_imag)
            y = apply_ssm(Lbar_r, Lbar_i, B_bar_r, B_bar_i, C_real, C_imag, D, x)
            return jax.nn.gelu(y, approximate=False)
        x_flip = jnp.flip(x, axis=1)
        y_f = s5(fwd_log_real, fwd_imag, fwd_log_Delta, fwd_B_real, fwd_B_imag, fwd_C_real, fwd_C_imag, fwd_D, x)
        y_b = s5(bwd_log_real, bwd_imag, bwd_log_Delta, bwd_B_real, bwd_B_imag, bwd_C_real, bwd_C_imag, bwd_D, x_flip)
        return y_f + jnp.flip(y_b, axis=1)

    def _L0_ffn_ref(x, Wq_pk, pk_keys, Wq, keys_table, values_table, Wo):
        import jax, jax.numpy as jnp
        import numpy as np
        DIM = 64
        HEADS = 8
        NUM_KEYS = 64
        NUM_KV = NUM_KEYS ** 2
        PK_TOPK = 16
        FINAL_TOPK = 16
        DIM_KEY = DIM // 2
        P = 2

        def _pk(x, Wq_pk, pk_keys):
            b, n, _ = x.shape
            q = (x @ Wq_pk).reshape(b, n, P, HEADS, DIM_KEY).transpose(2, 0, 1, 3, 4)
            sim = jnp.einsum('pbnhd,pkhd->pbnhk', q, pk_keys)
            scores, idx = jax.lax.top_k(sim, PK_TOPK)
            idx0 = idx[0]
            idx1 = idx[1] * NUM_KEYS
            index = (idx0[..., :, None] + idx1[..., None, :]).reshape(b, n, HEADS, PK_TOPK * PK_TOPK)
            score = (scores[0][..., :, None] + scores[1][..., None, :]).reshape(b, n, HEADS, PK_TOPK * PK_TOPK)
            final_scores, pk_idx = jax.lax.top_k(score, FINAL_TOPK)
            final_indices = jnp.take_along_axis(index, pk_idx, axis=-1)
            final_scores = jax.nn.softmax(final_scores, axis=-1)
            return (final_scores, final_indices)
        b, n, d = x.shape
        q = (x @ Wq).reshape(b, n, HEADS, DIM) * DIM ** (-0.5)
        kv_scores, indices = _pk(x, Wq_pk, pk_keys)
        offsets = jnp.arange(HEADS, dtype=indices.dtype) * NUM_KV
        ind = indices + offsets[None, None, :, None]
        k = jnp.einsum('bnhk,bnhkd->bnhd', kv_scores, keys_table[ind])
        v = jnp.einsum('bnhk,bnhkd->bnhd', kv_scores, values_table[ind])
        sim = jnp.einsum('bihd,bjhd->bhij', q, k)
        neg = -jnp.finfo(sim.dtype).max
        causal = jnp.tril(jnp.ones((n, n), dtype=bool))
        sim = jnp.where(causal, sim, neg)
        attn = jax.nn.softmax(sim, axis=-1)
        out = jnp.einsum('bhij,bjhd->bhid', attn, v)
        out = out.transpose(0, 2, 1, 3).reshape(b, n, HEADS * DIM)
        return out @ Wo

    def _L1_attn_ref(x, qkv_w, qkv_b, proj_w, proj_b):
        import jax, jax.numpy as jnp
        import numpy as np
        B, N, C = (2, 12500, 64)
        H, W = (8, 64)
        HD = C // H
        Bv, Nv, Cv = x.shape
        pad = (W - Nv % W) % W
        xp = jnp.pad(x, ((0, 0), (0, pad), (0, 0)))
        nW = (Nv + pad) // W
        xw = xp.reshape(Bv, nW, W, Cv)
        qkv = xw @ qkv_w + qkv_b
        qkv = qkv.reshape(Bv, nW, W, 3, H, HD)
        q, k, v = (qkv[..., 0, :, :], qkv[..., 1, :, :], qkv[..., 2, :, :])
        scale = HD ** (-0.5)
        attn = jnp.einsum('bwihd,bwjhd->bwhij', q, k) * scale
        attn = jax.nn.softmax(attn, axis=-1)
        out = jnp.einsum('bwhij,bwjhd->bwihd', attn, v)
        out = out.reshape(Bv, nW, W, Cv)
        out = out @ proj_w + proj_b
        out = out.reshape(Bv, nW * W, Cv)[:, :Nv]
        return out

    def _L1_ffn_ref(input_embeddings, router_w, w1, b1, w2, b2):
        import jax, jax.numpy as jnp
        import numpy as np
        NUM_EXPERTS = 8
        TOP_K = 2
        B, S, D = (8, 2048, 64)

        def _moe(tokens, router_w, w1, b1, w2, b2):
            N = tokens.shape[0]
            E = router_w.shape[0]
            logits = tokens.astype(jnp.float32) @ router_w.astype(jnp.float32).T
            probs = jax.nn.softmax(logits, axis=-1)
            rw, re = jax.lax.top_k(probs, TOP_K)
            if TOP_K > 1:
                rw = rw / jnp.maximum(rw.sum(-1, keepdims=True), 1e-12)
            rw = rw.astype(tokens.dtype)
            combine = jnp.zeros((N, E), tokens.dtype).at[jnp.arange(N)[:, None], re].set(rw)
            out = tokens
            for e in range(E):
                h = jax.nn.gelu(tokens @ w1[e] + b1[e], approximate=False)
                y = h @ w2[e] + b2[e]
                out = out + combine[:, e:e + 1] * y
            return out
        b, s, d = input_embeddings.shape
        tokens = input_embeddings.reshape(b * s, d)
        return _moe(tokens, router_w, w1, b1, w2, b2).reshape(b, s, d)
    h = _L0_tok_ref(x, itok_BS_0_255, itok_BS_0_511, itok_BS_0_127, itok_BS_0_63, itok_BS_0_3, L0_tok_E_et, L0_tok_E_fc, L0_tok_E_sc, L0_tok_E_of, L0_tok_E_tt, L0_tok_E_rc, L0_tok_W, L0_tok_b, L0_tok_gamma, L0_tok_beta)
    h = h + _L0_attn_ref(_layernorm(h, axis=-1), L0_attn_fwd_log_real, L0_attn_fwd_imag, L0_attn_fwd_log_Delta, L0_attn_fwd_B_real, L0_attn_fwd_B_imag, L0_attn_fwd_C_real, L0_attn_fwd_C_imag, L0_attn_fwd_D, L0_attn_bwd_log_real, L0_attn_bwd_imag, L0_attn_bwd_log_Delta, L0_attn_bwd_B_real, L0_attn_bwd_B_imag, L0_attn_bwd_C_real, L0_attn_bwd_C_imag, L0_attn_bwd_D)
    h = h + _L0_ffn_ref(_layernorm(h, axis=-1), L0_ffn_Wq_pk, L0_ffn_pk_keys, L0_ffn_Wq, L0_ffn_keys_table, L0_ffn_values_table, L0_ffn_Wo)
    h = h + _L1_attn_ref(_layernorm(h, axis=-1), L1_attn_qkv_w, L1_attn_qkv_b, L1_attn_proj_w, L1_attn_proj_b)
    h = h + _L1_ffn_ref(_layernorm(h, axis=-1), L1_ffn_router_w, L1_ffn_w1, L1_ffn_b1, L1_ffn_w2, L1_ffn_b2)
    return h

_drawn_inputs = setup_inputs


def setup_inputs(seed=0):
    import zlib

    import numpy as np

    out = dict(_drawn_inputs(seed))
    spreads = {'L0_tok_b': (0.0, 0.1),
     'L0_tok_gamma': (1.0, 0.2),
     'L0_tok_beta': (0.0, 0.1),
     'L0_attn_fwd_log_Delta': (0.0, 0.1),
     'L0_attn_fwd_D': (1.0, 0.2),
     'L0_attn_bwd_log_Delta': (0.0, 0.1),
     'L0_attn_bwd_D': (1.0, 0.2),
     'L1_ffn_b1': (0.0, 0.566),
     'L1_ffn_b2': (0.0, 0.354)}
    factors = {'L0_ffn_Wq_pk': 29.273,
     'L0_ffn_pk_keys': 27.477,
     'L0_ffn_Wq': 64.0,
     'L0_ffn_keys_table': 64.0,
     'L0_ffn_values_table': 26.267,
     'L0_ffn_Wo': 25.359,
     'L1_attn_qkv_w': 3.522,
     'L1_attn_qkv_b': 6.12,
     'L1_attn_proj_w': 3.074,
     'L1_attn_proj_b': 4.038}
    for name, (base, spread) in spreads.items():
        noise = np.random.default_rng([zlib.crc32(name.encode()), seed]).standard_normal(out[name].shape)
        drawn = base * np.exp(spread * noise) if base else spread * noise
        out[name] = jnp.asarray(drawn.astype(out[name].dtype))
    for name, factor in factors.items():
        out[name] = (out[name] * factor).astype(out[name].dtype)
    return out
```

```python
from contextlib import ExitStack

import concourse.bass as bass
from concourse import mybir

F32 = mybir.dt.float32
F16 = mybir.dt.float16
BF16 = mybir.dt.bfloat16
I32 = mybir.dt.int32
ALU = mybir.AluOpType
ACT = mybir.ActivationFunctionType
AX = mybir.AxisListType

P = 128
B, S, D = 16, 512, 64
TT = S // P
NT = B * TT
EPS = 1e-5
ROUND = 1.5 * 2.0 ** 23

VOCAB = {0: ((0, 0, 64), (1, 64, 64)), 1: ((2, 0, 128),), 2: ((3, 0, 128),), 3: ((4, 0, 64), (5, 64, 4))}
ROWS = (128, 128, 128, 68)
EMB = 96

H = 8
DK = 32
NK = 64
JT = NK * NK // P
TOPK = 16
SHIFT = 44.0
CAP = 2 * SHIFT
LEAD = 2
W = 64
HD = D // H
EXPERTS = 8


class Chain:

    def __init__(self, eng, sem, base=0):
        self.eng, self.sem, self.base, self.n = eng, sem, base, 0

    def add(self, ins):
        ins.then_inc(self.sem, 1)
        self.n += 1

    def wait(self):
        self.eng.wait_ge(self.sem, self.base + self.n)

    def link(self, ins):
        self.add(ins)
        self.wait()


def hold(eng, sem):
    eng.sem_inc(sem, 1)


def bcast(ap, shape):
    return ap.broadcast_to(shape)


def program(nc, io, out, phases=9):
    with ExitStack() as ctx:
        def sb(name, shape, dt=F32, scope=ctx):
            return scope.enter_context(nc.sbuf_tensor(name, shape, dt))

        bank = [ctx.enter_context(nc.psum_tensor(f"bank{i}", [P, 512], F32)) for i in range(8)]
        k = {
            "sb": sb, "bank": bank,
            "h": sb("h", [P, NT, D]),
            "cen": sb("cen", [P, NT, D]),
            "rstd": sb("rstd", [P, NT]),
            "ident": sb("ident", [P, P]),
        }
        with ExitStack() as ssm:
            k["ssm"] = {
                "inw": sb("ssm_inw", [D, 2, 2, P], scope=ssm),
                "outw": sb("ssm_outw", [P, 2, 2, D], scope=ssm),
                "skip": sb("ssm_skip", [D, 2, D], scope=ssm),
                "cos": sb("ssm_cos", [P, 2, S], scope=ssm),
                "sin": sb("ssm_sin", [P, 2, S], scope=ssm),
                "decay": sb("ssm_decay", [P, 2, S], scope=ssm),
            }
            with ExitStack() as emb:
                k["rowtab"] = sb("rowtab", [P, 4, D], scope=emb)
                prepare(nc, io, k)
                embed(nc, io, k)
            if phases >= 1:
                norm_affine(nc, io, k)
                ssm_layer(nc, io, k)
        if phases >= 3:
            statistics(nc, k, "pk")
            product_key_layer(nc, io, k)
        if phases >= 4:
            statistics(nc, k, "win")
            window_attention(nc, io, k)
        if phases >= 5:
            statistics(nc, k, "moe")
            experts(nc, io, k)
        store(nc, k, out)


def prepare(nc, io, k):
    bank, ssm = k["bank"], k["ssm"]
    with ExitStack() as c:
        def sb(name, shape, dt=F32):
            return c.enter_context(nc.sbuf_tensor(name, shape, dt))

        def sem(name):
            return c.enter_context(nc.semaphore(name))

        wt = sb("wt", [EMB + 1, D])
        tern = sb("tern", [EMB, D])
        tab = sb("tab", [EMB + 1, 4 * P])
        ones = sb("ones", [EMB, EMB])
        colsum = sb("colsum", [EMB, 4])
        prm = sb("prm", [P, 2, 3])
        bx = sb("bx", [P, 2, 2, D])
        cx = sb("cx", [P, 2, 2, D])
        dx = sb("dx", [D, 2])
        sgn = sb("sgn", [P, 1])
        g = sb("g", [P, 2, 2, D])
        q = sb("q", [P, 24, 2])
        tmp = sb("tmp", [P, 2, S // 2])
        loaded = sem("p_loaded")
        dve = sem("p_dve")
        act_done = sem("p_act")
        pe_done = sem("p_pe")
        act_need = sem("p_act_need")
        block = c.enter_context(nc.Block())
        LR, IM, LD, DEL, AD, BD, R, N1, ARG, SN, CS, NRM, LBR, LBI, DEN, IR, II, T0, T1, CR, CI, SCI, SCR, ARGC = range(24)

        def v(i):
            return q[:, i, :]

        @block.sync
        def _(sp):
            loads = [(k["ident"][:], io["ident"]), (wt[0:EMB, :], io["w_t"]), (wt[EMB:EMB + 1, :], io["w_bias"]),
                     (tab[:], io["tables_t"]), (prm[:], io["ssm_prm"]), (bx[:], io["ssm_b"]), (cx[:], io["ssm_c"]),
                     (dx[:], io["ssm_d"]), (sgn[:], io["sign_half"])]
            for dst, src in loads:
                sp.dma_start(dst, src).then_inc(loaded, 16)

        NLOAD = 9 * 16

        @block.scalar
        def _(act):
            act.wait_ge(loaded, NLOAD)
            nc.scalar.activation(v(LR), prm[:, :, 0], ACT.Exp).then_inc(act_done, 1)
            nc.scalar.activation(v(DEL), prm[:, :, 2], ACT.Exp).then_inc(act_done, 1)
            act.wait_ge(act_need, 1)
            nc.scalar.activation(v(R), v(AD), ACT.Exp).then_inc(act_done, 1)
            act.wait_ge(act_need, 2)
            nc.scalar.activation(v(SN), v(ARG), ACT.Sin).then_inc(act_done, 1)
            nc.scalar.activation(v(CS), v(ARGC), ACT.Sin).then_inc(act_done, 1)

        @block.tensor
        def _(pe):
            pe.wait_ge(loaded, NLOAD)
            pe.wait_ge(act_need, 3)
            nc.tensor.matmul(bank[0][0:EMB, 0:1], ones[:], colsum[:, 0:1], start=True, stop=True).then_inc(pe_done, 1)
            pe.wait_ge(act_need, 4)
            for ch in range(4):
                last = nc.tensor.matmul(bank[1][:, ch * D:(ch + 1) * D], tab[:, ch * P:(ch + 1) * P], wt[:],
                                        start=True, stop=True)
            last.then_inc(pe_done, 1)
            pe.wait_ge(act_need, 5)
            for d in range(2):
                for j in range(2):
                    last = nc.tensor.transpose(bank[2][0:D, (2 * d + j) * P:(2 * d + j + 1) * P], g[:, d, j, :],
                                               k["ident"][:])
            last.then_inc(pe_done, 1)

        @block.vector
        def _(e):
            ch = Chain(e, dve)
            V = nc.vector
            turn = (6.28125, 0.0019353071795864769)

            def tt(o, a, b, op):
                ch.link(V.tensor_tensor(o, a, b, op))

            def ts(o, a, s1, s2, op0, op1=None):
                ch.link(V.tensor_scalar(o, a, s1, s2, op0, op1) if op1 is not None else V.tensor_scalar(o, a, s1, s2, op0))

            e.wait_ge(loaded, NLOAD)
            e.wait_ge(act_done, 2)
            ts(v(LR), v(LR), -1.0, None, ALU.mult)
            tt(v(AD), v(LR), v(DEL), ALU.mult)
            V.tensor_tensor(v(BD), prm[:, :, 1], v(DEL), ALU.mult).then_inc(act_need, 1)
            e.wait_ge(act_need, 1)
            for dst, add in ((ARG, 0.0), (ARGC, 1.5707963267948966)):
                ts(v(BD if add else T0), v(BD), add, None, ALU.add)
                ts(v(N1), v(BD), 1.0 / 6.283185307179586, None, ALU.mult)
                ts(v(N1), v(N1), ROUND, None, ALU.add)
                ts(v(N1), v(N1), -ROUND, None, ALU.add)
                ts(v(T1), v(N1), -turn[0], None, ALU.mult)
                tt(v(dst), v(BD), v(T1), ALU.add)
                ts(v(T1), v(N1), -turn[1], None, ALU.mult)
                tt(v(dst), v(dst), v(T1), ALU.add)
                ts(v(dst), v(dst), -3.1415925, 3.1415925, ALU.max, ALU.min)
            V.memset(ones[:], 1.0).then_inc(act_need, 1)
            e.wait_ge(act_need, 2)
            V.tensor_reduce(colsum[:, 0:1], wt[0:EMB, :], AX.X, ALU.add, apply_absolute_value=True).then_inc(act_need, 1)
            e.wait_ge(pe_done, 1)
            ts(colsum[:, 1:2], bank[0][0:EMB, 0:1], 1.0 / (EMB * D), None, ALU.mult)
            ts(colsum[:, 2:3], colsum[:, 1:2], 1e-8, None, ALU.add)
            ch.link(V.reciprocal(colsum[:, 3:4], colsum[:, 2:3]))
            ts(tern[:], wt[0:EMB, :], colsum[:, 3:4], None, ALU.mult)
            ts(tern[:], tern[:], ROUND, None, ALU.add)
            ts(tern[:], tern[:], -ROUND, None, ALU.add)
            ts(tern[:], tern[:], -1.0, 1.0, ALU.max, ALU.min)
            ts(tern[:], tern[:], colsum[:, 1:2], None, ALU.mult)
            tt(tern[:], tern[:], wt[0:EMB, :], ALU.subtract)
            V.tensor_tensor(wt[0:EMB, :], wt[0:EMB, :], tern[:], ALU.add).then_inc(act_need, 1)
            e.wait_ge(act_need, 4)
            e.wait_ge(pe_done, 2)
            ch.link(V.tensor_copy(k["rowtab"][:], bank[1][:, 0:4 * D].rearrange("p (c d) -> p c d", c=4)))
            e.wait_ge(act_done, 5)

            def unit():
                tt(v(T0), v(CS), v(CS), ALU.mult)
                tt(v(T1), v(SN), v(SN), ALU.mult)
                tt(v(NRM), v(T0), v(T1), ALU.add)
                ts(v(NRM), v(NRM), -0.5, 1.5, ALU.mult, ALU.add)
                tt(v(CS), v(CS), v(NRM), ALU.mult)
                tt(v(SN), v(SN), v(NRM), ALU.mult)

            unit()
            tt(v(LBR), v(R), v(CS), ALU.mult)
            tt(v(LBI), v(R), v(SN), ALU.mult)
            tt(v(T0), v(LR), v(LR), ALU.mult)
            tt(v(T1), prm[:, :, 1], prm[:, :, 1], ALU.mult)
            tt(v(DEN), v(T0), v(T1), ALU.add)
            ts(v(DEN), v(DEN), 1e-12, None, ALU.max)
            ch.link(V.reciprocal(v(DEN), v(DEN)))
            tt(v(IR), v(LR), v(DEN), ALU.mult)
            tt(v(II), prm[:, :, 1], v(DEN), ALU.mult)
            ts(v(II), v(II), -1.0, None, ALU.mult)
            ts(v(LBR), v(LBR), -1.0, None, ALU.add)
            tt(v(T0), v(IR), v(LBR), ALU.mult)
            tt(v(T1), v(II), v(LBI), ALU.mult)
            tt(v(CR), v(T0), v(T1), ALU.subtract)
            tt(v(T0), v(IR), v(LBI), ALU.mult)
            tt(v(T1), v(II), v(LBR), ALU.mult)
            tt(v(CI), v(T0), v(T1), ALU.add)
            ts(v(SCI), v(CI), sgn[:, 0:1], None, ALU.mult)
            ts(v(SCR), v(CR), sgn[:, 0:1], None, ALU.mult)
            for d in range(2):
                ts(g[:, d, 0, :], bx[:, d, 1, :], q[:, SCI, d:d + 1], -1.0, ALU.mult, ALU.mult)
                ch.link(V.scalar_tensor_tensor(g[:, d, 0, :], bx[:, d, 0, :], q[:, CR, d:d + 1], g[:, d, 0, :],
                                               ALU.mult, ALU.add))
                ts(g[:, d, 1, :], bx[:, d, 1, :], q[:, SCR, d:d + 1], None, ALU.mult)
                ch.link(V.scalar_tensor_tensor(g[:, d, 1, :], bx[:, d, 0, :], q[:, CI, d:d + 1], g[:, d, 1, :],
                                               ALU.mult, ALU.add))
                ts(ssm["outw"][:, d, 0, :], cx[:, d, 0, :], sgn[:, 0:1], None, ALU.mult)
                ts(ssm["outw"][:, d, 1, :], cx[:, d, 1, :], -1.0, None, ALU.mult)
                ts(ssm["skip"][:, d, :], k["ident"][0:D, 0:D], dx[:, d:d + 1], None, ALU.mult)
            V.memset(ssm["cos"][:, :, 0:1], 1.0).then_inc(act_need, 1)
            e.wait_ge(act_need, 5)
            ch.link(V.memset(ssm["sin"][:, :, 0:1], 0.0))
            ch.link(V.memset(ssm["decay"][:], 1.0))
            for d in range(2):
                ts(ssm["decay"][:, d, :], ssm["decay"][:, d, :], q[:, R, d:d + 1], None, ALU.mult)
            n = 1
            while n < S:
                for d in range(2):
                    old_c, old_s = ssm["cos"][:, d, 0:n], ssm["sin"][:, d, 0:n]
                    new_c, new_s = ssm["cos"][:, d, n:2 * n], ssm["sin"][:, d, n:2 * n]
                    cs, sn = q[:, CS, d:d + 1], q[:, SN, d:d + 1]
                    ch.add(V.tensor_scalar(tmp[:, 0, 0:n], old_s, sn, None, ALU.mult))
                    ch.link(V.tensor_scalar(tmp[:, 1, 0:n], old_c, sn, None, ALU.mult))
                    ch.add(V.scalar_tensor_tensor(new_c, old_c, cs, tmp[:, 0, 0:n], ALU.mult, ALU.subtract))
                    ch.link(V.scalar_tensor_tensor(new_s, old_s, cs, tmp[:, 1, 0:n], ALU.mult, ALU.add))
                n *= 2
                if n < S:
                    tt(v(T0), v(CS), v(CS), ALU.mult)
                    tt(v(T1), v(SN), v(SN), ALU.mult)
                    tt(v(NRM), v(CS), v(SN), ALU.mult)
                    tt(v(CS), v(T0), v(T1), ALU.subtract)
                    ts(v(SN), v(NRM), 2.0, None, ALU.mult)
                    unit()
            e.wait_ge(pe_done, 3)
            ch.link(V.tensor_copy(ssm["inw"][:], bank[2][0:D, :].rearrange("p (d j s) -> p d j s", d=2, j=2)))


def embed(nc, io, k):
    bank, h = k["bank"], k["h"]
    with ExitStack() as c:
        def sb(name, shape, dt=F32):
            return c.enter_context(nc.sbuf_tensor(name, shape, dt))

        def sem(name):
            return c.enter_context(nc.semaphore(name))

        ids = sb("ids", [P, 2, 4, S], I32)
        hot = sb("hot", [P, 2, 4, S])
        rowid = sb("rowid", [P, 4])
        row_ready = sem("e_row")
        ids_ready = [sem("e_ids0"), sem("e_ids1")]
        hot_ready, z_ready, z_used = sem("e_hot"), sem("e_z"), sem("e_used")
        block = c.enter_context(nc.Block())
        names = ["id0", "id1", "id2", "id3", "id4", "id5"]

        @block.sync
        def _(sp):
            sp.dma_start(rowid[:], io["rowid"]).then_inc(row_ready, 16)

            def load(b, j):
                for chn, parts in VOCAB.items():
                    for which, first, n in parts:
                        sp.dma_start(ids[first:first + n, j, chn, :],
                                     bcast(io[names[which]][bass.ds(b, 1), :], [n, S])).then_inc(ids_ready[j], 16)

            for j in range(2):
                load(j, j)
            with sp.Fori(1, B // 2) as i:
                for j in range(2):
                    sp.wait_ge(hot_ready, (2 * i + j - 1) * 4)
                    load(2 * i + j, j)

        @block.vector
        def _(e):
            e.wait_ge(row_ready, 16)
            e.sem_inc(z_used, 2)
            with e.Fori(0, B // 2) as i:
                for j in range(2):
                    e.wait_ge(ids_ready[j], (i + 1) * 96)
                    e.wait_ge(z_used, 2 * i + j + 1)
                    for chn in range(4):
                        n = ROWS[chn]
                        nc.vector.tensor_scalar(hot[0:n, j, chn, :], ids[0:n, j, chn, :], rowid[0:n, chn:chn + 1],
                                                None, ALU.is_equal).then_inc(hot_ready, 1)

        @block.tensor
        def _(pe):
            with pe.Fori(0, B // 2) as i:
                for j in range(2):
                    pe.wait_ge(hot_ready, (2 * i + j + 1) * 4)
                    pe.wait_ge(z_used, 2 * i + j + 1)
                    for t in range(TT):
                        for chn in range(4):
                            n = ROWS[chn]
                            last = nc.tensor.matmul(bank[j][:, t * D:(t + 1) * D], hot[0:n, j, chn, t * P:(t + 1) * P],
                                                    k["rowtab"][0:n, chn, :], start=(chn == 0), stop=(chn == 3))
                    last.then_inc(z_ready, 1)

        @block.scalar
        def _(act):
            with act.Fori(0, B // 2) as i:
                for j in range(2):
                    act.wait_ge(z_ready, 2 * i + j + 1)
                    nc.scalar.activation(h[:, bass.ds((2 * i + j) * TT, TT), :],
                                         bank[j][:, 0:TT * D].rearrange("p (t d) -> p t d", t=TT),
                                         ACT.Copy).then_inc(z_used, 1)


def statistics(nc, k, tag, affine=None):
    h, cen, rstd = k["h"], k["cen"], k["rstd"]
    Q = 4
    N = NT // Q
    with ExitStack() as c:
        def sb(name, shape, dt=F32):
            return c.enter_context(nc.sbuf_tensor(f"{tag}_{name}", shape, dt))

        def sem(name):
            return c.enter_context(nc.semaphore(f"{tag}_{name}"))

        sq = sb("sq", [P, NT, D])
        st = sb("st", [P, 2, NT])
        gb = sb("gb", [P, 2, D])
        dve, centred, squared, var, std, loaded = (sem(x) for x in ("dve", "cen", "sq", "var", "std", "ld"))
        block = c.enter_context(nc.Block())

        if affine is not None:
            @block.sync
            def _(sp):
                sp.dma_start(gb[:], affine).then_inc(loaded, 16)

        @block.scalar
        def _(act):
            for i in range(Q):
                s = slice(i * N, (i + 1) * N)
                act.wait_ge(centred, i + 1)
                nc.scalar.activation(sq[:, s, :], cen[:, s, :], ACT.Square).then_inc(squared, 1)
            for i in range(Q):
                s = slice(i * N, (i + 1) * N)
                act.wait_ge(var, i + 1)
                nc.scalar.activation(st[:, 1, s], st[:, 0, s], ACT.Sqrt).then_inc(std, 1)

        @block.vector
        def _(e):
            V = nc.vector
            ch = Chain(e, dve)
            for i in range(Q):
                s = slice(i * N, (i + 1) * N)
                ch.link(V.tensor_reduce(st[:, 0, s], h[:, s, :], AX.X, ALU.add))
                ch.link(V.tensor_scalar(st[:, 0, s], st[:, 0, s], 1.0 / D, None, ALU.mult))
                V.tensor_tensor(cen[:, s, :], h[:, s, :], bcast(st[:, 0, s].unsqueeze(2), [P, N, D]),
                                ALU.subtract).then_inc(centred, 1)
            for i in range(Q):
                s = slice(i * N, (i + 1) * N)
                e.wait_ge(squared, i + 1)
                ch.link(V.tensor_reduce(st[:, 0, s], sq[:, s, :], AX.X, ALU.add))
                V.tensor_scalar(st[:, 0, s], st[:, 0, s], 1.0 / D, EPS, ALU.mult, ALU.add).then_inc(var, 1)
            for i in range(Q):
                s = slice(i * N, (i + 1) * N)
                e.wait_ge(std, i + 1)
                ch.link(V.reciprocal(rstd[:, s], st[:, 1, s]))
                if affine is not None:
                    if i == 0:
                        e.wait_ge(loaded, 16)
                        e.wait_ge(centred, Q)
                    ch.link(V.tensor_tensor(h[:, s, :], cen[:, s, :], bcast(rstd[:, s].unsqueeze(2), [P, N, D]), ALU.mult))
                    ch.link(V.tensor_tensor(h[:, s, :], h[:, s, :], bcast(gb[:, 0:1, :], [P, N, D]), ALU.mult))
                    ch.link(V.tensor_tensor(h[:, s, :], h[:, s, :], bcast(gb[:, 1:2, :], [P, N, D]), ALU.add))


def norm_affine(nc, io, k):
    statistics(nc, k, "tok", io["gamma_beta"])
    statistics(nc, k, "ssm")


def ssm_layer(nc, io, k):
    bank, h, cen, rstd, ssm = k["bank"], k["h"], k["cen"], k["rstd"], k["ssm"]
    with ExitStack() as c:
        def sb(name, shape, dt=F32):
            return c.enter_context(nc.sbuf_tensor(f"s_{name}", shape, dt))

        def sem(name):
            return c.enter_context(nc.semaphore(f"s_{name}"))

        stage = sb("stage", [P, 2, TT, D])
        xs = sb("xs", [D, 2, S])
        part = sb("part", [P, 2, 2, S])
        turned = sb("turned", [P, 2, S])
        state = sb("state", [P, 2, 2, S])
        back = sb("back", [P, 2, 2, 2, S])
        act_out = sb("act_out", [P, B, 2, TT * D])
        staged, turned_t, xs_ready, u_ready, u_used, parts, sums, scanned, backed, y_ready, y_used, added = (
            sem(x) for x in ("staged", "tr", "xs", "u", "uused", "parts", "sums", "scan", "back", "y", "yused", "added"))
        held = sem("held")
        block = c.enter_context(nc.Block())

        def along(table, d):
            return ssm[table][:, d, :] if d == 0 else ssm[table][:, d, ::-1]

        @block.tensor
        def _(pe):
            def transposes(g, j):
                pe.wait_ge(staged, g + 1)
                hold(pe, held)
                for t in range(TT):
                    last = nc.tensor.transpose(bank[0][0:D, t * P:(t + 1) * P], stage[:, j, t, :], k["ident"][:])
                last.then_inc(turned_t, 1)

            def inputs(g, j):
                pe.wait_ge(xs_ready, g + 1)
                for d in range(2):
                    for half in range(2):
                        pe.wait_ge(u_used, g * 4 + 2 * d + half + 1)
                        nc.tensor.matmul(bank[1 + 2 * d + half][:], ssm["inw"][:, d, half, :], xs[:, j, :],
                                         start=True, stop=True).then_inc(u_ready, 1)

            def outputs(g, j):
                pe.wait_ge(y_used, g + 1)
                pe.wait_ge(backed, 4 * g + 4)
                for d in range(2):
                    for t in range(TT):
                        o = bank[5 + j][:, (d * TT + t) * D:(d * TT + t + 1) * D]
                        s = slice(t * P, (t + 1) * P)
                        nc.tensor.matmul(o, back[:, j, d, 0, s], ssm["outw"][:, d, 0, :], start=True, stop=False)
                        nc.tensor.matmul(o, back[:, j, d, 1, s], ssm["outw"][:, d, 1, :], start=False, stop=False)
                        last = nc.tensor.matmul(o, xs[:, j, s], ssm["skip"][:, d, :], start=False, stop=True)
                last.then_inc(y_ready, 1)

            transposes(0, 0)
            pe.wait_ge(xs_ready, 1)
            transposes(1, 1)
            inputs(0, 0)
            with pe.Fori(0, B // 2) as i:
                for j in range(2):
                    g = 2 * i + j
                    inputs(g + 1, 1 - j)
                    transposes(g + 2, j)
                    outputs(g, j)

        @block.scalar
        def _(act):
            def copy(g, j):
                act.wait_ge(turned_t, g + 1)
                nc.scalar.activation(xs[:, j, :], bank[0][0:D, :], ACT.Copy).then_inc(xs_ready, 1)

            act.sem_inc(y_used, 2)
            copy(0, 0)
            copy(1, 1)
            with act.Fori(0, B // 2) as i:
                for j in range(2):
                    g = 2 * i + j
                    act.wait_ge(y_ready, g + 1)
                    copy(g + 2, j)
                    nc.scalar.activation(act_out[:, bass.ds(g, 1), :, :],
                                         bank[5 + j][:].rearrange("p (o d x) -> p o d x", o=1, d=2),
                                         ACT.Gelu).then_inc(y_used, 1)

        @block.gpsimd
        def _(pool):
            pool.sem_inc(sums, 1)
            with pool.Fori(0, B // 2) as i:
                for j in range(2):
                    g = 2 * i + j
                    pool.wait_ge(parts, g + 1)
                    nc.gpsimd.tensor_tensor(turned[:, 1, :], part[:, 1, 0, :], part[:, 1, 1, :], ALU.add).then_inc(sums, 1)
                    pool.wait_ge(y_used, g + 1)
                    for d in range(2):
                        pool.wait_ge(scanned, 2 * g + d + 1)
                        for half, table in enumerate(("cos", "sin")):
                            nc.gpsimd.tensor_tensor(back[:, j, d, half, :], state[:, j, d, :], along(table, d),
                                                    ALU.mult).then_inc(backed, 1)
            s = slice(0, B // 4)
            pool.wait_ge(y_used, B + 2)
            hs = h[:, 0:NT // 4, :].rearrange("p (b t) d -> p b (t d)", b=B // 4)
            for d in range(2):
                pool.wait_ge(added, d)
                nc.gpsimd.tensor_tensor(hs, hs, act_out[:, s, d, :], ALU.add).then_inc(added, 1)

        @block.vector
        def _(e):
            V = nc.vector

            def to_stage(g, j):
                e.wait_ge(turned_t, g - 1)
                at = bass.ds(g % B * TT, TT) if not isinstance(g, int) else slice(g * TT, (g + 1) * TT)
                V.tensor_tensor(stage[:, j], cen[:, at, :], bcast(rstd[:, at].unsqueeze(2), [P, TT, D]),
                                ALU.mult).then_inc(staged, 1)

            e.sem_inc(u_used, 4)
            for g in range(2):
                V.tensor_tensor(stage[:, g], cen[:, g * TT:(g + 1) * TT, :],
                                bcast(rstd[:, g * TT:(g + 1) * TT].unsqueeze(2), [P, TT, D]), ALU.mult).then_inc(staged, 1)
            with e.Fori(0, B // 2) as i:
                for j in range(2):
                    g = 2 * i + j
                    e.wait_ge(sums, g + 1)
                    for d in range(2):
                        for half, table in enumerate(("cos", "sin")):
                            e.wait_ge(u_ready, 4 * g + 2 * d + half + 1)
                            V.tensor_tensor(part[:, d, half, :], bank[1 + 2 * d + half][:], along(table, d),
                                            ALU.mult).then_inc(u_used, 1)
                    e.wait_ge(u_used, 4 * g + 8)
                    V.tensor_tensor(turned[:, 0, :], part[:, 0, 0, :], part[:, 0, 1, :], ALU.add).then_inc(parts, 1)
                    to_stage(g + 2, j)
                    e.wait_ge(backed, 4 * g)
                    e.wait_ge(parts, g + 1)
                    V.tensor_tensor_scan(state[:, j, 0, :], ssm["decay"][:, 0, :], turned[:, 0, :], 0.0,
                                         ALU.mult, ALU.add).then_inc(scanned, 1)
                    e.wait_ge(sums, g + 2)
                    V.tensor_tensor_scan(state[:, j, 1, ::-1], ssm["decay"][:, 1, :], turned[:, 1, ::-1], 0.0,
                                         ALU.mult, ALU.add).then_inc(scanned, 1)
            e.wait_ge(y_used, B + 2)
            hs = h[:, NT // 4:, :].rearrange("p (b t) d -> p b (t d)", b=3 * B // 4)
            V.tensor_tensor(hs, hs, act_out[:, B // 4:, 0, :], ALU.add).then_inc(scanned, 1)
            e.wait_ge(scanned, 2 * B + 1)
            V.tensor_tensor(hs, hs, act_out[:, B // 4:, 1, :], ALU.add).then_inc(scanned, 1)


def product_key_layer(nc, io, k):
    with ExitStack() as c:
        def sb(name, shape, dt=F32):
            return c.enter_context(nc.sbuf_tensor(f"k_{name}", shape, dt))

        t = {
            "xt": sb("xt", [D, B * S]),
            "keyw": sb("keyw", [D, H, 2 * NK]),
            "wq": sb("wq", [D, H, D]),
            "wo": sb("wo", [D, H, D]),
        }
        merge_keys(nc, io, k, t)
        turn_tokens(nc, k, "kt", t["xt"])
        memory_turns(nc, io, k, t)


def merge_keys(nc, io, k, t):
    bank = k["bank"]
    with ExitStack() as c:
        def sb(name, shape, dt=F32):
            return c.enter_context(nc.sbuf_tensor(f"m_{name}", shape, dt))

        def sem(name):
            return c.enter_context(nc.semaphore(f"m_{name}"))

        wpk = sb("wpk", [DK, 2 * H, D])
        keys = sb("keys", [DK, 2 * H, NK])
        loaded, merged, copied = sem("loaded"), sem("merged"), sem("copied")
        block = c.enter_context(nc.Block())

        @block.sync
        def _(sp):
            for dst, src in ((wpk[:], io["wq_pk_t"]), (keys[:], io["pk_keys_t"]), (t["wq"][:], io["wq"]), (t["wo"][:], io["wo"])):
                sp.dma_start(dst, src).then_inc(loaded, 16)

        @block.tensor
        def _(pe):
            pe.wait_ge(loaded, 64)
            for i in range(2 * H):
                last = nc.tensor.matmul(bank[i // H][0:D, (i % H) * NK:(i % H + 1) * NK], wpk[:, i, :], keys[:, i, :],
                                        start=True, stop=True)
            last.then_inc(merged, 1)

        @block.vector
        def _(e):
            e.wait_ge(merged, 1)
            for half in range(2):
                nc.vector.tensor_copy(t["keyw"][:, :, half * NK:(half + 1) * NK],
                                      bank[half][0:D, :].rearrange("p (h n) -> p h n", h=H)).then_inc(copied, 1)


def turn_tokens(nc, k, tag, xt):
    bank, cen, rstd = k["bank"], k["cen"], k["rstd"]
    with ExitStack() as c:
        def sem(name):
            return c.enter_context(nc.semaphore(f"{tag}_{name}"))

        stage = c.enter_context(nc.sbuf_tensor(f"{tag}_stage", [P, 2, TT, D], F32))
        staged, turned, copied, held = sem("staged"), sem("turned"), sem("copied"), sem("held")
        block = c.enter_context(nc.Block())

        @block.vector
        def _(e):
            e.sem_inc(turned, 2)
            with e.Fori(0, B // 2) as i:
                for j in range(2):
                    g = 2 * i + j
                    at = bass.ds(g * TT, TT)
                    e.wait_ge(turned, g + 1)
                    nc.vector.tensor_tensor(stage[:, j], cen[:, at, :], bcast(rstd[:, at].unsqueeze(2), [P, TT, D]),
                                            ALU.mult).then_inc(staged, 1)

        @block.tensor
        def _(pe):
            with pe.Fori(0, B // 2) as i:
                for j in range(2):
                    g = 2 * i + j
                    pe.wait_ge(copied, g + 1)
                    pe.wait_ge(staged, g + 1)
                    hold(pe, held)
                    for x in range(TT):
                        last = nc.tensor.transpose(bank[j][0:D, x * P:(x + 1) * P], stage[:, j, x, :], k["ident"][:])
                    last.then_inc(turned, 1)

        @block.scalar
        def _(act):
            act.sem_inc(copied, 2)
            with act.Fori(0, B // 2) as i:
                for j in range(2):
                    g = 2 * i + j
                    act.wait_ge(turned, g + 3)
                    nc.scalar.activation(xt[0:D, bass.ds(g * S, S)], bank[j][0:D, :], ACT.Copy).then_inc(copied, 1)


def candidates():
    runs, at, a = [], 0, 0
    while a < TOPK:
        n = TOPK // (a + 1)
        m = sum(1 for x in range(a, TOPK) if TOPK // (x + 1) == n)
        runs.append((a, m, n, at))
        at += m * n
        a += m
    return runs, at


def memory_turns(nc, io, k, t):
    bank, h, ident = k["bank"], k["h"], k["ident"]
    Z = bank[0:4]
    KV, SC, X, Y = bank[4:8]
    SC16 = SC[:].bitcast(F16)
    RUNS, NCAND = candidates()
    CANDS = len(RUNS) + 1
    CONSTS = 4
    N = H * B
    ATT = [dict(sim=6, peak=7, exp=8, turn=9, copy=10, out=11, add=12),
           dict(sim=9, peak=10, exp=11, turn=12, copy=13, out=14, add=15),
           dict(sim=12, peak=13, exp=14, turn=16, copy=17, out=18, add=19),
           dict(sim=16, peak=17, exp=18, turn=20, copy=21, out=22, add=23)]
    with ExitStack() as c:
        def sb(name, shape, dt=F32):
            return c.enter_context(nc.sbuf_tensor(f"k_{name}", shape, dt))

        def sem(name):
            return c.enter_context(nc.semaphore(f"k_{name}"))

        table = sb("table", [P, 2, JT, P])
        sel = sb("sel", [P, 2, JT // 4, P], F16)
        ident16 = sb("ident16", [P, P], F16)
        selz = sb("selz", [TT, TT, D])
        causal = sb("causal", [P, P])
        cmask = sb("cmask", [P, P], BF16)
        identb = sb("identb", [P, P], BF16)
        halves = sb("halves", [P, TT, 5, 2, NK // 2], F16)
        pieces = sb("pieces", [P, 2, 4, S], F16)
        ew = sb("ew", [P, 4, S])
        wt = sb("w", [P, 4, S])
        xs = sb("xs", [D, 2, S])
        wqs = sb("wqs", [D, 2, D])
        ss = sb("ss", [P, TT, 2, NK])
        rest = sb("rest", [P, TT, 2, NK])
        best = sb("best", [P, 2, TT, TOPK])
        under = sb("under", [P, 2, TT, TOPK])
        cand = sb("cand", [P, TT, NCAND])
        crest = sb("crest", [P, TT, NCAND])
        final = sb("final", [P, TT, TOPK])
        junk = sb("junk", [P, TT, TOPK])
        sm = sb("sm", [P, 2, TT])
        ab = sb("ab", [P, TT, 5, NK // 2])
        zsum = sb("zsum", [P, TT])
        zi = sb("zi", [P, 2, TT])
        kvs = sb("kvs", [P, S])
        zr = sb("zr", [TT, P])
        ks = sb("ks", [D, S])
        qs = sb("qs", [D, S])
        vp = sb("vp", [P, TT, D])
        pr = sb("pr", [P, 2, S])
        pt = sb("pt", [P, S])
        peak = sb("peak", [P, TT])
        rsum = sb("rsum", [P, TT])
        rinv = sb("rinv", [P, TT])
        S_ = {x: sem(x) for x in (
            "ready", "table0", "table1", "consts", "masks", "zeroed", "staged", "scores", "sscopy", "ranked", "cands", "offsets",
            "zsummed", "abready", "abturned", "hi", "lo", "pieces", "zready", "exp", "weight", "product", "kvcopy",
            "qready", "qcopy", "zrow", "zrcopy", "zbcast", "kready", "vproj", "vready", "sim", "peaked", "prob",
            "probt", "ptcopy", "attout", "added", "dve", "held", "peheld")}
        block = c.enter_context(nc.Block())
        s = S_

        @block.sync
        def _(sp):
            for dst, src in ((sel[:], io["pair_sel"]), (selz[:], io["tile_sel"]), (causal[:], io["causal"]),
                             (ident16[:], io["ident16"])):
                sp.dma_start(dst, src).then_inc(s["consts"], 16)

            def load(head, j):
                cols = bass.ds(head * JT * P, JT * P)
                sp.dma_start(table[:, j].rearrange("p t d -> p (t d)"), io["table"][:, cols]).then_inc(s[f"table{j}"], 16)

            for j in range(2):
                load(j, j)
            with sp.Fori(1, H // 2) as i:
                for j in range(2):
                    sp.wait_ge(s["product"], (2 * i + j - 1) * B * JT + 4)
                    load(2 * i + j, j)

        def turns(eng, body):
            with eng.Fori(0, H // 2) as i:
                for tb in range(2):
                    with eng.Fori(0, B // 2) as y:
                        for j in range(2):
                            body((2 * i + tb) * B + 2 * y + j, j, tb, 2 * y + j, 2 * i + tb, i)

        @block.gpsimd
        def _(pool):
            G = nc.gpsimd
            for x in (zi, kvs, qs):
                G.memset(x[:], 0.0).then_inc(s["zeroed"], 1)

            def stage(n, j):
                if isinstance(n, int):
                    at, hd = slice(0, S), slice(0, 1)
                else:
                    at, hd = bass.ds(n % B * S, S), bass.ds(n // B % H, 1)
                G.tensor_copy(xs[:, j, :], t["xt"][:, at]).then_inc(s["staged"], 1)
                G.tensor_copy(wqs[:, j:j + 1, :], t["wq"][:, hd, :]).then_inc(s["staged"], 1)

            def combine(n):
                pool.wait_ge(s["ranked"], 2 * TT * (n + 1))
                G.tensor_tensor(under[:], best[:], bcast(best[:, :, :, 0:1], [P, 2, TT, TOPK]), ALU.subtract).then_inc(s["cands"], 1)
                pool.wait_ge(s["cands"], CANDS * n + 1)
                for a, m, cnt, at in RUNS:
                    o = cand[:, :, at:at + m * cnt].rearrange("p t (m c) -> p t m c", m=m)
                    G.tensor_tensor(o, bcast(under[:, 0, :, a:a + m].unsqueeze(3), [P, TT, m, cnt]),
                                    bcast(under[:, 1, :, 0:cnt].unsqueeze(2), [P, TT, m, cnt]), ALU.add).then_inc(s["cands"], 1)

            stage(0, 0)
            combine(0)

            def body(n, j, tb, b, hd, i):
                pool.wait_ge(s["qready"], n + 1)
                stage(n + 1, 1 - j)
                combine(n + 1)
            turns(pool, body)

        @block.tensor
        def _(pe):
            T = nc.tensor

            def scores(n, j):
                pe.wait_ge(s["staged"], 2 * n + 2)
                pe.wait_ge(s["pieces"], 2 * n)
                hd = 0 if isinstance(n, int) else bass.ds(n // B % H, 1)
                rhs = t["keyw"][:, 0:1, :] if isinstance(n, int) else t["keyw"][:, hd, :]
                for x in range(TT):
                    last = T.matmul(SC[:, x * P:(x + 1) * P], xs[:, j, x * P:(x + 1) * P], rhs, start=True, stop=True)
                last.then_inc(s["scores"], 1)

            def turn_pieces(n, r):
                if r == 0:
                    pe.wait_ge(s["lo"], n + 1)
                else:
                    pe.wait_ge(s["pieces"], 2 * n + 1)
                hold(pe, s["peheld"])
                for bb in range(2):
                    for x in range(TT):
                        at = bb * S + x * P
                        last = T.transpose(SC16[:, at:at + P], halves[:, x, 2 * r + bb:2 * r + bb + 2].rearrange("p b q k -> p (b q k)"), ident16[:])
                last.then_inc(s["abturned"], 1)

            def pair_scores(n, jp, j):
                g = n * JT + jp
                if jp % (JT // 2) == 0:
                    pe.wait_ge(s["pieces"], 2 * n + 2 * jp // JT + 1)
                pe.wait_ge(s["weight"], g + 1)
                T.matmul(Z[jp % 4][:], sel[:, jp // (JT // 4) % 2, jp % (JT // 4), :], pieces[:, j, jp // (JT // 4), :],
                         start=True, stop=True).then_inc(s["zready"], 1)

            def product(n, jp, tb, i):
                if jp == 0:
                    pe.wait_ge(s["kvcopy"], n + 1)
                    pe.wait_ge(s[f"table{tb}"], 16 * i + 16)
                pe.wait_ge(s["weight"], n * JT + jp + 5)
                last = T.matmul(KV[:], table[:, tb, jp, :], wt[:, jp % 4, :], start=(jp == 0), stop=(jp == JT - 1))
                last.then_inc(s["product"], 1)
                if jp == JT - 1:
                    return last

            def query(n, j):
                pe.wait_ge(s["prob"], 4 * n + 4)
                hold(pe, s["peheld"])
                T.matmul(X[0:D, :], wqs[:, j, :], xs[:, j, :], start=True, stop=True).then_inc(s["qready"], 1)

            def zinv_row(n, j):
                pe.wait_ge(s["added"], 4 * n + 1)
                hold(pe, s["peheld"])
                T.transpose(Y[0:TT, 0:P], zi[:, 1 - j, :], ident[:]).then_inc(s["zrow"], 1)

            def zinv_spread(n):
                pe.wait_ge(s["zrcopy"], n + 1)
                hold(pe, s["peheld"])
                for x in range(TT):
                    last = T.matmul(Y[0:D, x * P:(x + 1) * P], selz[:, x, :], zr[:], start=True, stop=True)
                last.then_inc(s["zbcast"], 1)

            def value_project(n):
                pe.wait_ge(s["kready"], n + 1)
                hold(pe, s["peheld"])
                hd = (n + (H * B - 1)) // B % H
                for x in range(TT):
                    last = T.matmul(Y[:, x * D:(x + 1) * D], kvs[0:D, x * P:(x + 1) * P], t["wo"][:, bass.ds(hd, 1), :],
                                    start=True, stop=True)
                last.then_inc(s["vproj"], 1)

            def value_project_last():
                pe.wait_ge(s["kready"], N + 1)
                for x in range(TT):
                    last = T.matmul(Y[:, x * D:(x + 1) * D], kvs[0:D, x * P:(x + 1) * P], t["wo"][:, H - 1, :],
                                    start=True, stop=True)
                last.then_inc(s["vproj"], 1)

            def sim(n, it):
                w = (it + 1) * P
                if it == 0:
                    pe.wait_ge(s["qcopy"], n + 1)
                else:
                    pe.wait_ge(s["prob"], 4 * n + it)
                if it:
                    T.matmul(X[:, 0:w - P], qs[:, it * P:w], ks[:, 0:w - P], start=True, stop=True)
                T.matmul(X[:, w - P:w], qs[:, it * P:w], ks[:, w - P:w], start=True, stop=False)
                T.matmul(X[:, w - P:w], identb[:], cmask[:], start=False, stop=True).then_inc(s["sim"], 1)

            def prob_turn(n, it):
                if it == 0:
                    pe.wait_ge(s["vready"], n + 1)
                else:
                    pe.wait_ge(s["added"], 4 * n + it + 1)
                pe.wait_ge(s["prob"], 4 * n + it + 1)
                for x in range(it + 1):
                    last = T.transpose(Y[:, x * P:(x + 1) * P], pr[:, it % 2, x * P:(x + 1) * P], ident[:])
                last.then_inc(s["probt"], 1)

            def att_out(n, it):
                pe.wait_ge(s["ptcopy"], 4 * n + it + 1)
                for x in range(it + 1):
                    last = T.matmul(Y[:, 0:D], pt[:, x * P:(x + 1) * P], vp[:, x, :], start=(x == 0), stop=(x == it))
                last.then_inc(s["attout"], 1)

            for x in ("qready", "probt", "attout"):
                pe.sem_inc(s[x], 1)
            pe.wait_ge(s["consts"], CONSTS * 16)
            pe.wait_ge(s["zeroed"], 3)
            pe.wait_ge(s["masks"], 2)
            scores(0, 0)
            turn_pieces(0, 0)
            turn_pieces(0, 1)
            for jp in range(3):
                pair_scores(0, jp, 0)

            def body(n, j, tb, b, hd, i):
                for jp in range(JT):
                    if jp == 0:
                        scores(n + 1, 1 - j)
                    if jp == 1:
                        zinv_row(n, j)
                    if jp == 3:
                        zinv_spread(n)
                    if jp == 5:
                        value_project(n)
                    for it, at in enumerate(ATT):
                        if jp == at["out"]:
                            att_out(n, it)
                        if jp == at["turn"]:
                            prob_turn(n, it)
                    for it, at in enumerate(ATT):
                        if jp == at["sim"]:
                            sim(n, it)
                    if jp in (24, 26):
                        turn_pieces(n + 1, (jp - 24) // 2)
                    if jp == 27:
                        query(n, j)
                    if jp + 3 < JT:
                        pair_scores(n, jp + 3, j)
                    else:
                        pair_scores(n + 1, jp + 3 - JT, 1 - j)
                    last = product(n, jp, tb, i)
            turns(pe, body)
            zinv_row(N, 0)
            zinv_spread(N)
            value_project_last()
            for it in range(TT):
                sim(N, it)
                prob_turn(N, it)
                att_out(N, it)

        @block.scalar
        def _(act):
            A = nc.scalar

            def copy_scores(n):
                act.wait_ge(s["scores"], n + 1)
                act.wait_ge(s["abready"], n)
                A.activation(ss[:].rearrange("p t a k -> p (t a k)"), SC[:], ACT.Copy).then_inc(s["sscopy"], 1)

            def sums(n):
                act.wait_ge(s["offsets"], n + 1)
                for x in range(TT):
                    last = A.activation(junk[:, x, :], final[:, x, :], ACT.Exp, bias=sm[:, 1, x:x + 1],
                                        accum_out=zsum[:, x:x + 1])
                    last.then_inc(s["zsummed"], 1)

            def high(n):
                act.wait_ge(s["abready"], n + 1)
                act.wait_ge(s["abturned"], 2 * n)
                A.activation(halves[:].rearrange("p t b q k -> p (t b) q k")[:, :, 0, :],
                             ab[:].rearrange("p t b k -> p (t b) k"), ACT.Copy).then_inc(s["hi"], 1)

            def copy_pieces(n, j, r):
                act.wait_ge(s["abturned"], 2 * n + r + 1)
                A.activation(pieces[:, j, 2 * r:2 * r + 2, :].rearrange("p b t -> p (b t)"), SC16, ACT.Copy).then_inc(s["pieces"], 1)

            def exps(n, jp):
                g = n * JT + jp
                act.wait_ge(s["zready"], g + 1)
                act.wait_ge(s["weight"], g + 1)
                A.activation(ew[:, jp % 4, :], Z[jp % 4][:], ACT.Exp).then_inc(s["exp"], 1)

            def att_exp(n, it):
                w = (it + 1) * P
                act.wait_ge(s["peaked"], 4 * n + it + 1)
                act.wait_ge(s["probt"], 4 * n + max(it - 1, 0) + 1)
                A.activation(pr[:, it % 2, 0:w], X[:, 0:w], ACT.Exp, bias=peak[:, it:it + 1],
                             accum_out=rsum[:, it:it + 1]).then_inc(s["prob"], 1)

            def att_copy(n, it):
                w = (it + 1) * P
                act.wait_ge(s["probt"], 4 * n + it + 2)
                act.wait_ge(s["attout"], 4 * n + it + 1)
                A.activation(pt[:, 0:w], Y[:, 0:w], ACT.Copy).then_inc(s["ptcopy"], 1)

            for x in ("kvcopy", "qcopy"):
                act.sem_inc(s[x], 1)
            act.wait_ge(s["ready"], 1)
            act.wait_ge(s["zeroed"], 3)
            copy_scores(0)
            sums(0)
            high(0)
            copy_pieces(0, 0, 0)
            copy_pieces(0, 0, 1)
            exps(0, 0)
            exps(0, 1)

            def zr_copy(n):
                act.wait_ge(s["zrow"], n + 1)
                A.activation(zr[:], Y[0:TT, 0:P], ACT.Copy).then_inc(s["zrcopy"], 1)

            def body(n, j, tb, b, hd, i):
                for jp in range(JT):
                    if jp == 1:
                        copy_scores(n + 1)
                    if jp == 2:
                        zr_copy(n)
                    for it, at in enumerate(ATT):
                        if jp == at["exp"]:
                            att_exp(n, it)
                        if jp == at["copy"]:
                            att_copy(n, it)
                    if jp == 22:
                        sums(n + 1)
                    if jp == 23:
                        high(n + 1)
                    if jp in (25, 27):
                        copy_pieces(n + 1, 1 - j, (jp - 25) // 2)
                    if jp == 29:
                        act.wait_ge(s["qready"], n + 2)
                        A.activation(qs[:], X[0:D, :], ACT.Copy, scale=D ** -0.5).then_inc(s["qcopy"], 1)
                    if jp + 2 < JT:
                        exps(n, jp + 2)
                    else:
                        exps(n + 1, jp + 2 - JT)
                act.wait_ge(s["product"], (n + 1) * JT + 4)
                act.wait_ge(s["vproj"], n + 1)
                A.activation(kvs[:], KV[:], ACT.Copy).then_inc(s["kvcopy"], 1)
            turns(act, body)
            zr_copy(N)
            for it in range(TT):
                att_exp(N, it)
                att_copy(N, it)

        @block.vector
        def _(e):
            V = nc.vector
            ch = Chain(e, s["dve"])

            def rank(n, x):
                if x == 0:
                    e.wait_ge(s["sscopy"], n + 1)
                    e.wait_ge(s["cands"], CANDS * n)
                    hold(e, s["held"])
                for a in range(2):
                    ch.add(V.max(best[:, a, x, 0:8], ss[:, x, a, :]))
                ch.wait()
                hold(e, s["held"])
                for a in range(2):
                    ch.add(V.match_replace(rest[:, x, a, :], best[:, a, x, 0:8], ss[:, x, a, :], -3e38))
                ch.wait()
                hold(e, s["held"])
                for a in range(2):
                    V.max(best[:, a, x, 8:16], rest[:, x, a, :]).then_inc(s["ranked"], 1)

            def select(n, xs_):
                if xs_[0] == 0:
                    e.wait_ge(s["cands"], CANDS * (n + 1))
                    e.wait_ge(s["zsummed"], 4 * n)
                    hold(e, s["held"])
                for x in xs_:
                    ch.add(V.max(final[:, x, 0:8], cand[:, x, :]))
                ch.wait()
                hold(e, s["held"])
                for x in xs_:
                    ch.add(V.match_replace(crest[:, x, :], final[:, x, 0:8], cand[:, x, :], -3e38))
                ch.wait()
                hold(e, s["held"])
                for x in xs_:
                    ch.add(V.max(final[:, x, 8:16], crest[:, x, :]))
                ch.wait()

            def offsets(n):
                ch.link(V.tensor_scalar(sm[:, 0, :], final[:, :, TOPK - 1], -(1.0 + 2.0 ** -20), 2.0 ** -16, ALU.mult, ALU.add))
                V.tensor_scalar(sm[:, 1, :], sm[:, 0, :], CAP, -SHIFT, ALU.min, ALU.add).then_inc(s["offsets"], 1)

            def parts(n):
                e.wait_ge(s["hi"], n)
                k2 = NK // 2
                for a, out, src in ((0, ab[:, :, 0:3:2, :], ss[:, :, 0, :]), (0, ab[:, :, 4:5, :], ss[:, :, 0, 0:k2]),
                                    (1, ab[:, :, 1:4:2, :], ss[:, :, 1, :])):
                    m = out.shape[2]
                    ch.add(V.tensor_tensor(out, src.rearrange("p t (b k) -> p t b k", b=m),
                                           bcast(best[:, a, :, 0:1].unsqueeze(3), [P, TT, m, k2]), ALU.subtract))
                ch.wait()
                e.wait_ge(s["offsets"], n + 1)
                ch.link(V.tensor_tensor(ab[:, :, 1:4:2, :], ab[:, :, 1:4:2, :],
                                        bcast(sm[:, 1, :].unsqueeze(2).unsqueeze(3), [P, TT, 2, k2]), ALU.add))
                V.tensor_scalar(ab[:], ab[:], -30000.0, None, ALU.max).then_inc(s["abready"], 1)

            def zinv(n, j):
                e.wait_ge(s["zsummed"], 4 * n + 4)
                ch.add(V.reciprocal(zi[:, j, :], zsum[:]))

            def low(n):
                e.wait_ge(s["hi"], n + 1)
                v = halves[:].rearrange("p t b q k -> p (t b) q k")
                V.tensor_tensor(v[:, :, 1, :], ab[:].rearrange("p t b k -> p (t b) k"), v[:, :, 0, :],
                                ALU.subtract).then_inc(s["lo"], 1)

            def weights(n, jp):
                g = n * JT + jp
                e.wait_ge(s["exp"], g + 1)
                e.wait_ge(s["product"], g + 1)
                V.scalar_tensor_tensor(wt[:, jp % 4, :], Z[jp % 4][:], -SHIFT, ew[:, jp % 4, :], ALU.is_ge,
                                       ALU.mult).then_inc(s["weight"], 1)

            def scale_keys(n):
                e.wait_ge(s["kvcopy"], n + 1)
                e.wait_ge(s["zbcast"], n + 1)
                V.tensor_tensor(ks[:], Y[0:D, :], kvs[D:P, :], ALU.mult).then_inc(s["kready"], 1)

            def scale_values(n, j):
                e.wait_ge(s["vproj"], n + 1)
                V.tensor_tensor(vp[:], Y[:, 0:TT * D].rearrange("p (t d) -> p t d", t=TT),
                                bcast(zi[:, 1 - j, :].unsqueeze(2), [P, TT, D]), ALU.mult).then_inc(s["vready"], 1)

            def att_peak(n, it):
                w = (it + 1) * P
                e.wait_ge(s["sim"], 4 * n + it + 1)
                V.tensor_reduce(peak[:, it:it + 1], X[:, 0:w], AX.X, ALU.max, negate=True).then_inc(s["peaked"], 1)

            def att_add(n, it):
                e.wait_ge(s["prob"], 4 * n + it + 1)
                ch.add(V.reciprocal(rinv[:, it:it + 1], rsum[:, it:it + 1]))
                e.wait_ge(s["attout"], 4 * n + it + 2)
                ch.wait()
                if isinstance(n, int):
                    at = h[:, (B - 1) * TT + it, :]
                    V.scalar_tensor_tensor(at, Y[:, 0:D], rinv[:, it:it + 1], at, ALU.mult, ALU.add).then_inc(s["added"], 1)
                else:
                    at = h[:, bass.ds((n + (B - 1)) % B * TT + it, 1), :]
                    V.scalar_tensor_tensor(at, Y[:, 0:D].unsqueeze(1), rinv[:, it:it + 1], at, ALU.mult,
                                           ALU.add).then_inc(s["added"], 1)

            e.sem_inc(s["weight"], 4)
            e.sem_inc(s["product"], 4)
            e.sem_inc(s["added"], 1)
            e.sem_inc(s["ready"], 1)
            e.wait_ge(s["zeroed"], 3)
            e.wait_ge(s["consts"], CONSTS * 16)
            V.tensor_copy(cmask[:], causal[:]).then_inc(s["masks"], 1)
            V.tensor_copy(identb[:], ident[:]).then_inc(s["masks"], 1)

            def first_half(n):
                for x in range(TT):
                    rank(n, x)

            first_half(0)
            select(0, (0, 1))
            select(0, (2, 3))
            offsets(0)
            parts(0)
            zinv(0, 0)
            low(0)
            e.wait_ge(s["exp"], 1)
            V.scalar_tensor_tensor(wt[:, 0, :], Z[0][:], -SHIFT, ew[:, 0, :], ALU.is_ge, ALU.mult).then_inc(s["weight"], 1)
            start = ch.n
            per_turn = 38

            def body(n, j, tb, b, hd, i):
                ch.base, ch.n = n * per_turn + start, 0
                for jp in range(JT):
                    if jp in (3, 5, 8, 9):
                        rank(n + 1, (3, 5, 8, 9).index(jp))
                    if jp == 4:
                        scale_keys(n)
                    if jp == 6:
                        scale_values(n, j)
                    for it, at in enumerate(ATT):
                        if jp == at["peak"]:
                            att_peak(n, it)
                        if jp == at["add"]:
                            att_add(n, it)
                    if jp == 14:
                        select(n + 1, (0, 1))
                    if jp == 16:
                        select(n + 1, (2, 3))
                    if jp == 18:
                        offsets(n + 1)
                    if jp == 20:
                        parts(n + 1)
                    if jp == 25:
                        zinv(n + 1, 1 - j)
                    if jp == 23:
                        low(n + 1)
                    if jp + 1 < JT:
                        weights(n, jp + 1)
                    else:
                        weights(n + 1, 0)
                assert ch.n == per_turn
            turns(e, body)
            ch.base, ch.n = N * per_turn + start, 0
            scale_keys(N)
            scale_values(N, 0)
            for it in range(TT):
                att_peak(N, it)
                att_add(N, it)


def window_attention(nc, io, k):
    bank, h, cen, rstd, ident = k["bank"], k["h"], k["cen"], k["rstd"], k["ident"]
    XT, QK, VAL, S0, S1, PT, OUT, TAIL = bank
    NW = S // W
    with ExitStack() as c:
        def sb(name, shape, dt=F32):
            return c.enter_context(nc.sbuf_tensor(f"w_{name}", shape, dt))

        def sem(name):
            return c.enter_context(nc.semaphore(f"w_{name}"))

        wqk = sb("wqk", [D + 1, P])
        wv = sb("wv", [D + 1, D])
        wp = sb("wp", [D + 1, D])
        hmask = sb("hmask", [D, H])
        vmask = sb("vmask", [P, 2])
        stage = sb("stage", [P, TT, D])
        xs = sb("xs", [D + 1, NW, 2, W])
        q = sb("q", [D, S])
        kk = sb("kk", [D, S])
        kblk = sb("kblk", [D, NW, H, W])
        vblk = sb("vblk", [P, 2, NW * H // 2, 2, HD + 1])
        mx = sb("mx", [P, 2, H])
        low = sb("low", [P, 2, H, W])
        ex = sb("ex", [P, 2, H * W])
        pt = sb("pt", [P, S])
        rs = sb("rs", [P, TT, H])
        o = sb("o", [P, TT, D])
        ot = sb("ot", [D + 1, S])
        loaded, ones, staged, turned, xs_ready, qk_ready, q_ready, k_ready, kblk_ready, v_ready, vblk_ready, scored, \
            lowered, exped, pturned, pt_ready, o_ready, o_scaled, oturned, ot_ready, projected, added, dve, held = (
                sem(x) for x in ("loaded", "ones", "staged", "turned", "xs", "qk", "q", "k", "kblk", "v", "vblk", "scored",
                                 "lowered", "exped", "pturned", "pt", "o", "oscaled", "oturned", "ot", "proj", "added",
                                 "dve", "held"))
        block = c.enter_context(nc.Block())

        @block.sync
        def _(sp):
            for dst, src in ((wqk, "w_qk"), (wv, "w_v"), (wp, "w_p"), (hmask, "head_rows"), (vmask, "half_rows")):
                sp.dma_start(dst[:], io[src]).then_inc(loaded, 16)

        @block.tensor
        def _(pe):
            T = nc.tensor

            def turn_in(g):
                pe.wait_ge(staged, g + 1)
                pe.wait_ge(xs_ready, g)
                hold(pe, held)
                for x in range(TT):
                    last = T.transpose(XT[0:D, x * P:(x + 1) * P], stage[:, x, :], ident[:])
                last.then_inc(turned, 1)

            def queries_keys(g):
                pe.wait_ge(xs_ready, g + 1)
                pe.wait_ge(k_ready, g)
                hold(pe, held)
                T.matmul(QK[:], wqk[:], xs[:, :, 0, :], start=True, stop=True).then_inc(qk_ready, 1)

            def values(g):
                pe.wait_ge(vblk_ready, g)
                hold(pe, held)
                for w in range(NW):
                    last = T.matmul(VAL[:, w * D:(w + 1) * D], xs[:, w].rearrange("p a t -> p (a t)"), wv[:],
                                    start=True, stop=True)
                last.then_inc(v_ready, 1)

            def scores(g, x):
                if x == 0:
                    pe.wait_ge(q_ready, g + 1)
                if x % 2 == 0:
                    pe.wait_ge(kblk_ready, 2 * g + x // 2 + 1)
                pe.wait_ge(lowered, 4 * g + x + 1)
                hold(pe, held)
                for w2 in range(2):
                    w = 2 * x + w2
                    last = T.matmul((S0, S1)[x % 2][w2 * W:(w2 + 1) * W, :], q[:, w * W:(w + 1) * W],
                                    kblk[:, w].rearrange("p h t -> p (h t)"), start=True, stop=True)
                last.then_inc(scored, 1)

            def turn_probs(g, x):
                pe.wait_ge(exped, 4 * g + x + 3)
                pe.wait_ge(pt_ready, 4 * g + x + 1)
                for pair in range(H // 2):
                    s = slice(pair * P, (pair + 1) * P)
                    last = T.transpose(PT[:, s], ex[:, x % 2, s], ident[:])
                last.then_inc(pturned, 1)

            def weigh(g, j, x):
                if x == 0:
                    pe.wait_ge(vblk_ready, g + 1)
                    pe.wait_ge(o_scaled, g + 1)
                pe.wait_ge(pt_ready, 4 * g + x + 2)
                hold(pe, held)
                n = 2 * (HD + 1)
                for pair in range(H // 2):
                    for w2 in range(2):
                        at = x * 4 * n + pair * n
                        last = T.matmul(OUT[w2 * W:(w2 + 1) * W, at:at + n], pt[:, pair * P + w2 * W:pair * P + (w2 + 1) * W],
                                        vblk[:, j, (2 * x + w2) * (H // 2) + pair].rearrange("p a d -> p (a d)"),
                                        start=True, stop=True)
                if x == TT - 1:
                    last.then_inc(o_ready, 1)

            def turn_out(g):
                pe.wait_ge(o_scaled, g + 2)
                pe.wait_ge(added, g + 1)
                hold(pe, held)
                for x in range(TT):
                    last = T.transpose(TAIL[0:D, x * P:(x + 1) * P], o[:, x, :], ident[:])
                last.then_inc(oturned, 1)

            def project(g):
                pe.wait_ge(ot_ready, g + 1)
                hold(pe, held)
                for x in range(TT):
                    last = T.matmul(TAIL[:, x * D:(x + 1) * D], ot[:, x * P:(x + 1) * P], wp[:], start=True, stop=True)
                last.then_inc(projected, 1)

            pe.wait_ge(loaded, 80)
            pe.wait_ge(ones, 2)
            turn_in(0)
            queries_keys(0)
            values(0)
            scores(0, 0)
            scores(0, 1)
            with pe.Fori(0, B // 2) as i:
                for j in range(2):
                    g = 2 * i + j
                    turn_probs(g, 0)
                    scores(g, 2)
                    turn_in(g + 1)
                    weigh(g, j, 0)
                    turn_probs(g, 1)
                    scores(g, 3)
                    queries_keys(g + 1)
                    weigh(g, j, 1)
                    turn_probs(g, 2)
                    values(g + 1)
                    weigh(g, j, 2)
                    turn_probs(g, 3)
                    weigh(g, j, 3)
                    scores(g + 1, 0)
                    scores(g + 1, 1)
                    turn_out(g)
                    project(g)

        @block.scalar
        def _(act):
            A = nc.scalar

            def copy_in(g):
                act.wait_ge(turned, g + 1)
                A.activation(xs[0:D], bcast(XT[0:D, :].rearrange("p (w t) -> p w t", w=NW).unsqueeze(2), [D, NW, 2, W]),
                             ACT.Copy).then_inc(xs_ready, 1)

            def copy_qk(g):
                act.wait_ge(qk_ready, g + 1)
                A.activation(kk[:], QK[D:P, :], ACT.Copy).then_inc(k_ready, 1)
                A.activation(q[:], QK[0:D, :], ACT.Copy, scale=HD ** -0.5).then_inc(q_ready, 1)

            def exp(g, x):
                act.wait_ge(lowered, 4 * g + x + 3)
                A.activation(ex[:, x % 2, :], low[:, x % 2].rearrange("p h t -> p (h t)"), ACT.Exp).then_inc(exped, 1)

            def copy_probs(g, x):
                act.wait_ge(pturned, 4 * g + x + 1)
                A.activation(pt[:], PT[:], ACT.Copy).then_inc(pt_ready, 1)

            act.sem_inc(pt_ready, 1)
            copy_in(0)
            copy_qk(0)
            with act.Fori(0, B // 2) as i:
                for j in range(2):
                    g = 2 * i + j
                    exp(g, 0)
                    exp(g, 1)
                    copy_probs(g, 0)
                    exp(g, 2)
                    copy_in(g + 1)
                    copy_probs(g, 1)
                    exp(g, 3)
                    copy_qk(g + 1)
                    copy_probs(g, 2)
                    copy_probs(g, 3)
                    act.wait_ge(oturned, g + 1)
                    A.activation(ot[0:D, :], TAIL[0:D, :], ACT.Copy).then_inc(ot_ready, 1)

        @block.gpsimd
        def _(pool):
            G = nc.gpsimd

            def key_blocks(g):
                pool.wait_ge(k_ready, g + 1)
                half = NW // 2
                for s in (slice(0, half), slice(half, NW)):
                    G.tensor_tensor(kblk[:, s], bcast(kk[:].rearrange("p (w t) -> p w t", w=NW)[:, s].unsqueeze(2), [D, half, H, W]),
                                    bcast(hmask[:].unsqueeze(1).unsqueeze(3), [D, half, H, W]), ALU.mult).then_inc(kblk_ready, 1)

            G.memset(xs[D:D + 1], 1.0).then_inc(ones, 1)
            G.memset(ot[D:D + 1, :], 1.0).then_inc(ones, 1)
            pool.wait_ge(loaded, 80)
            key_blocks(0)
            with pool.Fori(0, B // 2) as i:
                for j in range(2):
                    key_blocks(2 * i + j + 1)

        @block.vector
        def _(e):
            V = nc.vector
            ch = Chain(e, dve)

            def to_stage(g):
                at = slice(g * TT, (g + 1) * TT) if isinstance(g, int) else bass.ds(g % B * TT, TT)
                e.wait_ge(turned, g)
                V.tensor_tensor(stage[:], cen[:, at, :], bcast(rstd[:, at].unsqueeze(2), [P, TT, D]), ALU.mult).then_inc(staged, 1)

            def lower(g, x):
                s = (S0, S1)[x % 2][:].rearrange("p (h t) -> p h t", h=H)
                e.wait_ge(scored, 4 * g + x + 1)
                ch.link(V.tensor_reduce(mx[:, x % 2, :], s, AX.X, ALU.max))
                e.wait_ge(exped, 4 * g + x + 1)
                V.tensor_tensor(low[:, x % 2], s, bcast(mx[:, x % 2, :].unsqueeze(2), [P, H, W]), ALU.subtract).then_inc(lowered, 1)

            def value_blocks(g, j):
                e.wait_ge(v_ready, g + 1)
                V.tensor_tensor(vblk[:, j, :, :, 0:HD], VAL[:].rearrange("p (n a d) -> p n a d", a=2, d=HD),
                                bcast(vmask[:].unsqueeze(1).unsqueeze(3), [P, NW * H // 2, 2, HD]), ALU.mult).then_inc(vblk_ready, 1)

            def scale(g):
                out = OUT[:, 0:TT * H * (HD + 1)].rearrange("p (x h d) -> p x h d", x=TT, h=H)
                e.wait_ge(o_ready, g + 1)
                ch.link(V.reciprocal(rs[:], out[:, :, :, HD]))
                V.tensor_tensor(o[:].rearrange("p x (h d) -> p x h d", h=H), out[:, :, :, 0:HD],
                                bcast(rs[:].unsqueeze(3), [P, TT, H, HD]), ALU.mult).then_inc(o_scaled, 1)

            def add(g):
                at = bass.ds(g * TT, TT)
                e.wait_ge(projected, g + 1)
                V.tensor_tensor(h[:, at, :], h[:, at, :], TAIL[:, 0:TT * D].rearrange("p (x d) -> p x d", x=TT),
                                ALU.add).then_inc(added, 1)

            e.sem_inc(lowered, 2)
            e.sem_inc(exped, 2)
            e.sem_inc(o_scaled, 1)
            e.sem_inc(added, 1)
            to_stage(0)
            e.wait_ge(loaded, 80)
            for j in range(2):
                ch.add(V.tensor_copy(vblk[:, j, :, :, HD], bcast(vmask[:].unsqueeze(1), [P, NW * H // 2, 2])))
            ch.wait()
            to_stage(1)
            value_blocks(0, 0)
            lower(0, 0)
            lower(0, 1)
            start = ch.n
            per_group = 5
            with e.Fori(0, B // 2) as i:
                for j in range(2):
                    g = 2 * i + j
                    ch.base, ch.n = g * per_group + start, 0
                    lower(g, 2)
                    lower(g, 3)
                    value_blocks(g + 1, 1 - j)
                    scale(g)
                    lower(g + 1, 0)
                    lower(g + 1, 1)
                    add(g)
                    to_stage(g + 2)
                    assert ch.n == per_group


def experts(nc, io, k):
    bank, h, cen, rstd, ident = k["bank"], k["h"], k["cen"], k["rstd"], k["ident"]
    XT, LG = bank[0:2]
    HID, OUT = bank[2:4], bank[4:6]
    E, PAIRS = EXPERTS, EXPERTS // 2
    with ExitStack() as c:
        def sb(name, shape, dt=F32):
            return c.enter_context(nc.sbuf_tensor(f"e_{name}", shape, dt))

        def sem(name):
            return c.enter_context(nc.semaphore(f"e_{name}"))

        router = sb("router", [D, E])
        w1 = sb("w1", [D + 1, E * D])
        w2 = sb("w2", [P, PAIRS, 2, D])
        w2in = sb("w2in", [P, PAIRS, D])
        pmask = sb("pmask", [P, 2])
        b2 = sb("b2", [1, E * D])
        one = sb("one", [1, P])
        stage = sb("stage", [P, TT, D])
        xs = sb("xs", [D + 1, S])
        hid = sb("hid", [P, 2, PAIRS, S])
        mx = sb("mx", [P, TT])
        low = sb("low", [P, TT, E])
        ex = sb("ex", [P, TT, E])
        zs = sb("zs", [P, 2, TT])
        prob = sb("prob", [P, TT, E])
        top = sb("top", [P, TT, 8])
        rest = sb("rest", [P, TT, E])
        den = sb("den", [P, 2, TT])
        comb = sb("comb", [P, 2, TT, E])
        weighed = sb("weighed", [P, 2, E, D])
        total = sb("total", [P, 2, TT, D])
        loaded, ones, w2_ready, staged, turned, xs_ready, routed, lowered, exped, hid_ready, gelued, out_ready, out_used, \
            summed, skipped, added, dve, held, vheld, pheld = (
                sem(x) for x in ("loaded", "ones", "w2", "staged", "turned", "xs", "routed", "lowered", "exped", "hid",
                                 "gelued", "out", "outused", "summed", "skipped", "added", "dve", "held", "vheld", "pheld"))
        block = c.enter_context(nc.Block())

        @block.sync
        def _(sp):
            for dst, src in ((router, "router_t"), (w1, "w1"), (w2in, "w2"), (pmask, "half_rows"), (b2, "b2")):
                sp.dma_start(dst[:], io[src]).then_inc(loaded, 16)

        @block.tensor
        def _(pe):
            T = nc.tensor

            def turn_in(g):
                pe.wait_ge(staged, g + 1)
                pe.wait_ge(xs_ready, g)
                hold(pe, held)
                for x in range(TT):
                    last = T.transpose(XT[0:D, x * P:(x + 1) * P], stage[:, x, :], ident[:])
                last.then_inc(turned, 1)

            def route(g):
                pe.wait_ge(xs_ready, g + 1)
                pe.wait_ge(lowered, g)
                hold(pe, held)
                for x in range(TT):
                    last = T.matmul(LG[:, x * E:(x + 1) * E], xs[0:D, x * P:(x + 1) * P], router[:], start=True, stop=True)
                last.then_inc(routed, 1)

            def hidden(g, p):
                pe.wait_ge(gelued, PAIRS * g + p + 1)
                hold(pe, held)
                T.matmul(HID[p % 2][:], w1[:, p * P:(p + 1) * P], xs[:], start=True, stop=True).then_inc(hid_ready, 1)

            def output(g, j, x):
                if x == 0:
                    pe.wait_ge(gelued, PAIRS * (g + 1) + 2)
                pe.wait_ge(out_used, TT * g + x + 1)
                hold(pe, held)
                for p in range(PAIRS):
                    s = slice(p * P, (p + 1) * P)
                    T.matmul(OUT[x % 2][:, s], one[:], b2[:, s], start=True, stop=False)
                    last = T.matmul(OUT[x % 2][:, s], hid[:, j, p, x * P:(x + 1) * P],
                                    w2[:, p].rearrange("p a d -> p (a d)"), start=False, stop=True)
                last.then_inc(out_ready, 1)

            pe.wait_ge(loaded, 80)
            pe.wait_ge(ones, 2)
            pe.wait_ge(w2_ready, 1)
            turn_in(0)
            route(0)
            for p in range(PAIRS):
                hidden(0, p)
            with pe.Fori(0, B // 2) as i:
                for j in range(2):
                    g = 2 * i + j
                    turn_in(g + 1)
                    output(g, j, 0)
                    route(g + 1)
                    output(g, j, 1)
                    hidden(g + 1, 0)
                    hidden(g + 1, 1)
                    output(g, j, 2)
                    hidden(g + 1, 2)
                    output(g, j, 3)
                    hidden(g + 1, 3)

        @block.scalar
        def _(act):
            A = nc.scalar

            def front(g, j):
                act.wait_ge(turned, g + 1)
                A.activation(xs[0:D, :], XT[0:D, :], ACT.Copy).then_inc(xs_ready, 1)
                act.wait_ge(lowered, g + 1)
                A.activation(ex[:], low[:], ACT.Exp).then_inc(exped, 1)
                for p in range(PAIRS):
                    act.wait_ge(hid_ready, PAIRS * g + p + 1)
                    A.activation(hid[:, j, p, :], HID[p % 2][:], ACT.Gelu).then_inc(gelued, 1)

            act.sem_inc(gelued, 2)
            front(0, 0)
            with act.Fori(0, B // 2) as i:
                for j in range(2):
                    front(2 * i + j + 1, 1 - j)

        @block.gpsimd
        def _(pool):
            G = nc.gpsimd

            def skip(g):
                at = slice(g * TT, (g + 1) * TT) if isinstance(g, int) else bass.ds(g * TT, TT)
                pool.wait_ge(staged, g + 1)
                pool.wait_ge(added, g + 2)
                hold(pool, pheld)
                G.tensor_tensor(h[:, at, :], h[:, at, :], stage[:], ALU.add).then_inc(skipped, 1)

            G.memset(xs[D:D + 1, :], 1.0).then_inc(ones, 1)
            G.memset(one[:], 1.0).then_inc(ones, 1)
            pool.wait_ge(ones, 2)
            with pool.Fori(0, B // 2) as i:
                for j in range(2):
                    g = 2 * i + j
                    skip(g)
                    pool.wait_ge(summed, TT * (g + 1) + 2)
                    pool.wait_ge(skipped, g + 1)
                    hold(pool, pheld)
                    at = bass.ds(g * TT, TT)
                    G.tensor_tensor(h[:, at, :], h[:, at, :], total[:, j], ALU.add).then_inc(added, 1)
            pool.sem_inc(skipped, 1)

        @block.vector
        def _(e):
            V = nc.vector
            ch = Chain(e, dve)

            def to_stage(g):
                at = slice(g * TT, (g + 1) * TT) if isinstance(g, int) else bass.ds(g % B * TT, TT)
                e.wait_ge(turned, g)
                if not isinstance(g, int) or g:
                    e.wait_ge(skipped, g)
                V.tensor_tensor(stage[:], cen[:, at, :], bcast(rstd[:, at].unsqueeze(2), [P, TT, D]), ALU.mult).then_inc(staged, 1)

            def lower(g):
                s = LG[:, 0:TT * E].rearrange("p (x e) -> p x e", x=TT)
                e.wait_ge(routed, g + 1)
                ch.link(V.tensor_reduce(mx[:], s, AX.X, ALU.max))
                V.tensor_tensor(low[:], s, bcast(mx[:].unsqueeze(2), [P, TT, E]), ALU.subtract).then_inc(lowered, 1)

            def choose(g, j):
                e.wait_ge(exped, g + 1)
                ch.link(V.tensor_reduce(zs[:, 0], ex[:], AX.X, ALU.add))
                ch.link(V.reciprocal(zs[:, 1], zs[:, 0]))
                ch.link(V.tensor_tensor(prob[:], ex[:], bcast(zs[:, 1].unsqueeze(2), [P, TT, E]), ALU.mult))
                hold(e, vheld)
                for x in range(TT):
                    ch.add(V.max(top[:, x, :], prob[:, x, :]))
                ch.wait()
                ch.add(V.tensor_tensor(den[:, 0], top[:, :, 0], top[:, :, 1], ALU.add))
                ch.link(V.memset(top[:, :, 2:8], -1.0))
                ch.link(V.tensor_scalar(den[:, 0], den[:, 0], 1e-12, None, ALU.max))
                hold(e, vheld)
                for x in range(TT):
                    ch.add(V.match_replace(rest[:, x, :], top[:, x, :], prob[:, x, :], 0.0))
                ch.add(V.reciprocal(den[:, 1], den[:, 0]))
                ch.wait()
                ch.link(V.tensor_tensor(rest[:], prob[:], rest[:], ALU.subtract))
                ch.link(V.tensor_tensor(comb[:, j], rest[:], bcast(den[:, 1].unsqueeze(2), [P, TT, E]), ALU.mult))

            def weigh(g, j, x):
                e.wait_ge(out_ready, TT * g + x + 1)
                e.wait_ge(summed, TT * g + x + 1)
                V.tensor_tensor(weighed[:, x % 2], OUT[x % 2][:].rearrange("p (e d) -> p e d", e=E),
                                bcast(comb[:, j, x, :].unsqueeze(2), [P, E, D]), ALU.mult).then_inc(out_used, 1)

            def add_up(g, j, x):
                e.wait_ge(out_used, TT * g + x + 3)
                V.tensor_reduce(total[:, j, x, :], weighed[:, x % 2].rearrange("p e d -> p d e"), AX.X, ALU.add).then_inc(summed, 1)

            e.sem_inc(out_used, 2)
            e.sem_inc(added, 2)
            e.sem_inc(summed, 2)
            e.wait_ge(loaded, 80)
            V.tensor_tensor(w2[:], bcast(w2in[:].unsqueeze(2), [P, PAIRS, 2, D]),
                            bcast(pmask[:].unsqueeze(1).unsqueeze(3), [P, PAIRS, 2, D]), ALU.mult).then_inc(w2_ready, 1)
            to_stage(0)
            lower(0)
            choose(0, 0)
            to_stage(1)
            start = ch.n
            per_group = 18
            with e.Fori(0, B // 2) as i:
                for j in range(2):
                    g = 2 * i + j
                    ch.base, ch.n = g * per_group + start, 0
                    weigh(g, j, 0)
                    lower(g + 1)
                    weigh(g, j, 1)
                    e.wait_ge(added, g + 1)
                    add_up(g, j, 0)
                    choose(g + 1, 1 - j)
                    add_up(g, j, 1)
                    weigh(g, j, 2)
                    weigh(g, j, 3)
                    add_up(g, j, 2)
                    add_up(g, j, 3)
                    to_stage(g + 2)
                    assert ch.n == per_group, ch.n


def store(nc, k, out):
    with nc.semaphore("stored") as stored, nc.Block() as block:
        @block.sync
        def _(sp):
            sp.dma_start(out.rearrange("(t p) d -> p t d", p=P), k["h"][:]).then_inc(stored, 16)
            sp.wait_ge(stored, 16)


def _layout(a):
    import numpy as np

    f = {n: np.ascontiguousarray(x) for n, x in a.items()}
    io = {}
    for i, n in enumerate(["x", "itok_BS_0_255", "itok_BS_0_511", "itok_BS_0_127", "itok_BS_0_63", "itok_BS_0_3"]):
        io[f"id{i}"] = f[n]
    rowid = np.full((P, 4), -1.0, np.float32)
    tables = np.zeros((EMB + 1, 4 * P), np.float32)
    names = ["E_et", "E_fc", "E_sc", "E_of", "E_tt", "E_rc"]
    for chn, parts in VOCAB.items():
        for which, first, n in parts:
            rowid[first:first + n, chn] = np.arange(n)
            tables[16 * which:16 * which + 16, chn * P + first:chn * P + first + n] = f["L0_tok_" + names[which]].T
    tables[EMB, P:2 * P] = 1.0
    io["rowid"], io["tables_t"] = rowid, tables
    io["ident"] = np.eye(P, dtype=np.float32)
    io["w_t"] = f["L0_tok_W"].T
    io["w_bias"] = f["L0_tok_b"][None]
    io["gamma_beta"] = np.broadcast_to(np.stack([f["L0_tok_gamma"], f["L0_tok_beta"]])[None], (P, 2, D))
    ssm = [{n: f[f"L0_attn_{d}_{n}"] for n in ("log_real", "imag", "log_Delta", "B_real", "B_imag", "C_real", "C_imag", "D")}
           for d in ("fwd", "bwd")]
    prm = np.stack([np.stack([s["log_real"], s["imag"], s["log_Delta"]], -1) for s in ssm], 1)
    io["ssm_prm"] = np.concatenate([prm, prm], 0)
    io["ssm_b"] = np.stack([np.stack([np.concatenate([s["B_real"], s["B_imag"]]), np.concatenate([s["B_imag"], s["B_real"]])], 1)
                            for s in ssm], 1)
    io["ssm_c"] = np.stack([np.stack([np.concatenate([s["C_real"].T, s["C_imag"].T]), np.concatenate([s["C_imag"].T, s["C_real"].T])], 1)
                            for s in ssm], 1)
    io["ssm_d"] = np.stack([s["D"] for s in ssm], 1)
    io["wq_pk_t"] = f["L0_ffn_Wq_pk"].reshape(D, 2 * H, DK).transpose(2, 1, 0)
    io["pk_keys_t"] = f["L0_ffn_pk_keys"].transpose(3, 0, 2, 1).reshape(DK, 2 * H, NK)
    io["wq"] = f["L0_ffn_Wq"].reshape(D, H, D)
    io["wo"] = f["L0_ffn_Wo"].reshape(H, D, D).transpose(1, 0, 2)
    rows = np.concatenate([f["L0_ffn_values_table"], f["L0_ffn_keys_table"]], 1)
    rows = rows.reshape(H, 2, JT // 4, 4, 2, NK // 2, P)
    rows = np.stack([rows[:, second, :, :, first] for first, second in ((0, 0), (1, 0), (1, 1), (0, 1))])
    io["table"] = rows.transpose(3, 4, 1, 0, 2, 5).reshape(P, H * JT * P)
    pair_sel = np.zeros((2, 2, 2, NK // 2, JT // 4, 4, NK // 2), np.float16)
    for order in range(2):
        for u in range(JT // 4):
            for s in range(4):
                pair_sel[order, order, :, np.arange(NK // 2), u, s, np.arange(NK // 2)] = 1
                pair_sel[order, 1 - order, :, 4 * u + s, u, s, :] = 1
    pair_sel = pair_sel.reshape(2, P, JT // 4, P).transpose(1, 0, 2, 3)
    io["pair_sel"] = pair_sel
    io["tile_sel"] = np.broadcast_to(np.eye(TT, dtype=np.float32)[:, :, None], (TT, TT, D))
    qkv_w = np.concatenate([f["L1_attn_qkv_w"], f["L1_attn_qkv_b"][None]])
    io["w_qk"], io["w_v"] = qkv_w[:, :P], qkv_w[:, P:]
    io["w_p"] = np.concatenate([f["L1_attn_proj_w"], f["L1_attn_proj_b"][None]])
    io["head_rows"] = np.repeat(np.eye(H, dtype=np.float32), HD, 0)
    io["half_rows"] = np.repeat(np.eye(2, dtype=np.float32), W, 0)
    io["router_t"] = f["L1_ffn_router_w"].T
    io["w1"] = np.concatenate([f["L1_ffn_w1"].transpose(1, 0, 2).reshape(D, -1), f["L1_ffn_b1"].reshape(1, -1)])
    io["w2"] = f["L1_ffn_w2"].reshape(EXPERTS // 2, P, D).transpose(1, 0, 2)
    io["b2"] = f["L1_ffn_b2"].reshape(1, -1)
    io["causal"] = np.triu(np.full((P, P), -1e30, np.float32), 1)
    io["ident16"] = np.eye(P, dtype=np.float16)
    io["sign_half"] = np.repeat(np.array([1.0, -1.0], np.float32), D)[:, None]
    return {n: np.ascontiguousarray(x) for n, x in io.items()}


def kernel(**inputs):
    import concourse.bacc as _bacc
    from concourse.bass_utils import run_bass_kernel_spmd as _run

    nc = _bacc.Bacc("TRN2", target_bir_lowering=False, num_devices=1)
    arrays = {f"in_{n}": a for n, a in _layout(inputs).items()}
    io = {n[3:]: nc.dram_tensor(n, list(a.shape), mybir.dt.from_np(a.dtype), kind="ExternalInput").ap() for n, a in arrays.items()}
    out = nc.dram_tensor("out", [B * S, D], F32, kind="ExternalOutput").ap()
    program(nc, io, out)
    r = _run(nc, [arrays], core_ids=[0])
    return r.results[0]["out"].reshape(B, S, D)
```

```python
from contextlib import ExitStack

import concourse.bass as bass
from concourse import mybir

F32 = mybir.dt.float32
F16 = mybir.dt.float16
BF16 = mybir.dt.bfloat16
I32 = mybir.dt.int32
ALU = mybir.AluOpType
ACT = mybir.ActivationFunctionType
AX = mybir.AxisListType

P = 128
B, S, D = 16, 512, 64
TT = S // P
NT = B * TT
EPS = 1e-5
ROUND = 1.5 * 2.0 ** 23

VOCAB = {0: ((0, 0, 64), (1, 64, 64)), 1: ((2, 0, 128),), 2: ((3, 0, 128),), 3: ((4, 0, 64), (5, 64, 4))}
ROWS = (128, 128, 128, 68)
EMB = 96

H = 8
DK = 32
NK = 64
JT = NK * NK // P
TOPK = 16
SHIFT = 44.0
CAP = 2 * SHIFT
W = 64
HD = D // H
EXPERTS = 8


class Chain:

    def __init__(self, eng, sem, base=0):
        self.eng, self.sem, self.base, self.n = eng, sem, base, 0

    def add(self, ins):
        ins.then_inc(self.sem, 1)
        self.n += 1

    def wait(self):
        self.eng.wait_ge(self.sem, self.base + self.n)

    def link(self, ins):
        self.add(ins)
        self.wait()


def hold(eng, sem):
    eng.sem_inc(sem, 1)


def warm_up(nc, k, out, n=4):
    for _ in range(n):
        nc.tensor.matmul(out[:], k["ident"][:], k["cen"][:, 0:8, :].rearrange("p t d -> p (t d)"), start=True, stop=True)


def bcast(ap, shape):
    return ap.broadcast_to(shape)


def program(nc, io, out):
    with ExitStack() as ctx:
        def sb(name, shape, dt=F32, scope=ctx):
            return scope.enter_context(nc.sbuf_tensor(name, shape, dt))

        bank = [ctx.enter_context(nc.psum_tensor(f"bank{i}", [P, 512], F32)) for i in range(8)]
        k = {
            "bank": bank,
            "h": sb("h", [P, NT, D]),
            "cen": sb("cen", [P, NT, D]),
            "rstd": sb("rstd", [P, NT]),
            "ident": sb("ident", [P, P]),
            "held": ctx.enter_context(nc.semaphore("held")),
        }
        with ExitStack() as ssm:
            k["ssm"] = {
                "inw": sb("ssm_inw", [D, 2, 2, P], scope=ssm),
                "outw": sb("ssm_outw", [P, 2, 2, D], scope=ssm),
                "skip": sb("ssm_skip", [D, 2, D], scope=ssm),
                "cos": sb("ssm_cos", [P, 2, S], scope=ssm),
                "sin": sb("ssm_sin", [P, 2, S], scope=ssm),
                "decay": sb("ssm_decay", [P, 2, S], scope=ssm),
            }
            with ExitStack() as emb:
                k["rowtab"] = sb("rowtab", [P, 4, D], scope=emb)
                prepare(nc, io, k)
                embed(nc, io, k)
            norm_affine(nc, io, k)
            ssm_layer(nc, io, k)
        statistics(nc, k, "pk")
        product_key_layer(nc, io, k)
        statistics(nc, k, "win")
        window_attention(nc, io, k)
        statistics(nc, k, "moe")
        experts(nc, io, k)
        store(nc, k, out)


def prepare(nc, io, k):
    bank, ssm = k["bank"], k["ssm"]
    with ExitStack() as c:
        def sb(name, shape, dt=F32):
            return c.enter_context(nc.sbuf_tensor(name, shape, dt))

        def sem(name):
            return c.enter_context(nc.semaphore(name))

        wt = sb("wt", [EMB + 1, D])
        tern = sb("tern", [EMB, D])
        tab = sb("tab", [EMB + 1, 4 * P])
        ones = sb("ones", [EMB, EMB])
        colsum = sb("colsum", [EMB, 4])
        prm = sb("prm", [P, 2, 3])
        bx = sb("bx", [P, 2, 2, D])
        cx = sb("cx", [P, 2, 2, D])
        dx = sb("dx", [D, 2])
        sgn = sb("sgn", [P, 1])
        g = sb("g", [P, 2, 2, D])
        q = sb("q", [P, 24, 2])
        tmp = sb("tmp", [P, 2, S // 2])
        loaded = sem("p_loaded")
        dve = sem("p_dve")
        act_done = sem("p_act")
        pe_done = sem("p_pe")
        act_need = sem("p_act_need")
        block = c.enter_context(nc.Block())
        LR, IM, LD, DEL, AD, BD, R, N1, ARG, SN, CS, NRM, LBR, LBI, DEN, IR, II, T0, T1, CR, CI, SCI, SCR, ARGC = range(24)

        def v(i):
            return q[:, i, :]

        @block.sync
        def _(sp):
            loads = [(k["ident"][:], io["ident"]), (wt[0:EMB, :], io["w_t"]), (wt[EMB:EMB + 1, :], io["w_bias"]),
                     (tab[:], io["tables_t"]), (prm[:], io["ssm_prm"]), (bx[:], io["ssm_b"]), (cx[:], io["ssm_c"]),
                     (dx[:], io["ssm_d"]), (sgn[:], io["sign_half"])]
            for dst, src in loads:
                sp.dma_start(dst, src).then_inc(loaded, 16)

        NLOAD = 9 * 16

        @block.scalar
        def _(act):
            act.wait_ge(loaded, NLOAD)
            nc.scalar.activation(v(LR), prm[:, :, 0], ACT.Exp).then_inc(act_done, 1)
            nc.scalar.activation(v(DEL), prm[:, :, 2], ACT.Exp).then_inc(act_done, 1)
            act.wait_ge(act_need, 1)
            nc.scalar.activation(v(R), v(AD), ACT.Exp).then_inc(act_done, 1)
            act.wait_ge(act_need, 2)
            nc.scalar.activation(v(SN), v(ARG), ACT.Sin).then_inc(act_done, 1)
            nc.scalar.activation(v(CS), v(ARGC), ACT.Sin).then_inc(act_done, 1)

        @block.tensor
        def _(pe):
            pe.wait_ge(loaded, NLOAD)
            pe.wait_ge(act_need, 3)
            nc.tensor.matmul(bank[0][0:EMB, 0:1], ones[:], colsum[:, 0:1], start=True, stop=True).then_inc(pe_done, 1)
            pe.wait_ge(act_need, 4)
            for ch in range(4):
                last = nc.tensor.matmul(bank[1][:, ch * D:(ch + 1) * D], tab[:, ch * P:(ch + 1) * P], wt[:],
                                        start=True, stop=True)
            last.then_inc(pe_done, 1)
            pe.wait_ge(act_need, 5)
            for d in range(2):
                for j in range(2):
                    last = nc.tensor.transpose(bank[2][0:D, (2 * d + j) * P:(2 * d + j + 1) * P], g[:, d, j, :],
                                               k["ident"][:])
            last.then_inc(pe_done, 1)

        @block.vector
        def _(e):
            ch = Chain(e, dve)
            V = nc.vector
            turn = (6.28125, 0.0019353071795864769)

            def tt(o, a, b, op):
                ch.link(V.tensor_tensor(o, a, b, op))

            def ts(o, a, s1, s2, op0, op1=None):
                ch.link(V.tensor_scalar(o, a, s1, s2, op0, op1) if op1 is not None else V.tensor_scalar(o, a, s1, s2, op0))

            e.wait_ge(loaded, NLOAD)
            e.wait_ge(act_done, 2)
            ts(v(LR), v(LR), -1.0, None, ALU.mult)
            tt(v(AD), v(LR), v(DEL), ALU.mult)
            V.tensor_tensor(v(BD), prm[:, :, 1], v(DEL), ALU.mult).then_inc(act_need, 1)
            e.wait_ge(act_need, 1)
            for dst, add in ((ARG, 0.0), (ARGC, 1.5707963267948966)):
                ts(v(BD if add else T0), v(BD), add, None, ALU.add)
                ts(v(N1), v(BD), 1.0 / 6.283185307179586, None, ALU.mult)
                ts(v(N1), v(N1), ROUND, None, ALU.add)
                ts(v(N1), v(N1), -ROUND, None, ALU.add)
                ts(v(T1), v(N1), -turn[0], None, ALU.mult)
                tt(v(dst), v(BD), v(T1), ALU.add)
                ts(v(T1), v(N1), -turn[1], None, ALU.mult)
                tt(v(dst), v(dst), v(T1), ALU.add)
                ts(v(dst), v(dst), -3.1415925, 3.1415925, ALU.max, ALU.min)
            V.memset(ones[:], 1.0).then_inc(act_need, 1)
            e.wait_ge(act_need, 2)
            V.tensor_reduce(colsum[:, 0:1], wt[0:EMB, :], AX.X, ALU.add, apply_absolute_value=True).then_inc(act_need, 1)
            e.wait_ge(pe_done, 1)
            ts(colsum[:, 1:2], bank[0][0:EMB, 0:1], 1.0 / (EMB * D), None, ALU.mult)
            ts(colsum[:, 2:3], colsum[:, 1:2], 1e-8, None, ALU.add)
            ch.link(V.reciprocal(colsum[:, 3:4], colsum[:, 2:3]))
            ts(tern[:], wt[0:EMB, :], colsum[:, 3:4], None, ALU.mult)
            ts(tern[:], tern[:], ROUND, None, ALU.add)
            ts(tern[:], tern[:], -ROUND, None, ALU.add)
            ts(tern[:], tern[:], -1.0, 1.0, ALU.max, ALU.min)
            ts(tern[:], tern[:], colsum[:, 1:2], None, ALU.mult)
            tt(tern[:], tern[:], wt[0:EMB, :], ALU.subtract)
            V.tensor_tensor(wt[0:EMB, :], wt[0:EMB, :], tern[:], ALU.add).then_inc(act_need, 1)
            e.wait_ge(act_need, 4)
            e.wait_ge(pe_done, 2)
            ch.link(V.tensor_copy(k["rowtab"][:], bank[1][:, 0:4 * D].rearrange("p (c d) -> p c d", c=4)))
            e.wait_ge(act_done, 5)

            def unit():
                tt(v(T0), v(CS), v(CS), ALU.mult)
                tt(v(T1), v(SN), v(SN), ALU.mult)
                tt(v(NRM), v(T0), v(T1), ALU.add)
                ts(v(NRM), v(NRM), -0.5, 1.5, ALU.mult, ALU.add)
                tt(v(CS), v(CS), v(NRM), ALU.mult)
                tt(v(SN), v(SN), v(NRM), ALU.mult)

            unit()
            tt(v(LBR), v(R), v(CS), ALU.mult)
            tt(v(LBI), v(R), v(SN), ALU.mult)
            tt(v(T0), v(LR), v(LR), ALU.mult)
            tt(v(T1), prm[:, :, 1], prm[:, :, 1], ALU.mult)
            tt(v(DEN), v(T0), v(T1), ALU.add)
            ts(v(DEN), v(DEN), 1e-12, None, ALU.max)
            ch.link(V.reciprocal(v(DEN), v(DEN)))
            tt(v(IR), v(LR), v(DEN), ALU.mult)
            tt(v(II), prm[:, :, 1], v(DEN), ALU.mult)
            ts(v(II), v(II), -1.0, None, ALU.mult)
            ts(v(LBR), v(LBR), -1.0, None, ALU.add)
            tt(v(T0), v(IR), v(LBR), ALU.mult)
            tt(v(T1), v(II), v(LBI), ALU.mult)
            tt(v(CR), v(T0), v(T1), ALU.subtract)
            tt(v(T0), v(IR), v(LBI), ALU.mult)
            tt(v(T1), v(II), v(LBR), ALU.mult)
            tt(v(CI), v(T0), v(T1), ALU.add)
            ts(v(SCI), v(CI), sgn[:, 0:1], None, ALU.mult)
            ts(v(SCR), v(CR), sgn[:, 0:1], None, ALU.mult)
            for d in range(2):
                ts(g[:, d, 0, :], bx[:, d, 1, :], q[:, SCI, d:d + 1], -1.0, ALU.mult, ALU.mult)
                ch.link(V.scalar_tensor_tensor(g[:, d, 0, :], bx[:, d, 0, :], q[:, CR, d:d + 1], g[:, d, 0, :],
                                               ALU.mult, ALU.add))
                ts(g[:, d, 1, :], bx[:, d, 1, :], q[:, SCR, d:d + 1], None, ALU.mult)
                ch.link(V.scalar_tensor_tensor(g[:, d, 1, :], bx[:, d, 0, :], q[:, CI, d:d + 1], g[:, d, 1, :],
                                               ALU.mult, ALU.add))
                ts(ssm["outw"][:, d, 0, :], cx[:, d, 0, :], sgn[:, 0:1], None, ALU.mult)
                ts(ssm["outw"][:, d, 1, :], cx[:, d, 1, :], -1.0, None, ALU.mult)
                ts(ssm["skip"][:, d, :], k["ident"][0:D, 0:D], dx[:, d:d + 1], None, ALU.mult)
            V.memset(ssm["cos"][:, :, 0:1], 1.0).then_inc(act_need, 1)
            e.wait_ge(act_need, 5)
            ch.link(V.memset(ssm["sin"][:, :, 0:1], 0.0))
            ch.link(V.memset(ssm["decay"][:], 1.0))
            for d in range(2):
                ts(ssm["decay"][:, d, :], ssm["decay"][:, d, :], q[:, R, d:d + 1], None, ALU.mult)
            n = 1
            while n < S:
                for d in range(2):
                    old_c, old_s = ssm["cos"][:, d, 0:n], ssm["sin"][:, d, 0:n]
                    new_c, new_s = ssm["cos"][:, d, n:2 * n], ssm["sin"][:, d, n:2 * n]
                    cs, sn = q[:, CS, d:d + 1], q[:, SN, d:d + 1]
                    ch.add(V.tensor_scalar(tmp[:, 0, 0:n], old_s, sn, None, ALU.mult))
                    ch.link(V.tensor_scalar(tmp[:, 1, 0:n], old_c, sn, None, ALU.mult))
                    ch.add(V.scalar_tensor_tensor(new_c, old_c, cs, tmp[:, 0, 0:n], ALU.mult, ALU.subtract))
                    ch.link(V.scalar_tensor_tensor(new_s, old_s, cs, tmp[:, 1, 0:n], ALU.mult, ALU.add))
                n *= 2
                if n < S:
                    tt(v(T0), v(CS), v(CS), ALU.mult)
                    tt(v(T1), v(SN), v(SN), ALU.mult)
                    tt(v(NRM), v(CS), v(SN), ALU.mult)
                    tt(v(CS), v(T0), v(T1), ALU.subtract)
                    ts(v(SN), v(NRM), 2.0, None, ALU.mult)
                    unit()
            e.wait_ge(pe_done, 3)
            ch.link(V.tensor_copy(ssm["inw"][:], bank[2][0:D, :].rearrange("p (d j s) -> p d j s", d=2, j=2)))


def embed(nc, io, k):
    bank, h = k["bank"], k["h"]
    with ExitStack() as c:
        def sb(name, shape, dt=F32):
            return c.enter_context(nc.sbuf_tensor(name, shape, dt))

        def sem(name):
            return c.enter_context(nc.semaphore(name))

        ids = sb("ids", [P, 2, 4, S], I32)
        hot = sb("hot", [P, 2, 4, S], BF16)
        tabp = sb("tabp", [P, 4, 3, D], BF16)
        left = sb("left", [P, 2, 4, D])
        z = sb("z", [P, 2, TT, 3, D])
        zsum = sb("zsum", [P, 2, TT, D])
        rowid = sb("rowid", [P, 4])
        row_ready = sem("e_row")
        ids_ready = [sem("e_ids0"), sem("e_ids1")]
        hot_ready, z_ready, pieced, z_copied, summed = (
            sem(x) for x in ("e_hot", "e_z", "e_pieced", "e_copied", "e_summed"))
        block = c.enter_context(nc.Block())
        names = ["id0", "id1", "id2", "id3", "id4", "id5"]

        @block.sync
        def _(sp):
            sp.dma_start(rowid[:], io["rowid"]).then_inc(row_ready, 16)

            def load(b, j):
                for chn, parts in VOCAB.items():
                    for which, first, n in parts:
                        sp.dma_start(ids[first:first + n, j, chn, :],
                                     bcast(io[names[which]][bass.ds(b, 1), :], [n, S])).then_inc(ids_ready[j], 16)

            for j in range(2):
                load(j, j)
            with sp.Fori(1, B // 2) as i:
                for j in range(2):
                    sp.wait_ge(hot_ready, (2 * i + j - 1) * 4)
                    load(2 * i + j, j)

        @block.vector
        def _(e):
            e.wait_ge(row_ready, 16)
            V, tab = nc.vector, k["rowtab"]
            ch = Chain(e, pieced)
            for n, c4 in ((slice(0, P), slice(0, 3)), (slice(0, ROWS[3]), slice(3, 4))):
                ch.link(V.tensor_copy(tabp[n, c4, 0, :], tab[n, c4, :]))
                ch.link(V.tensor_tensor(left[n, 0, c4, :], tab[n, c4, :], tabp[n, c4, 0, :], ALU.subtract))
                ch.link(V.tensor_copy(tabp[n, c4, 1, :], left[n, 0, c4, :]))
                ch.link(V.tensor_tensor(left[n, 1, c4, :], left[n, 0, c4, :], tabp[n, c4, 1, :], ALU.subtract))
                ch.link(V.tensor_copy(tabp[n, c4, 2, :], left[n, 1, c4, :]))
            with e.Fori(0, B // 2) as i:
                for j in range(2):
                    e.wait_ge(ids_ready[j], (i + 1) * 96)
                    e.wait_ge(z_ready, 2 * i + j + 1)
                    for chn in range(4):
                        n = ROWS[chn]
                        nc.vector.tensor_scalar(hot[0:n, j, chn, :], ids[0:n, j, chn, :], rowid[0:n, chn:chn + 1],
                                                None, ALU.is_equal).then_inc(hot_ready, 1)

        @block.tensor
        def _(pe):
            pe.wait_ge(pieced, 10)
            pe.sem_inc(z_ready, 2)
            with pe.Fori(0, B // 2) as i:
                for j in range(2):
                    g = 2 * i + j
                    pe.wait_ge(hot_ready, (g + 1) * 4)
                    pe.wait_ge(z_copied, 2 * g + 2)
                    for t in range(TT):
                        o = bank[2 * j + t // 2][:, t % 2 * 3 * D:(t % 2 + 1) * 3 * D]
                        for chn in range(4):
                            n = ROWS[chn]
                            last = nc.tensor.matmul(o, hot[0:n, j, chn, t * P:(t + 1) * P],
                                                    tabp[0:n, chn].rearrange("p q d -> p (q d)"), start=(chn == 0), stop=(chn == 3))
                    last.then_inc(z_ready, 1)

        @block.scalar
        def _(act):
            act.sem_inc(z_copied, 4)
            with act.Fori(0, B // 2) as i:
                for j in range(2):
                    g = 2 * i + j
                    act.wait_ge(z_ready, g + 3)
                    act.wait_ge(summed, 2 * g + 2)
                    for t in range(2):
                        nc.scalar.activation(z[:, j, 2 * t:2 * t + 2].rearrange("p t q d -> p (t q d)"),
                                             bank[2 * j + t][:, 0:6 * D], ACT.Copy).then_inc(z_copied, 1)

        @block.gpsimd
        def _(pool):
            pool.sem_inc(summed, 4)
            with pool.Fori(0, B // 2) as i:
                for j in range(2):
                    g = 2 * i + j
                    pool.wait_ge(z_copied, 2 * g + 6)
                    hold(pool, k["held"])
                    nc.gpsimd.tensor_tensor(zsum[:, j], z[:, j, :, 0, :], z[:, j, :, 1, :], ALU.add).then_inc(summed, 1)
                    pool.wait_ge(summed, 2 * g + 5)
                    hold(pool, k["held"])
                    nc.gpsimd.tensor_tensor(h[:, bass.ds(g * TT, TT), :], zsum[:, j], z[:, j, :, 2, :], ALU.add).then_inc(summed, 1)


def statistics(nc, k, tag, affine=None):
    h, cen, rstd = k["h"], k["cen"], k["rstd"]
    Q = 4
    N = NT // Q
    with ExitStack() as c:
        def sb(name, shape, dt=F32):
            return c.enter_context(nc.sbuf_tensor(f"{tag}_{name}", shape, dt))

        def sem(name):
            return c.enter_context(nc.semaphore(f"{tag}_{name}"))

        sq = sb("sq", [P, NT, D])
        st = sb("st", [P, 2, NT])
        gb = sb("gb", [P, 2, D])
        dve, centred, squared, var, std, loaded = (sem(x) for x in ("dve", "cen", "sq", "var", "std", "ld"))
        block = c.enter_context(nc.Block())

        if affine is not None:
            @block.sync
            def _(sp):
                sp.dma_start(gb[:], affine).then_inc(loaded, 16)

        @block.scalar
        def _(act):
            for i in range(Q):
                s = slice(i * N, (i + 1) * N)
                act.wait_ge(centred, i + 1)
                nc.scalar.activation(sq[:, s, :], cen[:, s, :], ACT.Square).then_inc(squared, 1)
            for i in range(Q):
                s = slice(i * N, (i + 1) * N)
                act.wait_ge(var, i + 1)
                nc.scalar.activation(st[:, 1, s], st[:, 0, s], ACT.Sqrt).then_inc(std, 1)

        @block.vector
        def _(e):
            V = nc.vector
            ch = Chain(e, dve)
            for i in range(Q):
                s = slice(i * N, (i + 1) * N)
                ch.link(V.tensor_reduce(st[:, 0, s], h[:, s, :], AX.X, ALU.add))
                ch.link(V.tensor_scalar(st[:, 0, s], st[:, 0, s], 1.0 / D, None, ALU.mult))
                V.tensor_tensor(cen[:, s, :], h[:, s, :], bcast(st[:, 0, s].unsqueeze(2), [P, N, D]),
                                ALU.subtract).then_inc(centred, 1)
            for i in range(Q):
                s = slice(i * N, (i + 1) * N)
                e.wait_ge(squared, i + 1)
                ch.link(V.tensor_reduce(st[:, 0, s], sq[:, s, :], AX.X, ALU.add))
                V.tensor_scalar(st[:, 0, s], st[:, 0, s], 1.0 / D, EPS, ALU.mult, ALU.add).then_inc(var, 1)
            for i in range(Q):
                s = slice(i * N, (i + 1) * N)
                e.wait_ge(std, i + 1)
                ch.link(V.reciprocal(rstd[:, s], st[:, 1, s]))
                if affine is not None:
                    if i == 0:
                        e.wait_ge(loaded, 16)
                        e.wait_ge(centred, Q)
                    ch.link(V.tensor_tensor(h[:, s, :], cen[:, s, :], bcast(rstd[:, s].unsqueeze(2), [P, N, D]), ALU.mult))
                    ch.link(V.tensor_tensor(h[:, s, :], h[:, s, :], bcast(gb[:, 0:1, :], [P, N, D]), ALU.mult))
                    ch.link(V.tensor_tensor(h[:, s, :], h[:, s, :], bcast(gb[:, 1:2, :], [P, N, D]), ALU.add))


def norm_affine(nc, io, k):
    statistics(nc, k, "tok", io["gamma_beta"])
    statistics(nc, k, "ssm")


def ssm_layer(nc, io, k):
    bank, h, cen, rstd, ssm = k["bank"], k["h"], k["cen"], k["rstd"], k["ssm"]
    with ExitStack() as c:
        def sb(name, shape, dt=F32):
            return c.enter_context(nc.sbuf_tensor(f"s_{name}", shape, dt))

        def sem(name):
            return c.enter_context(nc.semaphore(f"s_{name}"))

        stage = sb("stage", [P, 2, TT, D])
        xs = sb("xs", [D, 4, S])
        part = sb("part", [P, 2, 2, S])
        turned = sb("turned", [P, 2, S])
        state = sb("state", [P, 2, 2, S])
        back = sb("back", [P, 2, 2, 2, S])
        both = sb("both", [P, 2, S])
        pair = sb("pair", [P, D])
        layer_out = sb("layer_out", [P, B, TT * D])
        staged, turned_t, xs_ready, u_ready, u_used, parts, sums, scanned, backed, y_ready, y_used, added = (
            sem(x) for x in ("staged", "tr", "xs", "u", "uused", "parts", "sums", "scan", "back", "y", "yused", "added"))
        sum_ready, sum_used, pair_ready = sem("sum"), sem("sumused"), sem("pair")
        block = c.enter_context(nc.Block())

        def along(table, d):
            return ssm[table][:, d, :] if d == 0 else ssm[table][:, d, ::-1]

        @block.tensor
        def _(pe):
            def transposes(g, j):
                pe.wait_ge(staged, g + 1)
                hold(pe, k["held"])
                for t in range(TT):
                    last = nc.tensor.transpose(bank[0][0:D, t * P:(t + 1) * P], stage[:, j % 2, t, :], k["ident"][:])
                last.then_inc(turned_t, 1)

            def inputs(g, j):
                pe.wait_ge(xs_ready, g + 1)
                for d in range(2):
                    for half in range(2):
                        pe.wait_ge(u_used, g * 4 + 2 * d + half + 1)
                        nc.tensor.matmul(bank[1 + 2 * d + half][:], ssm["inw"][:, d, half, :], xs[:, j, :],
                                         start=True, stop=True).then_inc(u_ready, 1)

            def outputs(g, j):
                pe.wait_ge(y_used, g + 1)
                pe.wait_ge(backed, 4 * g + 5)
                o = bank[5 + j % 2]
                for n in range(3):
                    for d in range(2):
                        w = (ssm["outw"][:, d, 0, :], ssm["outw"][:, d, 1, :], ssm["skip"][:, d, :])[n]
                        x = (back[:, j % 2, d, 0, :], back[:, j % 2, d, 1, :], xs[:, j, :])[n]
                        last = nc.tensor.matmul(o[d * D:(d + 1) * D, :], w, x, start=(n == 0), stop=(n == 2))
                last.then_inc(y_ready, 1)

            def add_directions(g, j):
                pe.wait_ge(y_used, g + 3)
                pe.wait_ge(sum_used, g + 1)
                hold(pe, k["held"])
                for t in range(TT):
                    last = nc.tensor.matmul(bank[7][:, t * D:(t + 1) * D], both[:, j % 2, t * P:(t + 1) * P], pair[:],
                                            start=True, stop=True)
                last.then_inc(sum_ready, 1)

            pe.wait_ge(pair_ready, 1)
            transposes(0, 0)
            pe.wait_ge(xs_ready, 1)
            transposes(1, 1)
            inputs(0, 0)
            inputs(1, 1)
            transposes(2, 2)
            with pe.Fori(0, B // 4) as i:
                for j in range(4):
                    g = 4 * i + j
                    outputs(g, j)
                    inputs(g + 2, (j + 2) % 4)
                    transposes(g + 3, (j + 3) % 4)
                    add_directions(g, j)

        @block.scalar
        def _(act):
            def copy(g, j):
                act.wait_ge(turned_t, g + 1)
                nc.scalar.activation(xs[:, j, :], bank[0][0:D, :], ACT.Copy).then_inc(xs_ready, 1)

            act.sem_inc(y_used, 2)
            act.sem_inc(sum_used, 1)
            copy(0, 0)
            copy(1, 1)
            copy(2, 2)
            with act.Fori(0, B // 4) as i:
                for j in range(4):
                    g = 4 * i + j
                    act.wait_ge(y_ready, g + 1)
                    nc.scalar.activation(both[:, j % 2, :], bank[5 + j % 2][:], ACT.Gelu).then_inc(y_used, 1)
                    copy(g + 3, (j + 3) % 4)
                    act.wait_ge(sum_ready, g + 1)
                    nc.scalar.activation(layer_out[:, bass.ds(g, 1), :], bank[7][:, 0:TT * D].unsqueeze(1),
                                         ACT.Copy).then_inc(sum_used, 1)

        @block.gpsimd
        def _(pool):
            pool.sem_inc(sums, 1)
            pool.sem_inc(backed, 1)
            with pool.Fori(0, B // 2) as i:
                for j in range(2):
                    g = 2 * i + j
                    pool.wait_ge(parts, g + 1)
                    nc.gpsimd.tensor_tensor(turned[:, 1, :], part[:, 1, 0, :], part[:, 1, 1, :], ALU.add).then_inc(sums, 1)
                    pool.wait_ge(y_used, g + 1)
                    for d in range(2):
                        pool.wait_ge(scanned, 2 * g + d + 1)
                        for half, table in enumerate(("cos", "sin")):
                            nc.gpsimd.tensor_tensor(back[:, j, d, half, :], state[:, j, d, :], along(table, d),
                                                    ALU.mult).then_inc(backed, 1)
            pool.wait_ge(sum_used, B + 1)
            hs = h[:, 0:NT // 4, :].rearrange("p (b t) d -> p b (t d)", b=B // 4)
            nc.gpsimd.tensor_tensor(hs, hs, layer_out[:, 0:B // 4, :], ALU.add).then_inc(added, 1)

        @block.vector
        def _(e):
            V = nc.vector

            def to_stage(g, j):
                e.wait_ge(turned_t, g - 1)
                at = bass.ds(g % B * TT, TT) if not isinstance(g, int) else slice(g * TT, (g + 1) * TT)
                V.tensor_tensor(stage[:, j], cen[:, at, :], bcast(rstd[:, at].unsqueeze(2), [P, TT, D]),
                                ALU.mult).then_inc(staged, 1)

            e.sem_inc(u_used, 4)
            V.tensor_tensor(pair[:], k["ident"][:, 0:D], k["ident"][:, D:P], ALU.add).then_inc(pair_ready, 1)
            for g in range(2):
                V.tensor_tensor(stage[:, g], cen[:, g * TT:(g + 1) * TT, :],
                                bcast(rstd[:, g * TT:(g + 1) * TT].unsqueeze(2), [P, TT, D]), ALU.mult).then_inc(staged, 1)
            to_stage(2, 0)
            with e.Fori(0, B // 2) as i:
                for j in range(2):
                    g = 2 * i + j
                    e.wait_ge(sums, g + 1)
                    for d in range(2):
                        for half, table in enumerate(("cos", "sin")):
                            e.wait_ge(u_ready, 4 * g + 2 * d + half + 1)
                            V.tensor_tensor(part[:, d, half, :], bank[1 + 2 * d + half][:], along(table, d),
                                            ALU.mult).then_inc(u_used, 1)
                    e.wait_ge(u_used, 4 * g + 8)
                    V.tensor_tensor(turned[:, 0, :], part[:, 0, 0, :], part[:, 0, 1, :], ALU.add).then_inc(parts, 1)
                    to_stage(g + 3, 1 - j)
                    e.wait_ge(backed, 4 * g + 1)
                    e.wait_ge(parts, g + 1)
                    V.tensor_tensor_scan(state[:, j, 0, :], ssm["decay"][:, 0, :], turned[:, 0, :], 0.0,
                                         ALU.mult, ALU.add).then_inc(scanned, 1)
                    e.wait_ge(sums, g + 2)
                    V.tensor_tensor_scan(state[:, j, 1, ::-1], ssm["decay"][:, 1, :], turned[:, 1, ::-1], 0.0,
                                         ALU.mult, ALU.add).then_inc(scanned, 1)
            e.sem_inc(u_used, 4)
            e.wait_ge(sum_used, B + 1)
            hs = h[:, NT // 4:, :].rearrange("p (b t) d -> p b (t d)", b=3 * B // 4)
            V.tensor_tensor(hs, hs, layer_out[:, B // 4:, :], ALU.add).then_inc(scanned, 1)


def product_key_layer(nc, io, k):
    with ExitStack() as c:
        def sb(name, shape, dt=F32):
            return c.enter_context(nc.sbuf_tensor(f"k_{name}", shape, dt))

        t = {
            "xt": sb("xt", [D, B * S]),
            "keyw": sb("keyw", [D, H, 2 * NK]),
            "wq": sb("wq", [D, H, D]),
            "wo": sb("wo", [D, H, D]),
        }
        merge_keys(nc, io, k, t)
        turn_tokens(nc, k, "kt", t["xt"])
        memory_turns(nc, io, k, t)


def merge_keys(nc, io, k, t):
    bank = k["bank"]
    with ExitStack() as c:
        def sb(name, shape, dt=F32):
            return c.enter_context(nc.sbuf_tensor(f"m_{name}", shape, dt))

        def sem(name):
            return c.enter_context(nc.semaphore(f"m_{name}"))

        wpk = sb("wpk", [DK, 2 * H, D])
        keys = sb("keys", [DK, 2 * H, NK])
        loaded, merged, copied = sem("loaded"), sem("merged"), sem("copied")
        block = c.enter_context(nc.Block())

        @block.sync
        def _(sp):
            for dst, src in ((wpk[:], io["wq_pk_t"]), (keys[:], io["pk_keys_t"]), (t["wq"][:], io["wq"]), (t["wo"][:], io["wo"])):
                sp.dma_start(dst, src).then_inc(loaded, 16)

        @block.tensor
        def _(pe):
            pe.wait_ge(loaded, 64)
            for i in range(2 * H):
                last = nc.tensor.matmul(bank[i // H][0:D, (i % H) * NK:(i % H + 1) * NK], wpk[:, i, :], keys[:, i, :],
                                        start=True, stop=True)
            last.then_inc(merged, 1)

        @block.vector
        def _(e):
            e.wait_ge(merged, 1)
            for half in range(2):
                nc.vector.tensor_copy(t["keyw"][:, :, half * NK:(half + 1) * NK],
                                      bank[half][0:D, :].rearrange("p (h n) -> p h n", h=H)).then_inc(copied, 1)


def turn_tokens(nc, k, tag, xt):
    bank, cen, rstd = k["bank"], k["cen"], k["rstd"]
    with ExitStack() as c:
        def sem(name):
            return c.enter_context(nc.semaphore(f"{tag}_{name}"))

        stage = c.enter_context(nc.sbuf_tensor(f"{tag}_stage", [P, 2, TT, D], F32))
        staged, turned, copied = sem("staged"), sem("turned"), sem("copied")
        block = c.enter_context(nc.Block())

        @block.vector
        def _(e):
            e.sem_inc(turned, 2)
            with e.Fori(0, B // 2) as i:
                for j in range(2):
                    g = 2 * i + j
                    at = bass.ds(g * TT, TT)
                    e.wait_ge(turned, g + 1)
                    nc.vector.tensor_tensor(stage[:, j], cen[:, at, :], bcast(rstd[:, at].unsqueeze(2), [P, TT, D]),
                                            ALU.mult).then_inc(staged, 1)

        @block.tensor
        def _(pe):
            with pe.Fori(0, B // 2) as i:
                for j in range(2):
                    g = 2 * i + j
                    pe.wait_ge(copied, g + 1)
                    pe.wait_ge(staged, g + 1)
                    hold(pe, k["held"])
                    for x in range(TT):
                        last = nc.tensor.transpose(bank[j][0:D, x * P:(x + 1) * P], stage[:, j, x, :], k["ident"][:])
                    last.then_inc(turned, 1)

        @block.scalar
        def _(act):
            act.sem_inc(copied, 2)
            with act.Fori(0, B // 2) as i:
                for j in range(2):
                    g = 2 * i + j
                    act.wait_ge(turned, g + 3)
                    nc.scalar.activation(xt[0:D, bass.ds(g * S, S)], bank[j][0:D, :], ACT.Copy).then_inc(copied, 1)


def candidates():
    runs, at, a = [], 0, 0
    while a < TOPK:
        n = TOPK // (a + 1)
        m = sum(1 for x in range(a, TOPK) if TOPK // (x + 1) == n)
        runs.append((a, m, n, at))
        at += m * n
        a += m
    return runs, at


def memory_turns(nc, io, k, t):
    bank, h, ident = k["bank"], k["h"], k["ident"]
    Z = bank[0:4]
    KV, SC, X, Y = bank[4:8]
    SC16, Y16 = SC[:].bitcast(F16), Y[:].bitcast(BF16)
    RUNS, NCAND = candidates()
    CANDS = len(RUNS) + 1
    CONSTS = 4
    N = H * B
    ATT = [dict(sim=6, peak=7, exp=8, turn=9, copy=10, out=11, add=12),
           dict(sim=9, peak=10, exp=11, turn=12, copy=13, out=14, add=15),
           dict(sim=12, peak=13, exp=14, turn=16, copy=17, out=18, add=19),
           dict(sim=16, peak=17, exp=18, turn=20, copy=21, out=22, add=23)]
    with ExitStack() as c:
        def sb(name, shape, dt=F32):
            return c.enter_context(nc.sbuf_tensor(f"k_{name}", shape, dt))

        def sem(name):
            return c.enter_context(nc.semaphore(f"k_{name}"))

        table = sb("table", [P, 2, JT, P])
        sel = sb("sel", [P, 2, JT // 4, P], F16)
        ident16 = sb("ident16", [P, P], F16)
        selz = sb("selz", [3 * TT, TT, D], BF16)
        selz32 = sb("selz32", [3 * TT, TT, D])
        causal = sb("causal", [P, P])
        cmask = sb("cmask", [P, P], BF16)
        identb = sb("identb", [P, P], BF16)
        halves = sb("halves", [P, TT, 5, 2, NK // 2], F16)
        pieces = sb("pieces", [P, 2, 4, S], F16)
        ew = sb("ew", [P, 4, S])
        wt = sb("w", [P, 4, S])
        xs = sb("xs", [D, 2, S])
        wqs = sb("wqs", [D, 2, D])
        ss = sb("ss", [P, TT, 2, NK])
        rest = sb("rest", [P, TT, 2, NK])
        best = sb("best", [P, 2, TT, TOPK])
        under = sb("under", [P, 2, TT, TOPK])
        cand = sb("cand", [P, TT, NCAND])
        crest = sb("crest", [P, TT, NCAND])
        final = sb("final", [P, TT, TOPK])
        junk = sb("junk", [P, TT, TOPK])
        sm = sb("sm", [P, 2, TT])
        ab = sb("ab", [P, TT, 5, NK // 2])
        zsum = sb("zsum", [P, TT])
        zi = sb("zi", [P, 2, TT])
        kvs = sb("kvs", [P, S])
        zleft = sb("zleft", [P, 2, TT])
        zp = sb("zp", [P, 2, 3, TT], BF16)
        zr = sb("zr", [3 * TT, P], BF16)
        ks = sb("ks", [D, S])
        qs = sb("qs", [D, S])
        vp = sb("vp", [P, TT, D])
        pr = sb("pr", [P, 2, S])
        pt = sb("pt", [P, S])
        peak = sb("peak", [P, TT])
        rsum = sb("rsum", [P, TT])
        rinv = sb("rinv", [P, TT])
        S_ = {x: sem(x) for x in (
            "ready", "table0", "table1", "consts", "masks", "zpieces", "zeroed", "staged",
            "scores", "sscopy", "ranked", "cands", "offsets",
            "zsummed", "abready", "abturned", "hi", "lo", "pieces", "zready", "exp", "weight", "product", "kvcopy",
            "qready", "qcopy", "zrow", "zrcopy", "zbcast", "kready", "vproj", "vready", "sim", "peaked", "prob",
            "probt", "ptcopy", "attout", "added", "dve")}
        block = c.enter_context(nc.Block())
        s = S_

        @block.sync
        def _(sp):
            for dst, src in ((sel[:], io["pair_sel"]), (selz32[:], io["tile_sel"]), (causal[:], io["causal"]),
                             (ident16[:], io["ident16"])):
                sp.dma_start(dst, src).then_inc(s["consts"], 16)

            def load(head, j):
                cols = bass.ds(head * JT * P, JT * P)
                sp.dma_start(table[:, j].rearrange("p t d -> p (t d)"), io["table"][:, cols]).then_inc(s[f"table{j}"], 16)

            for j in range(2):
                load(j, j)
            with sp.Fori(1, H // 2) as i:
                for j in range(2):
                    sp.wait_ge(s["product"], (2 * i + j - 1) * B * JT + 4)
                    load(2 * i + j, j)

        def turns(eng, body):
            with eng.Fori(0, H // 2) as i:
                for tb in range(2):
                    with eng.Fori(0, B // 2) as y:
                        for j in range(2):
                            body((2 * i + tb) * B + 2 * y + j, j, tb, 2 * y + j, 2 * i + tb, i)

        @block.gpsimd
        def _(pool):
            G = nc.gpsimd
            for x in (zi, kvs, qs, zp):
                G.memset(x[:], 0.0).then_inc(s["zeroed"], 1)

            def stage(n, j):
                if isinstance(n, int):
                    at, hd = slice(0, S), slice(0, 1)
                else:
                    at, hd = bass.ds(n % B * S, S), bass.ds(n // B % H, 1)
                G.tensor_copy(xs[:, j, :], t["xt"][:, at]).then_inc(s["staged"], 1)
                G.tensor_copy(wqs[:, j:j + 1, :], t["wq"][:, hd, :]).then_inc(s["staged"], 1)

            def combine(n):
                pool.wait_ge(s["ranked"], 2 * TT * (n + 1))
                G.tensor_tensor(under[:], best[:], bcast(best[:, :, :, 0:1], [P, 2, TT, TOPK]), ALU.subtract).then_inc(s["cands"], 1)
                pool.wait_ge(s["cands"], CANDS * n + 1)
                for a, m, cnt, at in RUNS:
                    o = cand[:, :, at:at + m * cnt].rearrange("p t (m c) -> p t m c", m=m)
                    G.tensor_tensor(o, bcast(under[:, 0, :, a:a + m].unsqueeze(3), [P, TT, m, cnt]),
                                    bcast(under[:, 1, :, 0:cnt].unsqueeze(2), [P, TT, m, cnt]), ALU.add).then_inc(s["cands"], 1)

            stage(0, 0)
            combine(0)

            def body(n, j, tb, b, hd, i):
                pool.wait_ge(s["qready"], n + 1)
                stage(n + 1, 1 - j)
                combine(n + 1)
            turns(pool, body)

        @block.tensor
        def _(pe):
            T = nc.tensor

            def scores(n, j):
                pe.wait_ge(s["staged"], 2 * n + 2)
                pe.wait_ge(s["pieces"], 2 * n)
                hd = 0 if isinstance(n, int) else bass.ds(n // B % H, 1)
                rhs = t["keyw"][:, 0:1, :] if isinstance(n, int) else t["keyw"][:, hd, :]
                for x in range(TT):
                    last = T.matmul(SC[:, x * P:(x + 1) * P], xs[:, j, x * P:(x + 1) * P], rhs, start=True, stop=True)
                last.then_inc(s["scores"], 1)

            def turn_pieces(n, r):
                if r == 0:
                    pe.wait_ge(s["lo"], n + 1)
                else:
                    pe.wait_ge(s["pieces"], 2 * n + 1)
                hold(pe, k["held"])
                for bb in range(2):
                    for x in range(TT):
                        at = bb * S + x * P
                        last = T.transpose(SC16[:, at:at + P], halves[:, x, 2 * r + bb:2 * r + bb + 2].rearrange("p b q k -> p (b q k)"), ident16[:])
                last.then_inc(s["abturned"], 1)

            def pair_scores(n, jp, j):
                g = n * JT + jp
                if jp % (JT // 2) == 0:
                    pe.wait_ge(s["pieces"], 2 * n + 2 * jp // JT + 1)
                pe.wait_ge(s["weight"], g + 1)
                T.matmul(Z[jp % 4][:], sel[:, jp // (JT // 4) % 2, jp % (JT // 4), :], pieces[:, j, jp // (JT // 4), :],
                         start=True, stop=True).then_inc(s["zready"], 1)

            def product(n, jp, tb, i):
                if jp == 0:
                    pe.wait_ge(s["kvcopy"], n + 1)
                    pe.wait_ge(s[f"table{tb}"], 16 * i + 16)
                pe.wait_ge(s["weight"], n * JT + jp + 5)
                last = T.matmul(KV[:], table[:, tb, jp, :], wt[:, jp % 4, :], start=(jp == 0), stop=(jp == JT - 1))
                last.then_inc(s["product"], 1)
                if jp == JT - 1:
                    return last

            def query(n, j):
                pe.wait_ge(s["prob"], 4 * n + 4)
                hold(pe, k["held"])
                for a in range(2):
                    last = T.matmul(X[a * D:(a + 1) * D, 0:S // 2], wqs[:, j, :], xs[:, j, a * S // 2:(a + 1) * S // 2],
                                    start=True, stop=True)
                last.then_inc(s["qready"], 1)

            def zinv_row(n, j):
                pe.wait_ge(s["added"], 4 * n + 1)
                pe.wait_ge(s["zpieces"], n + 1)
                hold(pe, k["held"])
                T.transpose(Y16[0:3 * TT, 0:P], zp[:, 1 - j].rearrange("p a t -> p (a t)"), identb[:]).then_inc(s["zrow"], 1)

            def zinv_spread(n):
                pe.wait_ge(s["zrcopy"], n + 1)
                hold(pe, k["held"])
                for x in range(TT):
                    last = T.matmul(Y[0:D, x * P:(x + 1) * P], selz[:, x, :], zr[:], start=True, stop=True)
                last.then_inc(s["zbcast"], 1)

            def value_project(n):
                pe.wait_ge(s["kready"], n + 1)
                hold(pe, k["held"])
                hd = (n + (H * B - 1)) // B % H
                for x in range(TT):
                    last = T.matmul(Y[:, x * D:(x + 1) * D], kvs[0:D, x * P:(x + 1) * P], t["wo"][:, bass.ds(hd, 1), :],
                                    start=True, stop=True)
                last.then_inc(s["vproj"], 1)

            def value_project_last():
                pe.wait_ge(s["kready"], N + 1)
                for x in range(TT):
                    last = T.matmul(Y[:, x * D:(x + 1) * D], kvs[0:D, x * P:(x + 1) * P], t["wo"][:, H - 1, :],
                                    start=True, stop=True)
                last.then_inc(s["vproj"], 1)

            def sim(n, it):
                w = (it + 1) * P
                if it == 0:
                    pe.wait_ge(s["qcopy"], 2 * n + 1)
                else:
                    pe.wait_ge(s["prob"], 4 * n + it)
                if it:
                    T.matmul(X[:, 0:w - P], qs[:, it * P:w], ks[:, 0:w - P], start=True, stop=True)
                T.matmul(X[:, w - P:w], qs[:, it * P:w], ks[:, w - P:w], start=True, stop=False)
                T.matmul(X[:, w - P:w], identb[:], cmask[:], start=False, stop=True).then_inc(s["sim"], 1)

            def prob_turn(n, it):
                if it == 0:
                    pe.wait_ge(s["vready"], n + 1)
                else:
                    pe.wait_ge(s["added"], 4 * n + it + 1)
                pe.wait_ge(s["prob"], 4 * n + it + 1)
                for x in range(it + 1):
                    last = T.transpose(Y[:, x * P:(x + 1) * P], pr[:, it % 2, x * P:(x + 1) * P], ident[:])
                last.then_inc(s["probt"], 1)

            def att_out(n, it):
                pe.wait_ge(s["ptcopy"], 4 * n + it + 1)
                for x in range(it + 1):
                    last = T.matmul(Y[:, 0:D], pt[:, x * P:(x + 1) * P], vp[:, x, :], start=(x == 0), stop=(x == it))
                last.then_inc(s["attout"], 1)

            for x in ("qready", "probt", "attout"):
                pe.sem_inc(s[x], 1)
            pe.wait_ge(s["consts"], CONSTS * 16)
            pe.wait_ge(s["zeroed"], 4)
            pe.wait_ge(s["masks"], 3)
            scores(0, 0)
            turn_pieces(0, 0)
            turn_pieces(0, 1)
            for jp in range(3):
                pair_scores(0, jp, 0)

            def body(n, j, tb, b, hd, i):
                for jp in range(JT):
                    if jp == 0:
                        scores(n + 1, 1 - j)
                    if jp == 1:
                        zinv_row(n, j)
                    if jp == 3:
                        zinv_spread(n)
                    if jp == 5:
                        value_project(n)
                    for it, at in enumerate(ATT):
                        if jp == at["out"]:
                            att_out(n, it)
                        if jp == at["turn"]:
                            prob_turn(n, it)
                    for it, at in enumerate(ATT):
                        if jp == at["sim"]:
                            sim(n, it)
                    if jp in (24, 26):
                        turn_pieces(n + 1, (jp - 24) // 2)
                    if jp == 27:
                        query(n, j)
                    if jp + 3 < JT:
                        pair_scores(n, jp + 3, j)
                    else:
                        pair_scores(n + 1, jp + 3 - JT, 1 - j)
                    last = product(n, jp, tb, i)
            turns(pe, body)
            zinv_row(N, 0)
            zinv_spread(N)
            value_project_last()
            for it in range(TT):
                sim(N, it)
                prob_turn(N, it)
                att_out(N, it)

        @block.scalar
        def _(act):
            A = nc.scalar

            def copy_scores(n):
                act.wait_ge(s["scores"], n + 1)
                act.wait_ge(s["abready"], n)
                A.activation(ss[:].rearrange("p t a k -> p (t a k)"), SC[:], ACT.Copy).then_inc(s["sscopy"], 1)

            def sums(n):
                act.wait_ge(s["offsets"], n + 1)
                for x in range(TT):
                    last = A.activation(junk[:, x, :], final[:, x, :], ACT.Exp, bias=sm[:, 1, x:x + 1],
                                        accum_out=zsum[:, x:x + 1])
                    last.then_inc(s["zsummed"], 1)

            def high(n):
                act.wait_ge(s["abready"], n + 1)
                act.wait_ge(s["abturned"], 2 * n)
                A.activation(halves[:].rearrange("p t b q k -> p (t b) q k")[:, :, 0, :],
                             ab[:].rearrange("p t b k -> p (t b) k"), ACT.Copy).then_inc(s["hi"], 1)

            def copy_pieces(n, j, r):
                act.wait_ge(s["abturned"], 2 * n + r + 1)
                A.activation(pieces[:, j, 2 * r:2 * r + 2, :].rearrange("p b t -> p (b t)"), SC16, ACT.Copy).then_inc(s["pieces"], 1)

            def exps(n, jp):
                g = n * JT + jp
                act.wait_ge(s["zready"], g + 1)
                act.wait_ge(s["weight"], g + 1)
                A.activation(ew[:, jp % 4, :], Z[jp % 4][:], ACT.Exp).then_inc(s["exp"], 1)

            def att_exp(n, it):
                w = (it + 1) * P
                act.wait_ge(s["peaked"], 4 * n + it + 1)
                act.wait_ge(s["probt"], 4 * n + max(it - 1, 0) + 1)
                A.activation(pr[:, it % 2, 0:w], X[:, 0:w], ACT.Exp, bias=peak[:, it:it + 1],
                             accum_out=rsum[:, it:it + 1]).then_inc(s["prob"], 1)

            def att_copy(n, it):
                w = (it + 1) * P
                act.wait_ge(s["probt"], 4 * n + it + 2)
                act.wait_ge(s["attout"], 4 * n + it + 1)
                A.activation(pt[:, 0:w], Y[:, 0:w], ACT.Copy).then_inc(s["ptcopy"], 1)

            for x in ("kvcopy", "qcopy"):
                act.sem_inc(s[x], 1)
            act.wait_ge(s["ready"], 1)
            act.wait_ge(s["zeroed"], 4)
            copy_scores(0)
            sums(0)
            high(0)
            copy_pieces(0, 0, 0)
            copy_pieces(0, 0, 1)
            exps(0, 0)
            exps(0, 1)

            def zr_copy(n):
                act.wait_ge(s["zrow"], n + 1)
                A.activation(zr[:], Y16[0:3 * TT, 0:P], ACT.Copy).then_inc(s["zrcopy"], 1)

            def body(n, j, tb, b, hd, i):
                for jp in range(JT):
                    if jp == 1:
                        copy_scores(n + 1)
                    if jp == 2:
                        zr_copy(n)
                    for it, at in enumerate(ATT):
                        if jp == at["exp"]:
                            att_exp(n, it)
                        if jp == at["copy"]:
                            att_copy(n, it)
                    if jp == 22:
                        sums(n + 1)
                    if jp == 23:
                        high(n + 1)
                    if jp in (25, 27):
                        copy_pieces(n + 1, 1 - j, (jp - 25) // 2)
                    if jp == 29:
                        act.wait_ge(s["qready"], n + 2)
                        for a in range(2):
                            A.activation(qs[:, a * S // 2:(a + 1) * S // 2], X[a * D:(a + 1) * D, 0:S // 2], ACT.Copy,
                                         scale=D ** -0.5).then_inc(s["qcopy"], 1)
                    if jp + 2 < JT:
                        exps(n, jp + 2)
                    else:
                        exps(n + 1, jp + 2 - JT)
                act.wait_ge(s["product"], (n + 1) * JT + 4)
                act.wait_ge(s["vproj"], n + 1)
                A.activation(kvs[:], KV[:], ACT.Copy).then_inc(s["kvcopy"], 1)
            turns(act, body)
            zr_copy(N)
            for it in range(TT):
                att_exp(N, it)
                att_copy(N, it)

        @block.vector
        def _(e):
            V = nc.vector
            ch = Chain(e, s["dve"])

            def rank(n, x):
                if x == 0:
                    e.wait_ge(s["sscopy"], n + 1)
                    e.wait_ge(s["cands"], CANDS * n)
                    hold(e, k["held"])
                for a in range(2):
                    ch.add(V.max(best[:, a, x, 0:8], ss[:, x, a, :]))
                ch.wait()
                hold(e, k["held"])
                for a in range(2):
                    ch.add(V.match_replace(rest[:, x, a, :], best[:, a, x, 0:8], ss[:, x, a, :], -3e38))
                ch.wait()
                hold(e, k["held"])
                for a in range(2):
                    V.max(best[:, a, x, 8:16], rest[:, x, a, :]).then_inc(s["ranked"], 1)

            def select(n, xs_):
                if xs_[0] == 0:
                    e.wait_ge(s["cands"], CANDS * (n + 1))
                    e.wait_ge(s["zsummed"], 4 * n)
                    hold(e, k["held"])
                for x in xs_:
                    ch.add(V.max(final[:, x, 0:8], cand[:, x, :]))
                ch.wait()
                hold(e, k["held"])
                for x in xs_:
                    ch.add(V.match_replace(crest[:, x, :], final[:, x, 0:8], cand[:, x, :], -3e38))
                ch.wait()
                hold(e, k["held"])
                for x in xs_:
                    ch.add(V.max(final[:, x, 8:16], crest[:, x, :]))
                ch.wait()

            def offsets(n):
                ch.link(V.tensor_scalar(sm[:, 0, :], final[:, :, TOPK - 1], -(1.0 + 2.0 ** -20), 2.0 ** -16, ALU.mult, ALU.add))
                V.tensor_scalar(sm[:, 1, :], sm[:, 0, :], CAP, -SHIFT, ALU.min, ALU.add).then_inc(s["offsets"], 1)

            def parts(n):
                e.wait_ge(s["hi"], n)
                k2 = NK // 2
                for a, out, src in ((0, ab[:, :, 0:3:2, :], ss[:, :, 0, :]), (0, ab[:, :, 4:5, :], ss[:, :, 0, 0:k2]),
                                    (1, ab[:, :, 1:4:2, :], ss[:, :, 1, :])):
                    m = out.shape[2]
                    ch.add(V.tensor_tensor(out, src.rearrange("p t (b k) -> p t b k", b=m),
                                           bcast(best[:, a, :, 0:1].unsqueeze(3), [P, TT, m, k2]), ALU.subtract))
                ch.wait()
                e.wait_ge(s["offsets"], n + 1)
                ch.link(V.tensor_tensor(ab[:, :, 1:4:2, :], ab[:, :, 1:4:2, :],
                                        bcast(sm[:, 1, :].unsqueeze(2).unsqueeze(3), [P, TT, 2, k2]), ALU.add))
                V.tensor_scalar(ab[:], ab[:], -30000.0, None, ALU.max).then_inc(s["abready"], 1)

            def zinv(n, j):
                e.wait_ge(s["zsummed"], 4 * n + 4)
                ch.link(V.reciprocal(zi[:, j, :], zsum[:]))
                ch.link(V.tensor_copy(zp[:, j, 0], zi[:, j, :]))
                ch.link(V.tensor_tensor(zleft[:, 0], zi[:, j, :], zp[:, j, 0], ALU.subtract))
                ch.link(V.tensor_copy(zp[:, j, 1], zleft[:, 0]))
                ch.link(V.tensor_tensor(zleft[:, 1], zleft[:, 0], zp[:, j, 1], ALU.subtract))
                V.tensor_copy(zp[:, j, 2], zleft[:, 1]).then_inc(s["zpieces"], 1)

            def low(n):
                e.wait_ge(s["hi"], n + 1)
                v = halves[:].rearrange("p t b q k -> p (t b) q k")
                V.tensor_tensor(v[:, :, 1, :], ab[:].rearrange("p t b k -> p (t b) k"), v[:, :, 0, :],
                                ALU.subtract).then_inc(s["lo"], 1)

            def weights(n, jp):
                g = n * JT + jp
                e.wait_ge(s["exp"], g + 1)
                e.wait_ge(s["product"], g + 1)
                V.scalar_tensor_tensor(wt[:, jp % 4, :], Z[jp % 4][:], -SHIFT, ew[:, jp % 4, :], ALU.is_ge,
                                       ALU.mult).then_inc(s["weight"], 1)

            def scale_keys(n):
                e.wait_ge(s["kvcopy"], n + 1)
                e.wait_ge(s["zbcast"], n + 1)
                V.tensor_tensor(ks[:], Y[0:D, :], kvs[D:P, :], ALU.mult).then_inc(s["kready"], 1)

            def scale_values(n, j):
                e.wait_ge(s["vproj"], n + 1)
                V.tensor_tensor(vp[:], Y[:, 0:TT * D].rearrange("p (t d) -> p t d", t=TT),
                                bcast(zi[:, 1 - j, :].unsqueeze(2), [P, TT, D]), ALU.mult).then_inc(s["vready"], 1)

            def att_peak(n, it):
                w = (it + 1) * P
                e.wait_ge(s["sim"], 4 * n + it + 1)
                V.tensor_reduce(peak[:, it:it + 1], X[:, 0:w], AX.X, ALU.max, negate=True).then_inc(s["peaked"], 1)

            def att_add(n, it):
                e.wait_ge(s["prob"], 4 * n + it + 1)
                ch.add(V.reciprocal(rinv[:, it:it + 1], rsum[:, it:it + 1]))
                e.wait_ge(s["attout"], 4 * n + it + 2)
                ch.wait()
                if isinstance(n, int):
                    at = h[:, (B - 1) * TT + it, :]
                    V.scalar_tensor_tensor(at, Y[:, 0:D], rinv[:, it:it + 1], at, ALU.mult, ALU.add).then_inc(s["added"], 1)
                else:
                    at = h[:, bass.ds((n + (B - 1)) % B * TT + it, 1), :]
                    V.scalar_tensor_tensor(at, Y[:, 0:D].unsqueeze(1), rinv[:, it:it + 1], at, ALU.mult,
                                           ALU.add).then_inc(s["added"], 1)

            e.sem_inc(s["weight"], 4)
            e.sem_inc(s["product"], 4)
            e.sem_inc(s["added"], 1)
            e.sem_inc(s["ready"], 1)
            e.wait_ge(s["zeroed"], 4)
            e.wait_ge(s["consts"], CONSTS * 16)
            V.tensor_copy(cmask[:], causal[:]).then_inc(s["masks"], 1)
            V.tensor_copy(identb[:], ident[:]).then_inc(s["masks"], 1)
            V.tensor_copy(selz[:], selz32[:]).then_inc(s["masks"], 1)
            e.sem_inc(s["zpieces"], 1)

            def first_half(n):
                for x in range(TT):
                    rank(n, x)

            first_half(0)
            select(0, (0, 1))
            select(0, (2, 3))
            offsets(0)
            parts(0)
            zinv(0, 0)
            low(0)
            e.wait_ge(s["exp"], 1)
            V.scalar_tensor_tensor(wt[:, 0, :], Z[0][:], -SHIFT, ew[:, 0, :], ALU.is_ge, ALU.mult).then_inc(s["weight"], 1)
            start = ch.n
            per_turn = 42

            def body(n, j, tb, b, hd, i):
                ch.base, ch.n = n * per_turn + start, 0
                for jp in range(JT):
                    if jp in (3, 5, 8, 9):
                        rank(n + 1, (3, 5, 8, 9).index(jp))
                    if jp == 4:
                        scale_keys(n)
                    if jp == 6:
                        scale_values(n, j)
                    for it, at in enumerate(ATT):
                        if jp == at["peak"]:
                            att_peak(n, it)
                        if jp == at["add"]:
                            att_add(n, it)
                    if jp == 14:
                        select(n + 1, (0, 1))
                    if jp == 16:
                        select(n + 1, (2, 3))
                    if jp == 18:
                        offsets(n + 1)
                    if jp == 20:
                        parts(n + 1)
                    if jp == 25:
                        zinv(n + 1, 1 - j)
                    if jp == 23:
                        low(n + 1)
                    if jp + 1 < JT:
                        weights(n, jp + 1)
                    else:
                        weights(n + 1, 0)
                assert ch.n == per_turn
            turns(e, body)
            ch.base, ch.n = N * per_turn + start, 0
            scale_keys(N)
            scale_values(N, 0)
            for it in range(TT):
                att_peak(N, it)
                att_add(N, it)


def window_attention(nc, io, k):
    bank, h, cen, rstd, ident = k["bank"], k["h"], k["cen"], k["rstd"], k["ident"]
    XT, IN, PT0, PT1, S0, S1, OUT, TAIL = bank
    NW = S // W
    with ExitStack() as c:
        def sb(name, shape, dt=F32):
            return c.enter_context(nc.sbuf_tensor(f"w_{name}", shape, dt))

        def sem(name):
            return c.enter_context(nc.semaphore(f"w_{name}"))

        wqk = sb("wqk", [D + 1, P])
        wv = sb("wv", [D + 1, D])
        wp = sb("wp", [D + 1, D])
        hmask = sb("hmask", [P, H])
        vmask = sb("vmask", [P, 2])
        stage = sb("stage", [P, TT, D])
        xs = sb("xs", [D + 1, NW, 2, W])
        q = sb("q", [P, 2, TT, P])
        kk = sb("kk", [P, TT, W])
        kblk = sb("kblk", [P, 2, TT, H, W])
        vblk = sb("vblk", [P, 2, NW * H // 2, 2, 2 * HD])
        raw = sb("raw", [P, S])
        mx = sb("mx", [P, 2, H])
        low = sb("low", [P, 2, H, W])
        ex = sb("ex", [P, 2, H * W])
        pt = sb("pt", [P, 2, S])
        rs = sb("rs", [P, TT, H])
        o = sb("o", [P, TT, D])
        ot = sb("ot", [D + 1, S])
        loaded, ones, staged, turned, xs_ready, qk_ready, q_ready, k_ready, kblk_ready, v_ready, vblk_ready, scored, \
            lowered, exped, pturned, pt_ready, o_ready, o_scaled, oturned, ot_ready, projected, added, dve = (
                sem(x) for x in ("loaded", "ones", "staged", "turned", "xs", "qk", "q", "k", "kblk", "v", "vblk", "scored",
                                 "lowered", "exped", "pturned", "pt", "o", "oscaled", "oturned", "ot", "proj", "added",
                                 "dve"))
        raw_ready, back_ready, zeroed = sem("raw"), sem("back"), sem("zeroed")
        block = c.enter_context(nc.Block())

        @block.sync
        def _(sp):
            for dst, src in ((wqk, "w_qk"), (wv, "w_v"), (wp, "w_p"), (hmask, "head_rows"), (vmask, "half_rows")):
                sp.dma_start(dst[:], io[src]).then_inc(loaded, 16)

        @block.tensor
        def _(pe):
            T = nc.tensor

            def turn_in(g):
                pe.wait_ge(staged, g + 1)
                pe.wait_ge(xs_ready, g)
                hold(pe, k["held"])
                for x in range(TT):
                    last = T.transpose(XT[0:D, x * P:(x + 1) * P], stage[:, x, :], ident[:])
                last.then_inc(turned, 1)

            def queries_keys(g):
                pe.wait_ge(xs_ready, g + 1)
                pe.wait_ge(vblk_ready, g)
                hold(pe, k["held"])
                T.matmul(IN[:], wqk[:], xs[:, :, 0, :], start=True, stop=True).then_inc(qk_ready, 1)

            def values(g):
                pe.wait_ge(k_ready, 2 * g + 2)
                pe.wait_ge(q_ready, 2 * g + 2)
                hold(pe, k["held"])
                for w in range(NW):
                    last = T.matmul(IN[:, w * D:(w + 1) * D], xs[:, w].rearrange("p a t -> p (a t)"), wv[:],
                                    start=True, stop=True)
                last.then_inc(v_ready, 1)

            def scores(g, j, x):
                if x == 0:
                    pe.wait_ge(q_ready, 2 * g + 2)
                if x % 2 == 0:
                    pe.wait_ge(kblk_ready, 2 * g + x // 2 + 1)
                pe.wait_ge(lowered, 4 * g + x + 1)
                hold(pe, k["held"])
                last = T.matmul((S0, S1)[x % 2][:], q[:, j, x, :], kblk[:, j, x].rearrange("p h t -> p (h t)"), start=True, stop=True)
                last.then_inc(scored, 1)

            def turn_probs(g, x):
                pe.wait_ge(exped, 4 * g + x + 3)
                pe.wait_ge(pt_ready, 4 * g + x + 1)
                for pair in range(H // 2):
                    s = slice(pair * P, (pair + 1) * P)
                    last = T.transpose((PT0, PT1)[x % 2][:, s], ex[:, x % 2, s], ident[:])
                last.then_inc(pturned, 1)

            def weigh(g, j, x):
                if x == 0:
                    pe.wait_ge(vblk_ready, g + 1)
                    pe.wait_ge(o_scaled, g + 1)
                pe.wait_ge(pt_ready, 4 * g + x + 3)
                hold(pe, k["held"])
                n = 4 * HD
                for w2 in range(2):
                    w = 2 * x + w2
                    for pair in range(H // 2):
                        last = T.matmul(OUT[pair * n:(pair + 1) * n, w * W:(w + 1) * W],
                                        vblk[:, j, w * (H // 2) + pair].rearrange("p a d -> p (a d)"),
                                        pt[:, x % 2, pair * P + w2 * W:pair * P + (w2 + 1) * W], start=True, stop=True)
                if x == TT - 1:
                    last.then_inc(o_ready, 1)

            def turn_back(g):
                pe.wait_ge(raw_ready, g + 1)
                hold(pe, k["held"])
                for x in range(TT):
                    last = T.transpose(OUT[:, x * P:(x + 1) * P], raw[:, x * P:(x + 1) * P], ident[:])
                last.then_inc(back_ready, 1)

            def turn_out(g):
                pe.wait_ge(o_scaled, g + 2)
                pe.wait_ge(added, g + 1)
                hold(pe, k["held"])
                for x in range(TT):
                    last = T.transpose(TAIL[0:D, x * P:(x + 1) * P], o[:, x, :], ident[:])
                last.then_inc(oturned, 1)

            def project(g):
                pe.wait_ge(ot_ready, g + 1)
                hold(pe, k["held"])
                for x in range(TT):
                    last = T.matmul(TAIL[:, x * D:(x + 1) * D], ot[:, x * P:(x + 1) * P], wp[:], start=True, stop=True)
                last.then_inc(projected, 1)

            pe.wait_ge(loaded, 80)
            pe.wait_ge(ones, 2)
            for g in range(2):
                turn_in(g)
                queries_keys(g)
                values(g)
            turn_in(2)
            warm_up(nc, k, TAIL)
            for x in range(3):
                scores(0, 0, x)
            turn_probs(0, 0)
            with pe.Fori(0, B // 2) as i:
                for j in range(2):
                    g = 2 * i + j
                    for x in range(TT):
                        turn_probs(g + (x + 1) // TT, (x + 1) % TT)
                        scores(g + (x + 3) // TT, (j + (x + 3) // TT) % 2, (x + 3) % TT)
                        weigh(g, j, x)
                    queries_keys(g + 2)
                    turn_back(g)
                    turn_in(g + 3)
                    turn_out(g)
                    values(g + 2)
                    project(g)

        @block.scalar
        def _(act):
            A = nc.scalar

            def copy_in(g):
                act.wait_ge(turned, g + 1)
                act.wait_ge(v_ready, g)
                A.activation(xs[0:D], bcast(XT[0:D, :].rearrange("p (w t) -> p w t", w=NW).unsqueeze(2), [D, NW, 2, W]),
                             ACT.Copy).then_inc(xs_ready, 1)

            def copy_qk(g, j):
                act.wait_ge(qk_ready, g + 1)
                act.wait_ge(kblk_ready, 2 * g)
                act.wait_ge(zeroed, 1)
                v = IN[:].rearrange("p (x a t) -> p x a t", x=TT, a=2)
                for a in range(2):
                    A.activation(kk[a * D:(a + 1) * D], v[D:P, :, a, :], ACT.Copy).then_inc(k_ready, 1)
                for a in range(2):
                    A.activation(q[a * D:(a + 1) * D, j, :, a * W:(a + 1) * W], v[0:D, :, a, :], ACT.Copy,
                                 scale=HD ** -0.5).then_inc(q_ready, 1)

            def exp(g, x):
                act.wait_ge(lowered, 4 * g + x + 3)
                A.activation(ex[:, x % 2, :], low[:, x % 2].rearrange("p h t -> p (h t)"), ACT.Exp).then_inc(exped, 1)

            def copy_probs(g, x):
                act.wait_ge(pturned, 4 * g + x + 1)
                A.activation(pt[:, x % 2, :], (PT0, PT1)[x % 2][:], ACT.Copy).then_inc(pt_ready, 1)

            act.sem_inc(pt_ready, 2)
            for g in range(2):
                copy_in(g)
                copy_qk(g, g)
            copy_in(2)
            exp(0, 0)
            exp(0, 1)
            copy_probs(0, 0)
            with act.Fori(0, B // 2) as i:
                for j in range(2):
                    g = 2 * i + j
                    for x in range(TT):
                        exp(g + (x + 2) // TT, (x + 2) % TT)
                        copy_probs(g + (x + 1) // TT, (x + 1) % TT)
                    act.wait_ge(o_ready, g + 1)
                    A.activation(raw[:], OUT[:], ACT.Copy).then_inc(raw_ready, 1)
                    copy_qk(g + 2, j)
                    act.wait_ge(oturned, g + 1)
                    A.activation(ot[0:D, :], TAIL[0:D, :], ACT.Copy).then_inc(ot_ready, 1)
                    copy_in(g + 3)

        @block.gpsimd
        def _(pool):
            G = nc.gpsimd

            def key_blocks(g, j):
                pool.wait_ge(k_ready, 2 * g + 2)
                half = TT // 2
                for s in (slice(0, half), slice(half, TT)):
                    G.tensor_tensor(kblk[:, j, s], bcast(kk[:, s].unsqueeze(2), [P, half, H, W]),
                                    bcast(hmask[:].unsqueeze(1).unsqueeze(3), [P, half, H, W]), ALU.mult).then_inc(kblk_ready, 1)

            G.memset(xs[D:D + 1], 1.0).then_inc(ones, 1)
            G.memset(ot[D:D + 1, :], 1.0).then_inc(ones, 1)
            pool.wait_ge(loaded, 80)
            for g in range(2):
                key_blocks(g, g)
            with pool.Fori(0, B // 2) as i:
                for j in range(2):
                    key_blocks(2 * i + j + 2, j)

        @block.vector
        def _(e):
            V = nc.vector
            ch = Chain(e, dve)

            def to_stage(g):
                at = slice(g * TT, (g + 1) * TT) if isinstance(g, int) else bass.ds(g % B * TT, TT)
                e.wait_ge(turned, g)
                V.tensor_tensor(stage[:], cen[:, at, :], bcast(rstd[:, at].unsqueeze(2), [P, TT, D]), ALU.mult).then_inc(staged, 1)

            def lower(g, x):
                s = (S0, S1)[x % 2][:].rearrange("p (h t) -> p h t", h=H)
                e.wait_ge(scored, 4 * g + x + 1)
                ch.link(V.tensor_reduce(mx[:, x % 2, :], s, AX.X, ALU.max))
                e.wait_ge(exped, 4 * g + x + 1)
                V.tensor_tensor(low[:, x % 2], s, bcast(mx[:, x % 2, :].unsqueeze(2), [P, H, W]), ALU.subtract).then_inc(lowered, 1)

            def value_blocks(g, j):
                e.wait_ge(v_ready, g + 1)
                V.tensor_tensor(vblk[:, j, :, :, 0:HD], IN[:].rearrange("p (n a d) -> p n a d", a=2, d=HD),
                                bcast(vmask[:].unsqueeze(1).unsqueeze(3), [P, NW * H // 2, 2, HD]), ALU.mult).then_inc(vblk_ready, 1)

            def scale(g):
                out = OUT[:].rearrange("p (x h d) -> p x h d", x=TT, h=H)
                e.wait_ge(back_ready, g + 1)
                ch.link(V.reciprocal(rs[:], out[:, :, :, HD]))
                V.tensor_tensor(o[:].rearrange("p x (h d) -> p x h d", h=H), out[:, :, :, 0:HD],
                                bcast(rs[:].unsqueeze(3), [P, TT, H, HD]), ALU.mult).then_inc(o_scaled, 1)

            def add(g):
                at = bass.ds(g * TT, TT)
                e.wait_ge(projected, g + 1)
                V.tensor_tensor(h[:, at, :], h[:, at, :], TAIL[:, 0:TT * D].rearrange("p (x d) -> p x d", x=TT),
                                ALU.add).then_inc(added, 1)

            V.memset(q[:], 0.0).then_inc(zeroed, 1)
            e.sem_inc(lowered, 2)
            e.sem_inc(exped, 2)
            e.sem_inc(o_scaled, 1)
            e.sem_inc(added, 1)
            to_stage(0)
            e.wait_ge(loaded, 80)
            ch.link(V.memset(vblk[:], 0.0))
            for j in range(2):
                ch.add(V.tensor_copy(vblk[:, j, :, :, HD], bcast(vmask[:].unsqueeze(1), [P, NW * H // 2, 2])))
            ch.wait()
            for g in range(2):
                to_stage(g + 1)
                value_blocks(g, g)
            to_stage(3)
            for x in range(3):
                lower(0, x)
            start = ch.n
            per_group = 5
            with e.Fori(0, B // 2) as i:
                for j in range(2):
                    g = 2 * i + j
                    ch.base, ch.n = g * per_group + start, 0
                    for x in range(TT):
                        lower(g + (x + 3) // TT, (x + 3) % TT)
                    scale(g)
                    value_blocks(g + 2, j)
                    add(g)
                    to_stage(g + 4)
                    assert ch.n == per_group


def experts(nc, io, k):
    bank, h, cen, rstd, ident = k["bank"], k["h"], k["cen"], k["rstd"], k["ident"]
    XT, LG = bank[0:2]
    HID, OUT = bank[2:4], bank[4:6]
    E, PAIRS = EXPERTS, EXPERTS // 2
    with ExitStack() as c:
        def sb(name, shape, dt=F32):
            return c.enter_context(nc.sbuf_tensor(f"e_{name}", shape, dt))

        def sem(name):
            return c.enter_context(nc.semaphore(f"e_{name}"))

        router = sb("router", [D, E])
        w1 = sb("w1", [D + 1, E * D])
        w2 = sb("w2", [P, PAIRS, 2, D])
        w2in = sb("w2in", [P, PAIRS, D])
        pmask = sb("pmask", [P, 2])
        b2 = sb("b2", [1, E * D])
        b2part = sb("b2part", [1, 2, E * D])
        b2low = sb("b2low", [1, 2, E * D], BF16)
        b2rows = sb("b2rows", [D + 1, E * D], BF16)
        one = sb("one", [D + 1, P], BF16)
        skip = sb("skip", [P, 2, TT, D])
        stage = sb("stage", [P, TT, D])
        xs = sb("xs", [D + 1, S])
        hid = sb("hid", [P, 2, PAIRS, S])
        mx = sb("mx", [P, TT])
        low = sb("low", [P, TT, E])
        ex = sb("ex", [P, TT, E])
        zs = sb("zs", [P, 2, TT])
        prob = sb("prob", [P, TT, E])
        top = sb("top", [P, TT, 8])
        rest = sb("rest", [P, TT, E])
        den = sb("den", [P, 2, TT])
        comb = sb("comb", [P, 2, TT, E])
        weighed = sb("weighed", [P, 2, E, D])
        total = sb("total", [P, 2, TT, D])
        loaded, ones, w2_ready, staged, turned, xs_ready, routed, lowered, exped, hid_ready, gelued, out_ready, out_used, \
            summed, added, dve, skips, b2_ready = (
                sem(x) for x in ("loaded", "ones", "w2", "staged", "turned", "xs", "routed", "lowered", "exped", "hid",
                                 "gelued", "out", "outused", "summed", "added", "dve", "skips", "b2"))
        block = c.enter_context(nc.Block())

        @block.sync
        def _(sp):
            for dst, src in ((router, "router_t"), (w1, "w1"), (w2in, "w2"), (pmask, "half_rows"), (b2, "b2")):
                sp.dma_start(dst[:], io[src]).then_inc(loaded, 16)

        @block.tensor
        def _(pe):
            T = nc.tensor

            def turn_in(g):
                pe.wait_ge(staged, g + 1)
                pe.wait_ge(xs_ready, g)
                hold(pe, k["held"])
                for x in range(TT):
                    last = T.transpose(XT[0:D, x * P:(x + 1) * P], stage[:, x, :], ident[:])
                last.then_inc(turned, 1)

            def route(g):
                pe.wait_ge(xs_ready, g + 1)
                pe.wait_ge(lowered, g)
                hold(pe, k["held"])
                for x in range(TT):
                    last = T.matmul(LG[:, x * E:(x + 1) * E], xs[0:D, x * P:(x + 1) * P], router[:], start=True, stop=True)
                last.then_inc(routed, 1)

            def hidden(g, p):
                pe.wait_ge(gelued, PAIRS * g + p + 1)
                hold(pe, k["held"])
                T.matmul(HID[p % 2][:], w1[:, p * P:(p + 1) * P], xs[:], start=True, stop=True).then_inc(hid_ready, 1)

            def output(g, j, x):
                if x == 0:
                    pe.wait_ge(gelued, PAIRS * (g + 1) + 2)
                pe.wait_ge(out_used, TT * g + x + 1)
                hold(pe, k["held"])
                for p in range(PAIRS):
                    s = slice(p * P, (p + 1) * P)
                    T.matmul(OUT[x % 2][:, s], one[:], b2rows[:, s], start=True, stop=False)
                    last = T.matmul(OUT[x % 2][:, s], hid[:, j, p, x * P:(x + 1) * P],
                                    w2[:, p].rearrange("p a d -> p (a d)"), start=False, stop=True)
                last.then_inc(out_ready, 1)

            pe.wait_ge(loaded, 80)
            pe.wait_ge(ones, 2)
            pe.wait_ge(w2_ready, 1)
            pe.wait_ge(b2_ready, 2)
            turn_in(0)
            route(0)
            for p in range(PAIRS):
                hidden(0, p)
            turn_in(1)
            warm_up(nc, k, bank[7])
            route(1)
            with pe.Fori(0, B // 2) as i:
                for j in range(2):
                    g = 2 * i + j
                    output(g, j, 0)
                    hidden(g + 1, 0)
                    output(g, j, 1)
                    hidden(g + 1, 1)
                    hidden(g + 1, 2)
                    output(g, j, 2)
                    hidden(g + 1, 3)
                    turn_in(g + 2)
                    output(g, j, 3)
                    route(g + 2)

        @block.scalar
        def _(act):
            A = nc.scalar

            def front(g):
                act.wait_ge(turned, g + 1)
                A.activation(xs[0:D, :], XT[0:D, :], ACT.Copy).then_inc(xs_ready, 1)
                act.wait_ge(lowered, g + 1)
                A.activation(ex[:], low[:], ACT.Exp).then_inc(exped, 1)

            def gelu(g, j):
                for p in range(PAIRS):
                    act.wait_ge(hid_ready, PAIRS * g + p + 1)
                    A.activation(hid[:, j, p, :], HID[p % 2][:], ACT.Gelu).then_inc(gelued, 1)

            act.sem_inc(gelued, 2)
            front(0)
            gelu(0, 0)
            front(1)
            with act.Fori(0, B // 2) as i:
                for j in range(2):
                    gelu(2 * i + j + 1, 1 - j)
                    front(2 * i + j + 2)

        @block.gpsimd
        def _(pool):
            G = nc.gpsimd

            G.memset(xs[D:D + 1, :], 1.0).then_inc(ones, 1)
            pool.wait_ge(ones, 1)
            G.memset(one[:], 1.0).then_inc(ones, 1)
            pool.sem_inc(added, 2)
            pool.wait_ge(ones, 2)
            with pool.Fori(0, B // 2) as i:
                for j in range(2):
                    g = 2 * i + j
                    at = bass.ds(g * TT, TT)
                    pool.wait_ge(added, g + 2)
                    hold(pool, k["held"])
                    G.tensor_tensor(skip[:, j], cen[:, at, :], bcast(rstd[:, at].unsqueeze(2), [P, TT, D]), ALU.mult).then_inc(skips, 1)
                    pool.wait_ge(skips, 2 * g + 1)
                    hold(pool, k["held"])
                    G.tensor_tensor(h[:, at, :], h[:, at, :], skip[:, j], ALU.add).then_inc(skips, 1)
                    pool.wait_ge(summed, TT * (g + 1) + 2)
                    pool.wait_ge(skips, 2 * g + 2)
                    hold(pool, k["held"])
                    G.tensor_tensor(h[:, at, :], h[:, at, :], total[:, j], ALU.add).then_inc(added, 1)

        @block.vector
        def _(e):
            V = nc.vector
            ch = Chain(e, dve)

            def to_stage(g):
                at = slice(g * TT, (g + 1) * TT) if isinstance(g, int) else bass.ds(g % B * TT, TT)
                e.wait_ge(turned, g)
                V.tensor_tensor(stage[:], cen[:, at, :], bcast(rstd[:, at].unsqueeze(2), [P, TT, D]), ALU.mult).then_inc(staged, 1)

            def lower(g):
                s = LG[:, 0:TT * E].rearrange("p (x e) -> p x e", x=TT)
                e.wait_ge(routed, g + 1)
                ch.link(V.tensor_reduce(mx[:], s, AX.X, ALU.max))
                V.tensor_tensor(low[:], s, bcast(mx[:].unsqueeze(2), [P, TT, E]), ALU.subtract).then_inc(lowered, 1)

            def choose(g, j):
                e.wait_ge(exped, g + 1)
                ch.link(V.tensor_reduce(zs[:, 0], ex[:], AX.X, ALU.add))
                ch.link(V.reciprocal(zs[:, 1], zs[:, 0]))
                ch.link(V.tensor_tensor(prob[:], ex[:], bcast(zs[:, 1].unsqueeze(2), [P, TT, E]), ALU.mult))
                hold(e, k["held"])
                for x in range(TT):
                    ch.add(V.max(top[:, x, :], prob[:, x, :]))
                ch.wait()
                ch.add(V.tensor_tensor(den[:, 0], top[:, :, 0], top[:, :, 1], ALU.add))
                ch.link(V.memset(top[:, :, 2:8], -1.0))
                ch.link(V.tensor_scalar(den[:, 0], den[:, 0], 1e-12, None, ALU.max))
                hold(e, k["held"])
                for x in range(TT):
                    ch.add(V.match_replace(rest[:, x, :], top[:, x, :], prob[:, x, :], 0.0))
                ch.add(V.reciprocal(den[:, 1], den[:, 0]))
                ch.wait()
                ch.link(V.tensor_tensor(rest[:], prob[:], rest[:], ALU.subtract))
                ch.link(V.tensor_tensor(comb[:, j], rest[:], bcast(den[:, 1].unsqueeze(2), [P, TT, E]), ALU.mult))

            def weigh(g, j, x):
                e.wait_ge(out_ready, TT * g + x + 1)
                e.wait_ge(summed, TT * g + x + 1)
                V.tensor_tensor(weighed[:, x % 2], OUT[x % 2][:].rearrange("p (e d) -> p e d", e=E),
                                bcast(comb[:, j, x, :].unsqueeze(2), [P, E, D]), ALU.mult).then_inc(out_used, 1)

            def add_up(g, j, x):
                e.wait_ge(out_used, TT * g + x + 3)
                V.tensor_reduce(total[:, j, x, :], weighed[:, x % 2].rearrange("p e d -> p d e"), AX.X, ALU.add).then_inc(summed, 1)

            e.sem_inc(out_used, 2)
            e.sem_inc(summed, 2)
            e.wait_ge(loaded, 80)
            V.memset(b2rows[:], 0.0).then_inc(b2_ready, 1)
            e.wait_ge(b2_ready, 1)
            V.tensor_tensor(w2[:], bcast(w2in[:].unsqueeze(2), [P, PAIRS, 2, D]),
                            bcast(pmask[:].unsqueeze(1).unsqueeze(3), [P, PAIRS, 2, D]), ALU.mult).then_inc(w2_ready, 1)
            to_stage(0)
            ch.link(V.tensor_copy(b2rows[0:1, :], b2[:]))
            ch.link(V.tensor_tensor(b2part[:, 0], b2[:], b2rows[0:1, :], ALU.subtract))
            ch.link(V.tensor_copy(b2low[:, 0], b2part[:, 0]))
            ch.link(V.tensor_tensor(b2part[:, 1], b2part[:, 0], b2low[:, 0], ALU.subtract))
            ch.link(V.tensor_copy(b2rows[32:33, :], b2low[:, 0]))
            V.tensor_copy(b2rows[64:65, :], b2part[:, 1]).then_inc(b2_ready, 1)
            for g in range(2):
                lower(g)
                choose(g, g)
                to_stage(g + 1)
            start = ch.n
            per_group = 18
            with e.Fori(0, B // 2) as i:
                for j in range(2):
                    g = 2 * i + j
                    ch.base, ch.n = g * per_group + start, 0
                    weigh(g, j, 0)
                    weigh(g, j, 1)
                    e.wait_ge(added, g + 1)
                    add_up(g, j, 0)
                    add_up(g, j, 1)
                    weigh(g, j, 2)
                    weigh(g, j, 3)
                    add_up(g, j, 2)
                    add_up(g, j, 3)
                    lower(g + 2)
                    choose(g + 2, j)
                    to_stage(g + 3)
                    assert ch.n == per_group, ch.n


def store(nc, k, out):
    with nc.semaphore("stored") as stored, nc.Block() as block:
        @block.sync
        def _(sp):
            sp.dma_start(out.rearrange("(t p) d -> p t d", p=P), k["h"][:]).then_inc(stored, 16)
            sp.wait_ge(stored, 16)


def _layout(a):
    import numpy as np

    f = {n: np.ascontiguousarray(x) for n, x in a.items()}
    io = {}
    for i, n in enumerate(["x", "itok_BS_0_255", "itok_BS_0_511", "itok_BS_0_127", "itok_BS_0_63", "itok_BS_0_3"]):
        io[f"id{i}"] = f[n]
    rowid = np.full((P, 4), -1.0, np.float32)
    tables = np.zeros((EMB + 1, 4 * P), np.float32)
    names = ["E_et", "E_fc", "E_sc", "E_of", "E_tt", "E_rc"]
    for chn, parts in VOCAB.items():
        for which, first, n in parts:
            rowid[first:first + n, chn] = np.arange(n)
            tables[16 * which:16 * which + 16, chn * P + first:chn * P + first + n] = f["L0_tok_" + names[which]].T
    tables[EMB, P:2 * P] = 1.0
    io["rowid"], io["tables_t"] = rowid, tables
    io["ident"] = np.eye(P, dtype=np.float32)
    io["w_t"] = f["L0_tok_W"].T
    io["w_bias"] = f["L0_tok_b"][None]
    io["gamma_beta"] = np.broadcast_to(np.stack([f["L0_tok_gamma"], f["L0_tok_beta"]])[None], (P, 2, D))
    ssm = [{n: f[f"L0_attn_{d}_{n}"] for n in ("log_real", "imag", "log_Delta", "B_real", "B_imag", "C_real", "C_imag", "D")}
           for d in ("fwd", "bwd")]
    prm = np.stack([np.stack([s["log_real"], s["imag"], s["log_Delta"]], -1) for s in ssm], 1)
    io["ssm_prm"] = np.concatenate([prm, prm], 0)
    io["ssm_b"] = np.stack([np.stack([np.concatenate([s["B_real"], s["B_imag"]]), np.concatenate([s["B_imag"], s["B_real"]])], 1)
                            for s in ssm], 1)
    io["ssm_c"] = np.stack([np.stack([np.concatenate([s["C_real"].T, s["C_imag"].T]), np.concatenate([s["C_imag"].T, s["C_real"].T])], 1)
                            for s in ssm], 1)
    io["ssm_d"] = np.stack([s["D"] for s in ssm], 1)
    io["wq_pk_t"] = f["L0_ffn_Wq_pk"].reshape(D, 2 * H, DK).transpose(2, 1, 0)
    io["pk_keys_t"] = f["L0_ffn_pk_keys"].transpose(3, 0, 2, 1).reshape(DK, 2 * H, NK)
    io["wq"] = f["L0_ffn_Wq"].reshape(D, H, D)
    io["wo"] = f["L0_ffn_Wo"].reshape(H, D, D).transpose(1, 0, 2)
    rows = np.concatenate([f["L0_ffn_values_table"], f["L0_ffn_keys_table"]], 1)
    rows = rows.reshape(H, 2, JT // 4, 4, 2, NK // 2, P)
    rows = np.stack([rows[:, second, :, :, first] for first, second in ((0, 0), (1, 0), (1, 1), (0, 1))])
    io["table"] = rows.transpose(3, 4, 1, 0, 2, 5).reshape(P, H * JT * P)
    pair_sel = np.zeros((2, 2, 2, NK // 2, JT // 4, 4, NK // 2), np.float16)
    for order in range(2):
        for u in range(JT // 4):
            for s in range(4):
                pair_sel[order, order, :, np.arange(NK // 2), u, s, np.arange(NK // 2)] = 1
                pair_sel[order, 1 - order, :, 4 * u + s, u, s, :] = 1
    pair_sel = pair_sel.reshape(2, P, JT // 4, P).transpose(1, 0, 2, 3)
    io["pair_sel"] = pair_sel
    io["tile_sel"] = np.tile(np.broadcast_to(np.eye(TT, dtype=np.float32)[:, :, None], (TT, TT, D)), (3, 1, 1))
    qkv_w = np.concatenate([f["L1_attn_qkv_w"], f["L1_attn_qkv_b"][None]])
    io["w_qk"], io["w_v"] = qkv_w[:, :P], qkv_w[:, P:]
    io["w_p"] = np.concatenate([f["L1_attn_proj_w"], f["L1_attn_proj_b"][None]])
    io["head_rows"] = np.tile(np.repeat(np.eye(H, dtype=np.float32), HD, 0), (2, 1))
    io["half_rows"] = np.repeat(np.eye(2, dtype=np.float32), W, 0)
    io["router_t"] = f["L1_ffn_router_w"].T
    io["w1"] = np.concatenate([f["L1_ffn_w1"].transpose(1, 0, 2).reshape(D, -1), f["L1_ffn_b1"].reshape(1, -1)])
    io["w2"] = f["L1_ffn_w2"].reshape(EXPERTS // 2, P, D).transpose(1, 0, 2)
    io["b2"] = f["L1_ffn_b2"].reshape(1, -1)
    io["causal"] = np.triu(np.full((P, P), -1e30, np.float32), 1)
    io["ident16"] = np.eye(P, dtype=np.float16)
    io["sign_half"] = np.repeat(np.array([1.0, -1.0], np.float32), D)[:, None]
    return {n: np.ascontiguousarray(x) for n, x in io.items()}


def kernel(**inputs):
    import concourse.bacc as _bacc
    from concourse.bass_utils import run_bass_kernel_spmd as _run

    nc = _bacc.Bacc("TRN2", target_bir_lowering=False, num_devices=1)
    arrays = {f"in_{n}": a for n, a in _layout(inputs).items()}
    io = {n[3:]: nc.dram_tensor(n, list(a.shape), mybir.dt.from_np(a.dtype), kind="ExternalInput").ap() for n, a in arrays.items()}
    out = nc.dram_tensor("out", [B * S, D], F32, kind="ExternalOutput").ap()
    program(nc, io, out)
    r = _run(nc, [arrays], core_ids=[0])
    return r.results[0]["out"].reshape(B, S, D)
```
